# Optimizing a Trainium2 kernel written in Bass

```python
import numpy as np
import jax
import jax.numpy as jnp

def _softmax(x, axis=-1):
    return jax.nn.softmax(x, axis=axis)

def _gelu(x):
    return jax.nn.gelu(x, approximate=True)

def _silu(x):
    return jax.nn.silu(x)

def _sigmoid(x):
    return jax.nn.sigmoid(x)

def _layernorm(x, axis=-1, eps=1e-05):
    m = jnp.mean(x, axis=axis, keepdims=True)
    v = jnp.var(x, axis=axis, keepdims=True)
    return (x - m) / jnp.sqrt(v + eps)

def _scatter_add(tgt, idx, src, axis=0):
    return tgt.at[idx].add(src)

def _segment_sum(src, seg, n):
    return jax.ops.segment_sum(src, seg, n)
kernel_name = 'mk_adaln_d2_jaxref_r4_1b90d4'

def setup_inputs(seed: int=0):
    np.random.seed(seed)
    _w = jnp.asarray

    def _L0_attn_setup():
        import jax, jax.numpy as jnp
        import numpy as np
        HIDDEN_DIM = 256
        NUM_HEADS = 16
        LN_EPS = 1e-06

        def _layernorm(x, scale, bias):
            mu = jnp.mean(x, axis=-1, keepdims=True)
            var = jnp.mean(jnp.square(x - mu), axis=-1, keepdims=True)
            return (x - mu) * jax.lax.rsqrt(var + LN_EPS) * scale + bias
        key = jax.random.key(seed)
        ks = jax.random.split(key, 4)
        B, S, D = (2, 512, HIDDEN_DIM)
        x = jax.random.normal(ks[0], (B, S, D), dtype=jnp.float32)
        scale = 1.0 / np.sqrt(D)
        wq = jax.random.normal(ks[1], (D, HIDDEN_DIM), dtype=jnp.float32) * scale
        wk = jax.random.normal(ks[2], (D, HIDDEN_DIM), dtype=jnp.float32) * scale
        wv = jax.random.normal(ks[3], (D, HIDDEN_DIM), dtype=jnp.float32) * scale
        ln_scale = jnp.ones((D,), dtype=jnp.float32)
        ln_bias = jnp.zeros((D,), dtype=jnp.float32)
        return {'x': x, 'ln_scale': ln_scale, 'ln_bias': ln_bias, 'wq': wq, 'wk': wk, 'wv': wv}
    _L0_attn_in = _L0_attn_setup()

    def _L0_ffn_setup():
        import jax, jax.numpy as jnp
        import numpy as np
        EPS = 1e-05
        LN_EPS = 1e-05
        NUM_EXPERTS = 8
        TOP_K = 2
        HIDDEN = 256
        INTER = 512

        def _swiglu(x, wg, wu, wd):
            return jax.nn.silu(x @ wg) * (x @ wu) @ wd
        key = jax.random.key(seed)
        ks = jax.random.split(key, 10)
        B, S, H, I, E = (8, 1024, HIDDEN, INTER, NUM_EXPERTS)
        std_h = 1.0 / np.sqrt(H)
        std_i = 1.0 / np.sqrt(I)
        return {'x': jax.random.normal(ks[0], (B, S, H), dtype=jnp.float32), 'ln_scale': jnp.ones((H,), dtype=jnp.float32), 'ln_bias': jnp.zeros((H,), dtype=jnp.float32), 'gate_w': jax.random.normal(ks[1], (E, H), dtype=jnp.float32) * 0.01, 'Wg': jax.random.normal(ks[2], (E, H, I), dtype=jnp.float32) * std_h, 'Wu': jax.random.normal(ks[3], (E, H, I), dtype=jnp.float32) * std_h, 'Wd': jax.random.normal(ks[4], (E, I, H), dtype=jnp.float32) * std_i, 'sWg': jax.random.normal(ks[5], (H, I), dtype=jnp.float32) * std_h, 'sWu': jax.random.normal(ks[6], (H, I), dtype=jnp.float32) * std_h, 'sWd': jax.random.normal(ks[7], (I, H), dtype=jnp.float32) * std_i}
    _L0_ffn_in = _L0_ffn_setup()
    _L0_c = _w((lambda *s: np.random.randn(*s).astype(np.float32) * 0.05)(2, 256))
    _L0_wmod = _w((lambda *s: np.random.randn(*s).astype(np.float32) * 0.05)(256, 6 * 256) * 256 ** (-0.5))

    def _L1_attn_setup():
        import jax, jax.numpy as jnp
        import numpy as np
        D = 256
        H = 16
        KVH = 4
        HD = D // H
        LAT = 64
        WIN = 64
        B, S = (1, 512)
        BASE_G, BASE_L = (1000000.0, 10000.0)
        EPS = 1e-06

        def rmsnorm(x, w):
            return x * jax.lax.rsqrt(jnp.mean(x * x, axis=-1, keepdims=True) + EPS) * w

        def qk_norm(x):
            return x * jax.lax.rsqrt(jnp.mean(x * x, axis=-1, keepdims=True) + EPS)

        def rope(x, base):
            s, hd = (x.shape[-2], x.shape[-1])
            inv_freq = 1.0 / base ** (jnp.arange(0, hd, 2, dtype=jnp.float32) / hd)
            freqs = jnp.arange(s, dtype=jnp.float32)[:, None] * inv_freq[None, :]
            cos, sin = (jnp.cos(freqs), jnp.sin(freqs))
            xe, xo = (x[..., ::2], x[..., 1::2])
            out = jnp.stack([xe * cos - xo * sin, xe * sin + xo * cos], axis=-1)
            return out.reshape(x.shape)

        def split_heads(x, n_heads):
            b, s, _ = x.shape
            return x.reshape(b, s, n_heads, HD).transpose(0, 2, 1, 3)

        def repeat_kv(x):
            return jnp.repeat(x, H // KVH, axis=1)

        def sdpa(q, k, v, mask):
            scores = jnp.einsum('bhqd,bhkd->bhqk', q, k) / np.sqrt(HD).astype(np.float32)
            scores = jnp.where(mask, scores, jnp.float32(-1e+30))
            probs = jax.nn.softmax(scores, axis=-1)
            return jnp.einsum('bhqk,bhkd->bhqd', probs, v)

        def merge_heads(x):
            b, h, s, hd = x.shape
            return x.transpose(0, 2, 1, 3).reshape(b, s, h * hd)

        def global_latent_attn(x, wq, w_kv_down, w_k_up, w_v_up, wo):
            q = split_heads(x @ wq, H)
            latent = x @ w_kv_down
            k = split_heads(latent @ w_k_up, KVH)
            v = split_heads(latent @ w_v_up, KVH)
            q, k = (rope(q, BASE_G), rope(k, BASE_G))
            q, k = (qk_norm(q), qk_norm(k))
            k, v = (repeat_kv(k), repeat_kv(v))
            i = jnp.arange(x.shape[1])
            causal = i[:, None] >= i[None, :]
            return merge_heads(sdpa(q, k, v, causal)) @ wo

        def local_gqa_attn(x, wq, wk, wv, wo):
            q = split_heads(x @ wq, H)
            k = split_heads(x @ wk, KVH)
            v = split_heads(x @ wv, KVH)
            q, k = (rope(q, BASE_L), rope(k, BASE_L))
            q, k = (qk_norm(q), qk_norm(k))
            k, v = (repeat_kv(k), repeat_kv(v))
            i = jnp.arange(x.shape[1])
            diff = i[:, None] - i[None, :]
            mask = (diff >= 0) & (diff < WIN)
            return merge_heads(sdpa(q, k, v, mask)) @ wo
        key = jax.random.key(seed)
        ks = jax.random.split(key, 12)
        std = 0.02
        return {'hidden': jax.random.normal(ks[0], (B, S, D), dtype=jnp.float32), 'norm1_w': jnp.ones((D,), jnp.float32), 'norm2_w': jnp.ones((D,), jnp.float32), 'g_wq': jax.random.normal(ks[1], (D, H * HD), jnp.float32) * std, 'g_kv_down': jax.random.normal(ks[2], (D, LAT), jnp.float32) * std, 'g_k_up': jax.random.normal(ks[3], (LAT, KVH * HD), jnp.float32) * std, 'g_v_up': jax.random.normal(ks[4], (LAT, KVH * HD), jnp.float32) * std, 'g_wo': jax.random.normal(ks[5], (D, D), jnp.float32) * std, 'l_wq': jax.random.normal(ks[6], (D, H * HD), jnp.float32) * std, 'l_wk': jax.random.normal(ks[7], (D, KVH * HD), jnp.float32) * std, 'l_wv': jax.random.normal(ks[8], (D, KVH * HD), jnp.float32) * std, 'l_wo': jax.random.normal(ks[9], (D, D), jnp.float32) * std}
    _L1_attn_in = _L1_attn_setup()

    def _L1_ffn_setup():
        import jax, jax.numpy as jnp
        import numpy as np
        from jax import lax
        T, B, I, M, O = (64, 64, 256, 256, 256)

        def _xavier(key, shape):
            fan_out, fan_in = shape
            limit = float(np.sqrt(6.0 / (fan_in + fan_out)))
            return jax.random.uniform(key, shape, jnp.float32, -limit, limit)
        key = jax.random.key(seed)
        ks = jax.random.split(key, 9)
        x = jax.random.normal(ks[0], (T, B, I), jnp.float32)
        return {'x': x, 'wf': _xavier(ks[1], (M, I)), 'uf': _xavier(ks[2], (M, M)), 'bf': jnp.zeros((M,), jnp.float32), 'wi': _xavier(ks[3], (M, I)), 'ui': _xavier(ks[4], (M, M)), 'bi': jnp.zeros((M,), jnp.float32), 'wc': _xavier(ks[5], (M, I)), 'uc': _xavier(ks[6], (M, M)), 'bc': jnp.zeros((M,), jnp.float32), 'wo': _xavier(ks[7], (O, I)), 'uo': _xavier(ks[8], (O, M)), 'bo': jnp.zeros((O,), jnp.float32), 'in_c': jnp.zeros((M,), jnp.float32)}
    _L1_ffn_in = _L1_ffn_setup()
    _L1_c = _w((lambda *s: np.random.randn(*s).astype(np.float32) * 0.05)(2, 256))
    _L1_wmod = _w((lambda *s: np.random.randn(*s).astype(np.float32) * 0.05)(256, 6 * 256) * 256 ** (-0.5))
    _d = {'L0_attn_x': _L0_attn_in['x'], 'L0_attn_ln_scale': _L0_attn_in['ln_scale'], 'L0_attn_ln_bias': _L0_attn_in['ln_bias'], 'L0_attn_wq': _L0_attn_in['wq'], 'L0_attn_wk': _L0_attn_in['wk'], 'L0_attn_wv': _L0_attn_in['wv'], 'L0_ffn_ln_scale': _L0_ffn_in['ln_scale'], 'L0_ffn_ln_bias': _L0_ffn_in['ln_bias'], 'L0_ffn_gate_w': _L0_ffn_in['gate_w'], 'L0_ffn_Wg': _L0_ffn_in['Wg'], 'L0_ffn_Wu': _L0_ffn_in['Wu'], 'L0_ffn_Wd': _L0_ffn_in['Wd'], 'L0_ffn_sWg': _L0_ffn_in['sWg'], 'L0_ffn_sWu': _L0_ffn_in['sWu'], 'L0_ffn_sWd': _L0_ffn_in['sWd'], 'L0_c': _L0_c, 'L0_wmod': _L0_wmod, 'L1_attn_norm1_w': _L1_attn_in['norm1_w'], 'L1_attn_norm2_w': _L1_attn_in['norm2_w'], 'L1_attn_g_wq': _L1_attn_in['g_wq'], 'L1_attn_g_kv_down': _L1_attn_in['g_kv_down'], 'L1_attn_g_k_up': _L1_attn_in['g_k_up'], 'L1_attn_g_v_up': _L1_attn_in['g_v_up'], 'L1_attn_g_wo': _L1_attn_in['g_wo'], 'L1_attn_l_wq': _L1_attn_in['l_wq'], 'L1_attn_l_wk': _L1_attn_in['l_wk'], 'L1_attn_l_wv': _L1_attn_in['l_wv'], 'L1_attn_l_wo': _L1_attn_in['l_wo'], 'L1_ffn_wf': _L1_ffn_in['wf'], 'L1_ffn_uf': _L1_ffn_in['uf'], 'L1_ffn_bf': _L1_ffn_in['bf'], 'L1_ffn_wi': _L1_ffn_in['wi'], 'L1_ffn_ui': _L1_ffn_in['ui'], 'L1_ffn_bi': _L1_ffn_in['bi'], 'L1_ffn_wc': _L1_ffn_in['wc'], 'L1_ffn_uc': _L1_ffn_in['uc'], 'L1_ffn_bc': _L1_ffn_in['bc'], 'L1_ffn_wo': _L1_ffn_in['wo'], 'L1_ffn_uo': _L1_ffn_in['uo'], 'L1_ffn_bo': _L1_ffn_in['bo'], 'L1_ffn_in_c': _L1_ffn_in['in_c'], 'L1_c': _L1_c, 'L1_wmod': _L1_wmod}
    _x0 = _d['L0_attn_x']
    _d['L0_attn_x'] = jax.random.normal(jax.random.fold_in(jax.random.key(seed), 1), (2, 2048, 256), dtype=_x0.dtype)
    del _x0
    return _d

def reference(L0_attn_x, L0_attn_ln_scale, L0_attn_ln_bias, L0_attn_wq, L0_attn_wk, L0_attn_wv, L0_ffn_ln_scale, L0_ffn_ln_bias, L0_ffn_gate_w, L0_ffn_Wg, L0_ffn_Wu, L0_ffn_Wd, L0_ffn_sWg, L0_ffn_sWu, L0_ffn_sWd, L0_c, L0_wmod, L1_attn_norm1_w, L1_attn_norm2_w, L1_attn_g_wq, L1_attn_g_kv_down, L1_attn_g_k_up, L1_attn_g_v_up, L1_attn_g_wo, L1_attn_l_wq, L1_attn_l_wk, L1_attn_l_wv, L1_attn_l_wo, L1_ffn_wf, L1_ffn_uf, L1_ffn_bf, L1_ffn_wi, L1_ffn_ui, L1_ffn_bi, L1_ffn_wc, L1_ffn_uc, L1_ffn_bc, L1_ffn_wo, L1_ffn_uo, L1_ffn_bo, L1_ffn_in_c, L1_c, L1_wmod):

    def _L0_attn_ref(x, ln_scale, ln_bias, wq, wk, wv):
        import jax, jax.numpy as jnp
        import numpy as np
        HIDDEN_DIM = 256
        NUM_HEADS = 16
        LN_EPS = 1e-06

        def _layernorm(x, scale, bias):
            mu = jnp.mean(x, axis=-1, keepdims=True)
            var = jnp.mean(jnp.square(x - mu), axis=-1, keepdims=True)
            return (x - mu) * jax.lax.rsqrt(var + LN_EPS) * scale + bias
        bs, sl, fdim = x.shape
        h, hd = (NUM_HEADS, HIDDEN_DIM // NUM_HEADS)
        xn = _layernorm(x, ln_scale, ln_bias)
        q = (xn @ wq).reshape(bs, sl, h, hd).transpose(0, 2, 1, 3)
        k = (xn @ wk).reshape(bs, sl, h, hd).transpose(0, 2, 1, 3)
        v = (xn @ wv).reshape(bs, sl, h, hd).transpose(0, 2, 1, 3)
        scores = jnp.einsum('bhid,bhjd->bhij', q, k)
        probs = jax.nn.softmax(scores / jnp.sqrt(jnp.float32(HIDDEN_DIM)), axis=-1)
        out = jnp.einsum('bhij,bhjd->bhid', probs, v)
        out = out.transpose(0, 2, 1, 3).reshape(bs, sl, -1) + xn
        return out

    def _L0_ffn_ref(x, ln_scale, ln_bias, gate_w, Wg, Wu, Wd, sWg, sWu, sWd):
        import jax, jax.numpy as jnp
        import numpy as np
        EPS = 1e-05
        LN_EPS = 1e-05
        NUM_EXPERTS = 8
        TOP_K = 2
        HIDDEN = 256
        INTER = 512

        def _swiglu(x, wg, wu, wd):
            return jax.nn.silu(x @ wg) * (x @ wu) @ wd
        B, S, H = x.shape
        xf = x.reshape(-1, H)
        mu = jnp.mean(xf, axis=-1, keepdims=True)
        var = jnp.var(xf, axis=-1, keepdims=True)
        xn = (xf - mu) * jax.lax.rsqrt(var + LN_EPS) * ln_scale + ln_bias
        logits = xn @ gate_w.T
        probs = jax.nn.softmax(logits, axis=-1)
        tk_probs, tk_idx = jax.lax.top_k(probs, TOP_K)
        tk_probs = tk_probs / (jnp.sum(tk_probs, axis=-1, keepdims=True) + EPS)
        onehot = tk_idx[..., None] == jnp.arange(NUM_EXPERTS)[None, None, :]
        w = jnp.sum(tk_probs[..., None] * onehot.astype(tk_probs.dtype), axis=1)
        out = _swiglu(xf, sWg, sWu, sWd)
        for e in range(NUM_EXPERTS):
            out = out + w[:, e:e + 1] * _swiglu(xf, Wg[e], Wu[e], Wd[e])
        return out.reshape(B, S, H)

    def _L1_attn_ref(hidden, norm1_w, norm2_w, g_wq, g_kv_down, g_k_up, g_v_up, g_wo, l_wq, l_wk, l_wv, l_wo):
        import jax, jax.numpy as jnp
        import numpy as np
        D = 256
        H = 16
        KVH = 4
        HD = D // H
        LAT = 64
        WIN = 64
        B, S = (1, 512)
        BASE_G, BASE_L = (1000000.0, 10000.0)
        EPS = 1e-06

        def rmsnorm(x, w):
            return x * jax.lax.rsqrt(jnp.mean(x * x, axis=-1, keepdims=True) + EPS) * w

        def qk_norm(x):
            return x * jax.lax.rsqrt(jnp.mean(x * x, axis=-1, keepdims=True) + EPS)

        def rope(x, base):
            s, hd = (x.shape[-2], x.shape[-1])
            inv_freq = 1.0 / base ** (jnp.arange(0, hd, 2, dtype=jnp.float32) / hd)
            freqs = jnp.arange(s, dtype=jnp.float32)[:, None] * inv_freq[None, :]
            cos, sin = (jnp.cos(freqs), jnp.sin(freqs))
            xe, xo = (x[..., ::2], x[..., 1::2])
            out = jnp.stack([xe * cos - xo * sin, xe * sin + xo * cos], axis=-1)
            return out.reshape(x.shape)

        def split_heads(x, n_heads):
            b, s, _ = x.shape
            return x.reshape(b, s, n_heads, HD).transpose(0, 2, 1, 3)

        def repeat_kv(x):
            return jnp.repeat(x, H // KVH, axis=1)

        def sdpa(q, k, v, mask):
            scores = jnp.einsum('bhqd,bhkd->bhqk', q, k) / np.sqrt(HD).astype(np.float32)
            scores = jnp.where(mask, scores, jnp.float32(-1e+30))
            probs = jax.nn.softmax(scores, axis=-1)
            return jnp.einsum('bhqk,bhkd->bhqd', probs, v)

        def merge_heads(x):
            b, h, s, hd = x.shape
            return x.transpose(0, 2, 1, 3).reshape(b, s, h * hd)

        def global_latent_attn(x, wq, w_kv_down, w_k_up, w_v_up, wo):
            q = split_heads(x @ wq, H)
            latent = x @ w_kv_down
            k = split_heads(latent @ w_k_up, KVH)
            v = split_heads(latent @ w_v_up, KVH)
            q, k = (rope(q, BASE_G), rope(k, BASE_G))
            q, k = (qk_norm(q), qk_norm(k))
            k, v = (repeat_kv(k), repeat_kv(v))
            i = jnp.arange(x.shape[1])
            causal = i[:, None] >= i[None, :]
            return merge_heads(sdpa(q, k, v, causal)) @ wo

        def local_gqa_attn(x, wq, wk, wv, wo):
            q = split_heads(x @ wq, H)
            k = split_heads(x @ wk, KVH)
            v = split_heads(x @ wv, KVH)
            q, k = (rope(q, BASE_L), rope(k, BASE_L))
            q, k = (qk_norm(q), qk_norm(k))
            k, v = (repeat_kv(k), repeat_kv(v))
            i = jnp.arange(x.shape[1])
            diff = i[:, None] - i[None, :]
            mask = (diff >= 0) & (diff < WIN)
            return merge_heads(sdpa(q, k, v, mask)) @ wo
        x = hidden
        x = x + global_latent_attn(rmsnorm(x, norm1_w), g_wq, g_kv_down, g_k_up, g_v_up, g_wo)
        x = x + local_gqa_attn(rmsnorm(x, norm2_w), l_wq, l_wk, l_wv, l_wo)
        return x

    def _L1_ffn_ref(x, wf, uf, bf, wi, ui, bi, wc, uc, bc, wo, uo, bo, in_c):
        import jax, jax.numpy as jnp
        import numpy as np
        from jax import lax
        T, B, I, M, O = (64, 64, 256, 256, 256)

        def _xavier(key, shape):
            fan_out, fan_in = shape
            limit = float(np.sqrt(6.0 / (fan_in + fan_out)))
            return jax.random.uniform(key, shape, jnp.float32, -limit, limit)
        batch = x.shape[1]
        c0 = jnp.broadcast_to(in_c, (batch, in_c.shape[0]))

        def step(c, xt):
            ft = jax.nn.sigmoid(xt @ wf.T + c @ uf.T + bf)
            it = jax.nn.sigmoid(xt @ wi.T + c @ ui.T + bi)
            gt = jnp.tanh(xt @ wc.T + c @ uc.T + bc)
            c = ft * c + it * gt
            return (c, None)
        c_final, _ = lax.scan(step, c0, x)
        h = jnp.tanh(jnp.einsum('tbi,oi->tbo', x, wo) + c_final @ uo.T + bo)
        return h
    x = L0_attn_x
    mod = (_silu(L0_c) @ L0_wmod).reshape(L0_c.shape[0], 6, 1, -1)
    sa, ca, ga, sb, cb, gb = (mod[:, 0], mod[:, 1], mod[:, 2], mod[:, 3], mod[:, 4], mod[:, 5])
    ga = (2 * (ga >= 0) - 1) * jnp.maximum(jnp.abs(ga), 0.25)
    gb = (2 * (gb >= 0) - 1) * jnp.maximum(jnp.abs(gb), 0.25)
    h = _layernorm(x, axis=-1) * (1 + ca) + sa
    x = x + ga * _L0_attn_ref(h, L0_attn_ln_scale, L0_attn_ln_bias, L0_attn_wq, L0_attn_wk, L0_attn_wv)
    h = _layernorm(x, axis=-1) * (1 + cb) + sb
    x = x + gb * _L0_ffn_ref(h, L0_ffn_ln_scale, L0_ffn_ln_bias, L0_ffn_gate_w, L0_ffn_Wg, L0_ffn_Wu, L0_ffn_Wd, L0_ffn_sWg, L0_ffn_sWu, L0_ffn_sWd)
    mod = (_silu(L1_c) @ L1_wmod).reshape(L1_c.shape[0], 6, 1, -1)
    sa, ca, ga, sb, cb, gb = (mod[:, 0], mod[:, 1], mod[:, 2], mod[:, 3], mod[:, 4], mod[:, 5])
    ga = (2 * (ga >= 0) - 1) * jnp.maximum(jnp.abs(ga), 0.25)
    gb = (2 * (gb >= 0) - 1) * jnp.maximum(jnp.abs(gb), 0.25)
    h = _layernorm(x, axis=-1) * (1 + ca) + sa
    x = x + ga * _L1_attn_ref(h, L1_attn_norm1_w, L1_attn_norm2_w, L1_attn_g_wq, L1_attn_g_kv_down, L1_attn_g_k_up, L1_attn_g_v_up, L1_attn_g_wo, L1_attn_l_wq, L1_attn_l_wk, L1_attn_l_wv, L1_attn_l_wo)
    h = _layernorm(x, axis=-1) * (1 + cb) + sb
    x = x + gb * _L1_ffn_ref(h, L1_ffn_wf, L1_ffn_uf, L1_ffn_bf, L1_ffn_wi, L1_ffn_ui, L1_ffn_bi, L1_ffn_wc, L1_ffn_uc, L1_ffn_bc, L1_ffn_wo, L1_ffn_uo, L1_ffn_bo, L1_ffn_in_c)
    return x

_drawn_inputs = setup_inputs


def setup_inputs(seed=0):
    import zlib

    import numpy as np

    out = dict(_drawn_inputs(seed))
    spreads = {'L0_attn_ln_scale': (1.0, 0.2),
     'L0_attn_ln_bias': (0.0, 0.1),
     'L0_ffn_ln_scale': (1.0, 0.2),
     'L0_ffn_ln_bias': (0.0, 0.268),
     'L1_attn_norm1_w': (1.0, 0.6),
     'L1_attn_norm2_w': (1.0, 0.6),
     'L1_ffn_bf': (0.0, 2.0),
     'L1_ffn_bi': (0.0, 2.0),
     'L1_ffn_bc': (0.0, 0.8),
     'L1_ffn_bo': (0.0, 0.559),
     'L1_ffn_in_c': (0.0, 0.8)}
    factors = {'L0_attn_wq': 7.12,
     'L0_attn_wk': 7.08,
     'L1_attn_g_wq': 8.0,
     'L1_attn_g_kv_down': 8.0,
     'L1_attn_g_k_up': 8.0,
     'L1_attn_g_v_up': 8.0,
     'L1_attn_g_wo': 8.0,
     'L1_attn_l_wq': 8.0,
     'L1_attn_l_wk': 8.0,
     'L1_attn_l_wv': 8.0,
     'L1_attn_l_wo': 8.0,
     'L1_ffn_wf': 5.127,
     'L1_ffn_uf': 8.0,
     'L1_ffn_ui': 7.79,
     'L1_ffn_uc': 2.889,
     'L1_ffn_wi': 4.047}
    for name, (base, spread) in spreads.items():
        noise = np.random.default_rng([zlib.crc32(name.encode()), seed]).standard_normal(out[name].shape)
        drawn = base * np.exp(spread * noise) if base else spread * noise
        out[name] = jnp.asarray(drawn.astype(out[name].dtype))
    for name, factor in factors.items():
        out[name] = (out[name] * factor).astype(out[name].dtype)
    return out
```

```python
from contextlib import ExitStack

import numpy as np
import concourse.bass as bass
from concourse import mybir

F32 = mybir.dt.float32
BF16 = mybir.dt.bfloat16
I32 = mybir.dt.int32
ACT = mybir.ActivationFunctionType
ALU = mybir.AluOpType
AX = mybir.AxisListType

P = 128
B, S, D = 2, 2048, 256
T = B * S
NT = T // P
TB = S // P
KT = D // P
H, HD = 16, 16
KVH = 4
GH = 4
G = B * H // GH
CH = 512
NC = S // CH
WIN = 64
VW = 32
Q_PARTS = (0, 0, 1, 1, 0, 2)
K_PARTS = (0, 1, 0, 1, 2, 0)
NP_ = len(Q_PARTS)
ROWS = NP_ * HD
SHIFT = 3
SA, CA, GA, SB, CB, GB = range(6)


class Chain:

    def __init__(self, eng, sem):
        self.eng, self.sem, self.n = eng, sem, 0

    def __call__(self, instruction):
        self.n += 1
        instruction.then_inc(self.sem, 1)
        self.eng.wait_ge(self.sem, self.n)


class Scope:

    def __init__(self, nc, ctx, tag):
        self.nc, self.ctx, self.tag = nc, ctx, tag

    def sb(self, name, shape, dt=F32):
        return self.ctx.enter_context(self.nc.sbuf_tensor(f"{self.tag}_{name}", shape, dt))

    def ps(self, name, shape):
        used = int(np.prod(shape[1:]))
        banks = self.ctx.enter_context(self.nc.psum_tensor(f"{self.tag}_{name}", [P, -(-used // CH) * CH], F32))
        view = banks[:, 0:used]
        if len(shape) == 3:
            return view.rearrange("p (a b) -> p a b", b=shape[2])
        return view

    def sem(self, name):
        return self.ctx.enter_context(self.nc.semaphore(f"{self.tag}_{name}"))

    def software_sem(self, name):
        return self.nc.alloc_semaphore(f"{self.tag}_{name}")


def modulation(nc, tag, c_cols, w_mod, mod):
    with ExitStack() as ctx:
        sc = Scope(nc, ctx, tag)
        c_sb = sc.sb("c", [P, KT, B])
        sg = sc.sb("silu", [P, KT, B])
        ones = sc.sb("ones", [P, P])
        rep = sc.sb("rep", [P, KT, B, P])
        w_sb = sc.sb("w", [P, KT, 6 * D])
        sign = sc.sb("sign", [P, B, D])
        size = sc.sb("size", [P, B, D])
        bank = [sc.ps(f"bank{i}", [P, CH]) for i in range(6)]
        c_loaded, w_loaded = sc.sem("c_loaded"), sc.sem("w_loaded")
        silu_done, rep_done, rows_ready, dve = (sc.sem(n) for n in ("silu_done", "rep_done", "rows_ready", "dve"))
        block = ctx.enter_context(nc.Block())

        @block.sync
        def _(sp):
            sp.dma_start(c_sb[:], c_cols).then_inc(c_loaded, 16)
            sp.dma_start(w_sb[:], w_mod.rearrange("(k p) n -> p k n", p=P)).then_inc(w_loaded, 16)

        @block.scalar
        def _(act):
            act.wait_ge(c_loaded, 16)
            nc.scalar.activation(sg[:], c_sb[:], ACT.Silu).then_inc(silu_done, 1)

        @block.tensor
        def _(pe):
            pe.wait_ge(w_loaded, 16)
            pe.wait_ge(rep_done, 1)
            for b in range(B):
                for n in range(3):
                    for k in range(KT):
                        last = nc.tensor.matmul(bank[3 * b + n][:], rep[:, k, b, :], w_sb[:, k, n * CH:(n + 1) * CH],
                                                start=k == 0, stop=k == KT - 1)
                    last.then_inc(rows_ready, 1)

        @block.vector
        def _(v):
            step = Chain(v, dve)
            step(nc.vector.memset(ones[:], 1.0))
            v.wait_ge(silu_done, 1)
            for k in range(KT):
                for b in range(B):
                    last = nc.vector.tensor_scalar(rep[:, k, b, :], ones[:], sg[:, k, b:b + 1], None, ALU.mult)
            last.then_inc(rep_done, 1)
            for b in range(B):
                for n in range(3):
                    v.wait_ge(rows_ready, 3 * b + n + 1)
                    step(nc.vector.tensor_copy(mod[:, b, 2 * n:2 * n + 2, :].rearrange("p i d -> p (i d)"),
                                               bank[3 * b + n][:]))
            for i in (CA, CB):
                step(nc.vector.tensor_scalar(mod[:, :, i, :], mod[:, :, i, :], 1.0, None, ALU.add))
            for i in (GA, GB):
                gate = mod[:, :, i, :]
                step(nc.vector.tensor_scalar(sign[:], gate, 0.0, 2.0, ALU.is_ge, ALU.mult))
                step(nc.vector.scalar_tensor_tensor(size[:], gate, -1.0, gate, ALU.mult, ALU.max))
                step(nc.vector.tensor_scalar(size[:], size[:], 0.25, None, ALU.max))
                step(nc.vector.scalar_tensor_tensor(gate, sign[:], -1.0, size[:], ALU.add, ALU.mult))


def normalise(nc, v, step, act_io, src, dst, eps, work, rms=False):
    stats, mean, rstd, tmp = work
    asked, rooted, n = act_io
    for i in range(NT):
        last = nc.vector.bn_stats(stats[:, i, :], src[:, i, :])
    step(last)
    step(nc.vector.tensor_tensor(mean[:], stats[:, :, 1], stats[:, :, 4], ALU.add))
    step(nc.vector.tensor_scalar(mean[:], mean[:], 0.5, None, ALU.mult))
    step(nc.vector.tensor_tensor(tmp[:], stats[:, :, 1], stats[:, :, 4], ALU.subtract))
    step(nc.vector.scalar_tensor_tensor(tmp[:], tmp[:], 0.25, tmp[:], ALU.mult, ALU.mult))
    step(nc.vector.tensor_tensor(rstd[:], stats[:, :, 2], stats[:, :, 5], ALU.add))
    step(nc.vector.scalar_tensor_tensor(rstd[:], rstd[:], 1.0 / D, tmp[:], ALU.mult, ALU.add))
    if rms:
        step(nc.vector.tensor_tensor(tmp[:], mean[:], mean[:], ALU.mult))
        step(nc.vector.tensor_tensor(rstd[:], rstd[:], tmp[:], ALU.add))
        step(nc.vector.tensor_scalar(mean[:], mean[:], 0.0, None, ALU.mult))
    nc.vector.tensor_scalar(rstd[:], rstd[:], eps, None, ALU.add).then_inc(asked, 1)
    v.wait_ge(rooted, n)
    step(nc.vector.reciprocal(rstd[:], rstd[:]))
    for i in range(NT):
        last = nc.vector.tensor_scalar(dst[:, i, :], src[:, i, :], mean[:, i:i + 1], rstd[:, i:i + 1],
                                       ALU.subtract, ALU.mult)
    step(last)


def by_batch(nc, step, dst, src, row, op):
    for b in range(B):
        last = nc.vector.tensor_tensor(dst[:, b * TB:(b + 1) * TB, :], src[:, b * TB:(b + 1) * TB, :],
                                       row[:, b:b + 1, :].to_broadcast([P, TB, D]), op)
    step(last)


def by_row(nc, step, dst, src, row, op):
    step(nc.vector.tensor_tensor(dst[:], src[:], row.to_broadcast([P, NT, D]), op))


def square_roots(nc, act, rstd, asked, rooted, n):
    for i in range(n):
        act.wait_ge(asked, i + 1)
        nc.scalar.activation(rstd[:], rstd[:], ACT.Sqrt).then_inc(rooted, 1)


def norm_work(sc):
    return (sc.sb("stats", [P, NT, 6]), sc.sb("mean", [P, NT]), sc.sb("rstd", [P, NT]), sc.sb("tmp", [P, NT]))


def modulated_norms(nc, tag, x, x_dram, mod, first, second, h, hn, eps2, rows, rms=False, add_gated=False):
    with ExitStack() as ctx:
        sc = Scope(nc, ctx, tag)
        work = norm_work(sc)
        row = [sc.sb(f"row{i}", [P, 1, D]) for i in range(len(rows))]
        x_loaded, row_loaded, asked, rooted, dve = (sc.sem(n) for n in ("x_loaded", "row_loaded", "asked", "rooted", "dve"))
        block = ctx.enter_context(nc.Block())

        @block.sync
        def _(sp):
            if x_dram is not None:
                sp.dma_start(x[:], x_dram.rearrange("b (i p) d -> p (b i) d", p=P)).then_inc(x_loaded, 16)
            for r, source in zip(row, rows):
                sp.dma_start(r[:], source.rearrange("(o n d) -> o n d", o=1, n=1).to_broadcast([P, 1, D])).then_inc(row_loaded, 16)

        @block.scalar
        def _(act):
            square_roots(nc, act, work[2], asked, rooted, 2)

        @block.vector
        def _(v):
            step = Chain(v, dve)
            if x_dram is not None:
                v.wait_ge(x_loaded, 16)
            v.wait_ge(row_loaded, 16 * len(rows))
            normalise(nc, v, step, (asked, rooted, 1), x, h, 1e-5, work)
            by_batch(nc, step, h, h, mod[:, :, second, :], ALU.mult)
            by_batch(nc, step, h, h, mod[:, :, first, :], ALU.add)
            normalise(nc, v, step, (asked, rooted, 2), h, hn, eps2, work, rms)
            by_row(nc, step, hn, hn, row[0][:], ALU.mult)
            if len(rows) > 1:
                by_row(nc, step, hn, hn, row[1][:], ALU.add)
            if add_gated:
                by_batch(nc, step, h, hn, mod[:, :, GA, :], ALU.mult)
                step(nc.vector.tensor_tensor(x[:], x[:], h[:], ALU.add))


def transpose_tokens(nc, tag, src, dst, ident):
    pairs = NT // 2
    with ExitStack() as ctx:
        sc = Scope(nc, ctx, tag)
        bank = [sc.ps(f"bank{i}", [P, KT, 2 * P]) for i in range(4)]
        turned, copied_act, copied_dve = (sc.sem(n) for n in ("turned", "copied_act", "copied_dve"))
        block = ctx.enter_context(nc.Block())

        @block.tensor
        def _(pe):
            for n in range(pairs):
                if n >= 4:
                    pe.wait_ge((copied_act, copied_dve)[n % 2], (n - 4) // 2 + 1)
                for k in range(KT):
                    for t in range(2):
                        last = nc.tensor.transpose(bank[n % 4][:, k, t * P:(t + 1) * P],
                                                   src[:, 2 * n + t, k * P:(k + 1) * P], ident[:])
                last.then_inc(turned, 1)

        def out(n):
            return dst[:, :, 2 * n * P:2 * (n + 1) * P]

        @block.scalar
        def _(act):
            for n in range(0, pairs, 2):
                act.wait_ge(turned, n + 1)
                nc.scalar.activation(out(n), bank[n % 4][:], ACT.Copy).then_inc(copied_act, 1)

        @block.vector
        def _(v):
            for n in range(1, pairs, 2):
                v.wait_ge(turned, n + 1)
                nc.vector.tensor_copy(out(n), bank[n % 4][:]).then_inc(copied_dve, 1)


def split_and_store(nc, tag, jobs, make_chunk, loads):
    with ExitStack() as ctx:
        sc = Scope(nc, ctx, tag)
        bank = [sc.ps(f"bank{i}", [P, CH]) for i in range(8)]
        part = [[sc.sb(f"part{i}_{n}", [P, S], BF16) for n in range(3)] for i in range(2)]
        rest = [sc.sb(f"rest{i}", [P, CH]) for i in range(2)]
        made, high, rest1, mid, low = (sc.sem(n) for n in ("made", "high", "rest1", "mid", "low"))
        loaded = sc.sem("loaded")
        stored = [sc.sem(f"stored{i}") for i in range(2)]
        block = ctx.enter_context(nc.Block())
        chunks = [(n, job, c) for n, job in enumerate(jobs) for c in range(NC)]
        stores_before = [0] * len(jobs)
        for n in range(2, len(jobs)):
            stores_before[n] = stores_before[n - 2] + len(jobs[n - 2][2])

        @block.sync
        def _(sp):
            for out, source in loads:
                sp.dma_start(out, source).then_inc(loaded, 16)
            for n, (_, rows, stores) in enumerate(jobs):
                sp.wait_ge(low, NC * (n + 1))
                sp.wait_ge(mid, NC * (n + 1))
                sp.wait_ge(high, NC * (n + 1))
                for view, which in stores:
                    sp.dma_start(view, part[n % 2][which][0:rows, :]).then_inc(stored[n % 2], 16)
            for i in range(2):
                total = sum(len(job[2]) for job in jobs[i::2])
                if total:
                    sp.wait_ge(stored[i], 16 * total)

        @block.tensor
        def _(pe):
            if loads:
                pe.wait_ge(loaded, 16 * len(loads))
            for m, (n, job, c) in enumerate(chunks):
                if m >= 8:
                    pe.wait_ge(rest1, m - 8 + 1)
                make_chunk(job, c, bank[m % 8]).then_inc(made, 1)

        def middle(act, m):
            n, (_, rows, _s), c = chunks[m]
            act.wait_ge(rest1, m + 1)
            nc.scalar.activation(part[n % 2][1][0:rows, c * CH:(c + 1) * CH], rest[m % 2][0:rows, :],
                                 ACT.Copy).then_inc(mid, 1)

        @block.scalar
        def _(act):
            for m, (n, (_, rows, _s), c) in enumerate(chunks):
                cols = slice(c * CH, (c + 1) * CH)
                act.wait_ge(made, m + 1)
                if n >= 2 and c == 0:
                    act.wait_ge(stored[n % 2], 16 * stores_before[n])
                nc.scalar.activation(part[n % 2][0][0:rows, cols], bank[m % 8][0:rows, :], ACT.Copy).then_inc(high, 1)
                if m >= 1:
                    middle(act, m - 1)
            middle(act, len(chunks) - 1)

        def lowest(v, m):
            n, (_, rows, _s), c = chunks[m]
            cols = slice(c * CH, (c + 1) * CH)
            v.wait_ge(mid, m + 1)
            nc.vector.tensor_tensor(part[n % 2][2][0:rows, cols], rest[m % 2][0:rows, :],
                                    part[n % 2][1][0:rows, cols], ALU.subtract).then_inc(low, 1)

        @block.vector
        def _(v):
            for m, (n, (_, rows, _s), c) in enumerate(chunks):
                v.wait_ge(high, m + 1)
                if m >= 2:
                    v.wait_ge(low, m - 1)
                nc.vector.tensor_tensor(rest[m % 2][0:rows, :], bank[m % 8][0:rows, :],
                                        part[n % 2][0][0:rows, c * CH:(c + 1) * CH], ALU.subtract).then_inc(rest1, 1)
                if m >= 1:
                    lowest(v, m - 1)
            lowest(v, len(chunks) - 1)


def part_rows(scratch, first, rows):
    return [(scratch[n, first:first + rows, :], n) for n in range(3)]


def load_split(eng, dst, scratch, first, j0, j1, blocks, loaded):
    for block, n in enumerate(blocks):
        rows = scratch[n, bass.ds(first + j0 * HD, (j1 - j0) * HD), :]
        eng.dma_start(dst[block * HD:(block + 1) * HD, j0:j1, :],
                      rows.rearrange("(j d) t -> d j t", d=HD)).then_inc(loaded, 16)


def full_attention(nc, q_parts, k_parts, values, o_rows, identf, scale):
    steps = NC * TB
    units = TB * 4
    with ExitStack() as ctx:
        sc = Scope(nc, ctx, "a0")
        q_st = [sc.sb(f"q{i}", [ROWS + SHIFT, GH, S], BF16) for i in range(2)]
        k_st = [sc.sb(f"k{i}", [ROWS + SHIFT, GH, S], BF16) for i in range(2)]
        v_st = [sc.sb(f"v{i}", [P, TB, GH, VW]) for i in range(2)]
        prob = [sc.sb(f"prob{i}", [P, 2, CH]) for i in range(4)]
        o_sb = [sc.sb(f"o{i}", [P, S]) for i in range(2)]
        peak = sc.sb("peak", [P, GH * units])
        top = sc.sb("top", [P, P])
        shift = [sc.sb(f"shift{i}", [GH * TB, P], BF16) for i in range(3)]
        left = [sc.sb(f"left{i}", [GH * TB, P]) for i in range(2)]
        score = [sc.ps(f"score{i}", [P, 2, CH]) for i in range(2)]
        o_ps = sc.ps("o_ps", [P, CH])
        wide = [sc.ps(f"wide{i}", [P, CH]) for i in range(3)]
        first_loaded = [sc.sem(f"first_loaded{i}") for i in range(2)]
        rest_loaded = [sc.sem(f"rest_loaded{i}") for i in range(2)]
        shift_loaded = [sc.sem(f"shift_loaded{i}") for i in range(2)]
        o_stored = [sc.sem(f"o_stored{i}") for i in range(2)]
        v_ready, v_blank, ones_set = (sc.sem(n) for n in ("v_ready", "v_blank", "ones_set"))
        scores_ready, exp_done, pv_done, o_copied = (sc.sem(n) for n in ("scores_ready", "exp_done", "pv_done", "o_copied"))
        wide_ready, wide_used, top_ready, top_turned, shift_ready = (
            sc.sem(n) for n in ("wide_ready", "wide_used", "top_ready", "top_turned", "shift_ready"))
        dve = sc.sem("dve")
        block = ctx.enter_context(nc.Block())

        def groups(eng, one):
            with eng.Fori(0, G // 2 - 1) as pair:
                one(pair, 0, True)
                one(pair, 1, True)
            one(G // 2 - 1, 0, True)
            one(G // 2 - 1, 1, False)

        def load_group(sp, pair, i):
            rows = (2 * pair + i) * GH * HD
            load_split(sp, q_st[i], q_parts, rows, 0, 1, Q_PARTS, first_loaded[i])
            load_split(sp, k_st[i], k_parts, rows, 0, 1, K_PARTS, first_loaded[i])
            load_split(sp, q_st[i], q_parts, rows, 1, GH, Q_PARTS, rest_loaded[i])
            load_split(sp, k_st[i], k_parts, rows, 1, GH, K_PARTS, rest_loaded[i])

        def load_shift(sp, g, i):
            sp.wait_ge(shift_ready, g + 1)
            for n in range(SHIFT):
                sp.dma_start(q_st[i][ROWS + n:ROWS + n + 1, :, :].rearrange("o j t -> o (j t)")
                             .rearrange("o (a b) -> o a b", b=P), shift[n][:]).then_inc(shift_loaded[i], 16)

        @block.sync
        def _(sp):
            load_group(sp, 0, 0)
            load_group(sp, 0, 1)
            load_shift(sp, 0, 0)

            def one(pair, i, more):
                g = 2 * pair + i
                with sp.Fori(0, NC) as c:
                    sp.wait_ge(o_copied, NC * g + c + 2)
                    sp.dma_start(o_rows[bass.ds(g, 1), :, bass.ds(c * CH, CH)].rearrange("g p n -> (g p) n"),
                                 o_sb[i][:, bass.ds(c * CH, CH)]).then_inc(o_stored[i], 16)
                if more:
                    load_shift(sp, g + 1, 1 - i)
                if more and not isinstance(pair, int):
                    load_group(sp, pair + 1, i)

            groups(sp, one)
            for i in range(2):
                sp.wait_ge(o_stored[i], 16 * NC * (G // 2 + 1))

        @block.gpsimd
        def _(pool):
            for i in range(2):
                nc.gpsimd.memset(v_st[i][:], 0.0).then_inc(v_blank, 1)
                pool.wait_ge(v_blank, 2 * i + 1)
                nc.gpsimd.memset(v_st[i][:, :, :, HD:HD + 1], 1.0).then_inc(v_blank, 1)
            pool.wait_ge(v_blank, 4)

            def one(pair, i):
                g = 2 * pair + i
                if not isinstance(pair, int):
                    pool.wait_ge(pv_done, steps * (g - 1) + 2)
                nc.gpsimd.tensor_copy(v_st[i][:, :, :, 0:HD],
                                      values[:, bass.ds(g, 1), :, :].rearrange("p g i (j d) -> p (g i) j d", d=HD)).then_inc(v_ready, 1)

            one(0, 0)
            one(0, 1)
            with pool.Fori(1, G // 2) as pair:
                one(pair, 0)
                one(pair, 1)

        def scores(pe, i, c, kt, half):
            for j in range(2):
                head = 2 * half + j
                last = nc.tensor.matmul(score[half][:, j, :], k_st[i][:, head, kt * P:(kt + 1) * P],
                                        q_st[i][:, head, bass.ds(c * CH, CH)], start=True, stop=True)
            last.then_inc(scores_ready, 1)

        def wide_unit(pe, i, g, head, v):
            base = (g * GH + head) * units
            pe.wait_ge(wide_used, base + (v + 1 if v >= 3 else (3, 1, 2)[v]))
            qt, n = v // 4, v % 4
            q_flat = q_st[i][0:ROWS, :, :].rearrange("p j t -> p (j t)")
            k_flat = k_st[i][0:ROWS, :, :].rearrange("p j t -> p (j t)")
            nc.tensor.matmul(wide[v % 3][:], q_flat[:, bass.ds(head * S + qt * P, P)],
                             k_flat[:, bass.ds(head * S + n * CH, CH)], start=True, stop=True).then_inc(wide_ready, 1)

        loads = 16 * 2 * NP_

        def turn_top(pe, g):
            pe.wait_ge(top_ready, g + 1)
            nc.tensor.transpose(wide[0][:, 0:P], top[:], identf[:]).then_inc(top_turned, 1)

        @block.tensor
        def _(pe):
            nc.tensor.sem_inc(exp_done, 2)
            nc.tensor.sem_inc(pv_done, 2)
            nc.tensor.sem_inc(o_copied, 1)
            nc.tensor.sem_inc(wide_used, 3)
            pe.wait_ge(first_loaded[0], loads)
            with pe.Fori(0, GH) as head:
                for v in range(units):
                    wide_unit(pe, 0, 0, head, v)
                    if v == units // 2:
                        pe.wait_ge(rest_loaded[0], loads)
            turn_top(pe, 0)

            def one(pair, i, more):
                g = 2 * pair + i
                with pe.Fori(0, NC) as c:
                    pe.wait_ge(v_ready, g + 1)
                    pe.wait_ge(ones_set, 3)
                    pe.wait_ge(shift_loaded[i], 16 * SHIFT * (pair + 1))
                    if more:
                        pe.wait_ge(shift_ready, g + 1)
                        pe.wait_ge(first_loaded[1 - i], loads * (pair + i + 1))
                    base = steps * g + TB * c
                    for half in range(2):
                        pe.wait_ge(exp_done, 2 * base + half + 1)
                        scores(pe, i, c, 0, half)
                    for kt in range(TB):
                        s = base + kt
                        for half in range(2):
                            if kt + 1 < TB:
                                pe.wait_ge(exp_done, 2 * (s + 1) + half + 1)
                                scores(pe, i, c, kt + 1, half)
                            if more:
                                if kt == TB // 2 and half == 0:
                                    pe.wait_ge(rest_loaded[1 - i], loads * (pair + i + 1))
                                for n in range(2):
                                    wide_unit(pe, 1 - i, g + 1, c, 4 * kt + 2 * half + n)
                        if kt == 0:
                            pe.wait_ge(o_copied, NC * g + c + 1)
                        pe.wait_ge(exp_done, 2 * s + 4)
                        for head in range(GH):
                            last = nc.tensor.matmul(o_ps[head * VW:(head + 1) * VW, :], v_st[i][:, kt, head, :],
                                                    prob[2 * (kt % 2) + head // 2][:, head % 2, :],
                                                    start=kt == 0, stop=kt == TB - 1)
                        last.then_inc(pv_done, 1)
                if more:
                    turn_top(pe, g + 1)

            groups(pe, one)

        @block.scalar
        def _(act):
            nc.scalar.sem_inc(o_stored[0], 16 * NC)
            nc.scalar.sem_inc(o_stored[1], 16 * NC)

            def one(pair, i, more):
                g = 2 * pair + i
                act.wait_ge(o_stored[i], 16 * NC * (pair + 1))
                with act.Fori(0, NC) as c:
                    base = steps * g + TB * c
                    for kt in range(TB):
                        s = base + kt
                        act.wait_ge(pv_done, s + 1)
                        for half in range(2):
                            act.wait_ge(scores_ready, 2 * s + half + 1)
                            nc.scalar.activation(prob[2 * (kt % 2) + half][:], score[half][:], ACT.Exp,
                                                 scale=scale).then_inc(exp_done, 1)
                    act.wait_ge(pv_done, base + TB + 2)
                    nc.scalar.activation(o_sb[i][:, bass.ds(c * CH, CH)], o_ps[:], ACT.Copy).then_inc(o_copied, 1)

            groups(act, one)

        @block.vector
        def _(v):
            for i in range(2):
                nc.vector.memset(k_st[i][ROWS:ROWS + SHIFT, :, :], 1.0).then_inc(ones_set, 1)

            nc.vector.memset(top[:], 0.0).then_inc(ones_set, 1)

            def maxima(g, head):
                for u in range(units):
                    v.wait_ge(wide_ready, (g * GH + head) * units + u + 1)
                    nc.vector.tensor_reduce(peak[:, bass.ds(head * units + u, 1)], wide[u % 3][:],
                                            AX.X, ALU.max).then_inc(wide_used, 1)

            def shifts(g):
                v.wait_ge(wide_used, (g + 1) * GH * units + 3)
                nc.vector.tensor_reduce(top[:, 0:GH * TB], peak[:].rearrange("p (a n) -> p a n", n=4), AX.X, ALU.max,
                                        negate=True).then_inc(top_ready, 1)
                v.wait_ge(top_turned, g + 1)
                turned = wide[0][0:GH * TB, 0:P]
                nc.vector.tensor_copy(shift[0][:], turned).then_inc(dve, 1)
                v.wait_ge(dve, 4 * g + 1)
                nc.vector.tensor_tensor(left[0][:], turned, shift[0][:], ALU.subtract).then_inc(dve, 1)
                v.wait_ge(dve, 4 * g + 2)
                nc.vector.tensor_copy(shift[1][:], left[0][:]).then_inc(dve, 1)
                v.wait_ge(dve, 4 * g + 3)
                nc.vector.tensor_tensor(left[1][:], left[0][:], shift[1][:], ALU.subtract).then_inc(dve, 1)
                v.wait_ge(dve, 4 * g + 4)
                nc.vector.tensor_copy(shift[2][:], left[1][:]).then_inc(shift_ready, 1)

            with v.Fori(0, GH) as head:
                maxima(0, head)
            shifts(0)

            def one(pair, i, more):
                if more:
                    g = 2 * pair + i
                    with v.Fori(0, GH) as head:
                        maxima(g + 1, head)
                    v.wait_ge(shift_loaded[i], 16 * SHIFT * (pair + 1))
                    shifts(g + 1)

            groups(v, one)


def causal_plan():
    plan = []
    for c in range(NC):
        per = CH // P
        for kt in range(per * (c + 1)):
            skip = max(0, kt - per * c) * P
            plan.append((c, c * CH + skip, CH - skip, kt, 0 if kt >= per * c else None))
    return plan


def window_plan():
    plan = []
    for qt in range(TB):
        plan.append((qt, qt * P, P, qt, 0))
        if qt:
            plan.append((qt, qt * P, WIN, qt - 1, P))
    return plan


def masked_attention(nc, tag, q_parts, k_parts, values, o_rows, mask, identb, plan, span, scale):
    steps = len(plan)
    spans = S // span
    with ExitStack() as ctx:
        sc = Scope(nc, ctx, tag)
        q_st = [sc.sb(f"q{i}", [ROWS, GH, S], BF16) for i in range(2)]
        k_st = [sc.sb(f"k{i}", [ROWS, S], BF16) for i in range(2)]
        v_st = [sc.sb(f"v{i}", [P, TB, VW]) for i in range(2)]
        prob = [sc.sb(f"prob{i}", [P, 2, CH]) for i in range(4)]
        o_sb = [sc.sb(f"o{i}", [P, S]) for i in range(2)]
        score = [sc.ps(f"score{i}", [P, 2, CH]) for i in range(3)]
        o_ps = [sc.ps(f"o_ps{i}", [P, CH]) for i in range(2)]
        loaded = [sc.sem(f"loaded{i}") for i in range(2)]
        o_stored = [sc.sem(f"o_stored{i}") for i in range(2)]
        v_ready, v_blank = sc.sem("v_ready"), sc.sem("v_blank")
        scores_ready, exp_done, pv_done, o_copied = (sc.sem(n) for n in ("scores_ready", "exp_done", "pv_done", "o_copied"))
        block = ctx.enter_context(nc.Block())
        first_of = {}
        last_of = {}
        for n, (c, *_r) in enumerate(plan):
            first_of.setdefault(c, n)
            last_of[c] = n
        jobs = 2 * steps

        def buffer_before(e):
            if e >= 3:
                return e - 3
            return max(x for x in range(jobs) if x % 3 == e) - jobs

        @block.sync
        def _(sp):
            def load_group(pair, i):
                g = 2 * pair + i
                for block_, n in enumerate(Q_PARTS):
                    sp.dma_start(q_st[i][block_ * HD:(block_ + 1) * HD, :, :],
                                 q_parts[n, bass.ds(g * GH * HD, GH * HD), :].rearrange("(j d) t -> d j t", d=HD)
                                 ).then_inc(loaded[i], 16)
                for block_, n in enumerate(K_PARTS):
                    sp.dma_start(k_st[i][block_ * HD:(block_ + 1) * HD, :],
                                 k_parts[n, bass.ds(g * HD, HD), :]).then_inc(loaded[i], 16)

            def store(pair, i):
                g = 2 * pair + i
                for c in range(spans):
                    sp.wait_ge(o_copied, spans * g + c + 3)
                    sp.dma_start(o_rows[bass.ds(g, 1), :, c * span:(c + 1) * span].rearrange("g p n -> (g p) n"),
                                 o_sb[i][:, c * span:(c + 1) * span]).then_inc(o_stored[i], 16)

            load_group(0, 0)
            load_group(0, 1)
            with sp.Fori(0, G // 2 - 1) as pair:
                for i in range(2):
                    store(pair, i)
                    load_group(pair + 1, i)
            for i in range(2):
                store(G // 2 - 1, i)
            for i in range(2):
                sp.wait_ge(o_stored[i], 16 * spans * (G // 2 + 1))

        @block.gpsimd
        def _(pool):
            for i in range(2):
                nc.gpsimd.memset(v_st[i][:], 0.0).then_inc(v_blank, 1)
                pool.wait_ge(v_blank, 2 * i + 1)
                nc.gpsimd.memset(v_st[i][:, :, HD:HD + 1], 1.0).then_inc(v_blank, 1)
            pool.wait_ge(v_blank, 4)

            def one(pair, i):
                g = 2 * pair + i
                if not isinstance(pair, int):
                    pool.wait_ge(pv_done, steps * (g - 1) + 2)
                nc.gpsimd.tensor_copy(v_st[i][:, :, 0:HD],
                                      values[:, bass.ds(g, 1), :, :].rearrange("p g i n -> p (g i) n")).then_inc(v_ready, 1)

            one(0, 0)
            one(0, 1)
            with pool.Fori(1, G // 2) as pair:
                one(pair, 0)
                one(pair, 1)

        @block.tensor
        def _(pe):
            nc.tensor.sem_inc(exp_done, jobs)
            nc.tensor.sem_inc(pv_done, 2)
            nc.tensor.sem_inc(o_copied, 2)

            def scores(i, g, n):
                _, q0, w, kt, masked = plan[n]
                for half in range(2):
                    e = 2 * n + half
                    pe.wait_ge(exp_done, jobs * (g + 1) + buffer_before(e) + 1)
                    out = score[e % 3]
                    for j in range(2):
                        last = nc.tensor.matmul(out[:, j, 0:w], k_st[i][:, kt * P:(kt + 1) * P],
                                                q_st[i][:, 2 * half + j, q0:q0 + w], start=True, stop=True)
                    if masked is not None:
                        for j in range(2):
                            m = min(w, P)
                            last = nc.tensor.matmul(out[:, j, 0:m], identb[:], mask[:, masked:masked + m],
                                                    start=False, stop=True, skip_group_check=True)
                    last.then_inc(scores_ready, 1)

            with pe.Fori(0, G // 2) as pair:
                for i in range(2):
                    g = 2 * pair + i
                    pe.wait_ge(loaded[i], 16 * 2 * NP_ * (pair + 1))
                    scores(i, g, 0)
                    pe.wait_ge(v_ready, g + 1)
                    for n, (c, q0, w, kt, masked) in enumerate(plan):
                        if n + 1 < steps:
                            scores(i, g, n + 1)
                        if n == first_of[c]:
                            pe.wait_ge(o_copied, spans * g + c + 1)
                        pe.wait_ge(exp_done, jobs * (g + 1) + 2 * n + 2)
                        at = q0 - c * span
                        for head in range(GH):
                            last = nc.tensor.matmul(o_ps[c % 2][head * VW:(head + 1) * VW, at:at + w], v_st[i][:, kt, :],
                                                    prob[2 * (n % 2) + head // 2][:, head % 2, 0:w],
                                                    start=n == first_of[c], stop=n == last_of[c], skip_group_check=True)
                        last.then_inc(pv_done, 1)

        @block.scalar
        def _(act):
            nc.scalar.sem_inc(o_stored[0], 16 * spans)
            nc.scalar.sem_inc(o_stored[1], 16 * spans)
            with act.Fori(0, G // 2) as pair:
                for i in range(2):
                    g = 2 * pair + i
                    for n, (c, q0, w, kt, masked) in enumerate(plan):
                        act.wait_ge(pv_done, steps * g + n + 1)
                        for half in range(2):
                            e = 2 * n + half
                            act.wait_ge(scores_ready, jobs * g + e + 1)
                            nc.scalar.activation(prob[2 * (n % 2) + half][:, :, 0:w], score[e % 3][:, :, 0:w], ACT.Exp,
                                                 scale=scale).then_inc(exp_done, 1)

        @block.vector
        def _(v):
            with v.Fori(0, G // 2) as pair:
                for i in range(2):
                    g = 2 * pair + i
                    v.wait_ge(o_stored[i], 16 * spans * (pair + 1))
                    for c in range(spans):
                        v.wait_ge(pv_done, steps * g + last_of[c] + 1 + 2)
                        nc.vector.tensor_copy(o_sb[i][:, c * span:(c + 1) * span], o_ps[c % 2][:, 0:span]).then_inc(o_copied, 1)


def gather_heads(nc, tag, o_rows, att, ident):
    hg = H // GH
    with ExitStack() as ctx:
        sc = Scope(nc, ctx, tag)
        rows = [sc.sb(f"rows{b}", [P, hg, S]) for b in range(B)]
        inverse = [sc.sb(f"inverse{i}", [P, H, 1]) for i in range(2)]
        bank = [sc.ps(f"bank{i}", [P, H, VW]) for i in range(4)]
        loaded = [sc.sem(f"loaded{b}") for b in range(B)]
        turned, inverted, scaled = (sc.sem(n) for n in ("turned", "inverted", "scaled"))
        block = ctx.enter_context(nc.Block())

        @block.sync
        def _(sp):
            for b in range(B):
                sp.dma_start(rows[b][:], o_rows[b * hg:(b + 1) * hg].rearrange("g p t -> p g t")).then_inc(loaded[b], 16)

        @block.tensor
        def _(pe):
            for n in range(NT):
                b, i = n // TB, n % TB
                if i == 0:
                    pe.wait_ge(loaded[b], 16)
                if n >= 4:
                    pe.wait_ge(scaled, n - 3)
                for g in range(hg):
                    last = nc.tensor.transpose(bank[n % 4][:, g * GH:(g + 1) * GH, :].rearrange("p h n -> p (h n)"),
                                               rows[b][:, g, i * P:(i + 1) * P], ident[:])
                last.then_inc(turned, 1)

        @block.vector
        def _(v):
            for n in range(NT + 1):
                if n < NT:
                    v.wait_ge(turned, n + 1)
                    if n >= 2:
                        v.wait_ge(scaled, n - 1)
                    nc.vector.reciprocal(inverse[n % 2][:], bank[n % 4][:, :, HD:HD + 1]).then_inc(inverted, 1)
                if n >= 1:
                    v.wait_ge(inverted, n)
                    nc.vector.tensor_tensor(att[:, n - 1, :].rearrange("p (h n) -> p h n", n=HD),
                                            bank[(n - 1) % 4][:, :, 0:HD],
                                            inverse[(n - 1) % 2][:].to_broadcast([P, H, HD]), ALU.mult).then_inc(scaled, 1)


def project_split(nc, tag, xt, scratches, w_sb, w_loads):
    jobs = []
    for which, scratch in enumerate(scratches):
        for b in range(B):
            for half in range(2):
                jobs.append(((which, b, half), P, part_rows(scratch, b * D + half * P, P)))

    def make_chunk(job, c, bank):
        (which, b, half), _, _ = job
        for k in range(KT):
            last = nc.tensor.matmul(bank[:], w_sb[which][:, k, half * P:(half + 1) * P],
                                    xt[:, k, b * S + c * CH:b * S + (c + 1) * CH], start=k == 0, stop=k == KT - 1)
        return last

    split_and_store(nc, tag, jobs, make_chunk, w_loads)


def token_projection(nc, tag, lhs, kparts, rhs, width, out_of, loads=()):
    with ExitStack() as ctx:
        sc = Scope(nc, ctx, tag)
        bank = [sc.ps(f"bank{i}", [P, CH]) for i in range(6)]
        loaded, made, copied_act, copied_dve = (sc.sem(n) for n in ("loaded", "made", "copied_act", "copied_dve"))
        block = ctx.enter_context(nc.Block())

        @block.sync
        def _(sp):
            for out, source in loads:
                sp.dma_start(out, source).then_inc(loaded, 16)

        @block.tensor
        def _(pe):
            if loads:
                pe.wait_ge(loaded, 16 * len(loads))
            for n in range(NT):
                if n >= 6:
                    pe.wait_ge((copied_act, copied_dve)[n % 2], (n - 6) // 2 + 1)
                for k in range(kparts):
                    last = nc.tensor.matmul(bank[n % 6][:, 0:width], lhs(n, k), rhs(k), start=k == 0, stop=k == kparts - 1)
                last.then_inc(made, 1)

        @block.scalar
        def _(act):
            for n in range(0, NT, 2):
                act.wait_ge(made, n + 1)
                for view, cols in out_of(n):
                    last = nc.scalar.activation(view, bank[n % 6][:, cols], ACT.Copy)
                last.then_inc(copied_act, 1)

        @block.vector
        def _(v):
            for n in range(1, NT, 2):
                v.wait_ge(made, n + 1)
                for view, cols in out_of(n):
                    last = nc.vector.tensor_copy(view, bank[n % 6][:, cols])
                last.then_inc(copied_dve, 1)


def add_gated(nc, tag, x, gate, add):
    with ExitStack() as ctx:
        sc = Scope(nc, ctx, tag)
        dve = sc.sem("dve")
        block = ctx.enter_context(nc.Block())

        @block.vector
        def _(v):
            step = Chain(v, dve)
            by_batch(nc, step, add, add, gate, ALU.mult)
            step(nc.vector.tensor_tensor(x[:], x[:], add[:], ALU.add))


QK = (H + KVH) * HD


def rope_and_norm(nc, tag, qkv, tables):
    nh = H + KVH
    with ExitStack() as ctx:
        sc = Scope(nc, ctx, tag)
        cos, sin = sc.sb("cos", [P, TB, HD // 2]), sc.sb("sin", [P, TB, HD // 2])
        halves = sc.sb("halves", [P, 4, TB, nh, HD // 2])
        half = [halves[:, i] for i in range(4)]
        square = halves[:, 0:2].rearrange("p a i h n -> p (a i h n)").rearrange("p (x n) -> p x n", n=HD)
        total = [sc.sb(f"total{b}", [P, TB * nh]) for b in range(B)]
        loaded, dve, rotated, squared, asked, rooted = (sc.sem(n) for n in ("loaded", "dve", "rotated", "squared", "asked", "rooted"))
        block = ctx.enter_context(nc.Block())

        def qk(b):
            return qkv[:, b * TB:(b + 1) * TB, 0:QK].rearrange("p i (h n) -> p i h n", n=HD)

        @block.sync
        def _(sp):
            for t, s in ((cos, 0), (sin, 1)):
                sp.dma_start(t[:], tables[s]).then_inc(loaded, 16)

        @block.scalar
        def _(act):
            for b in range(B):
                act.wait_ge(rotated, b + 1)
                nc.scalar.activation(square.rearrange("p (i h) n -> p i (h n)", h=nh), qkv[:, b * TB:(b + 1) * TB, 0:QK],
                                     ACT.Square).then_inc(squared, 1)
                act.wait_ge(asked, b + 1)
                nc.scalar.activation(total[b][:], total[b][:], ACT.Sqrt).then_inc(rooted, 1)

        @block.vector
        def _(v):
            step = Chain(v, dve)
            v.wait_ge(loaded, 32)
            for b in range(B):
                x = qk(b)
                even, odd = x[:, :, :, 0::2], x[:, :, :, 1::2]
                c, s = (t[:].rearrange("p i (h n) -> p i h n", h=1).to_broadcast([P, TB, nh, HD // 2]) for t in (cos, sin))
                nc.vector.tensor_tensor(half[0], even, c, ALU.mult)
                nc.vector.tensor_tensor(half[1], odd, s, ALU.mult)
                nc.vector.tensor_tensor(half[2], even, s, ALU.mult)
                step(nc.vector.tensor_tensor(half[3], odd, c, ALU.mult))
                nc.vector.tensor_tensor(even, half[0], half[1], ALU.subtract)
                nc.vector.tensor_tensor(odd, half[2], half[3], ALU.add).then_inc(rotated, 1)
                v.wait_ge(rotated, b + 1)
                v.wait_ge(squared, b + 1)
                step(nc.vector.tensor_reduce(total[b][:], square, AX.X, ALU.add))
                nc.vector.tensor_scalar(total[b][:], total[b][:], 1.0 / HD, 1e-6, ALU.mult, ALU.add).then_inc(asked, 1)
                v.wait_ge(rooted, b + 1)
                step(nc.vector.reciprocal(total[b][:], total[b][:]))
                step(nc.vector.tensor_tensor(x, x, total[b][:].rearrange("p (i h n) -> p i h n", h=nh, n=1)
                                             .to_broadcast([P, TB, nh, HD]), ALU.mult))


def split_heads(nc, tag, qkv, ident, q_parts, k_parts):
    jobs = []
    for b in range(B):
        for half in range(2):
            jobs.append(((b, half * P, P), P, part_rows(q_parts, b * D + half * P, P)))
        jobs.append(((b, H * HD, KVH * HD), KVH * HD, part_rows(k_parts, b * KVH * HD, KVH * HD)))

    def make_chunk(job, c, bank):
        (b, col, rows), _, _ = job
        for t in range(CH // P):
            last = nc.tensor.transpose(bank[0:rows, t * P:(t + 1) * P],
                                       qkv[:, b * TB + c * (CH // P) + t, col:col + rows], ident[:])
        return last

    split_and_store(nc, tag, jobs, make_chunk, [])


def output_projection(nc, tag, att_t, w_sb, w_dram, x):
    with ExitStack() as ctx:
        sc = Scope(nc, ctx, tag)
        bank = [sc.ps(f"bank{i}", [P, D]) for i in range(4)]
        loaded, made, added = (sc.sem(n) for n in ("loaded", "made", "added"))
        block = ctx.enter_context(nc.Block())

        @block.sync
        def _(sp):
            sp.dma_start(w_sb[:], w_dram.rearrange("(k p) n -> p k n", p=P)).then_inc(loaded, 16)

        @block.tensor
        def _(pe):
            pe.wait_ge(loaded, 16)
            for n in range(NT):
                if n >= 4:
                    pe.wait_ge(added, n - 3)
                for k in range(KT):
                    last = nc.tensor.matmul(bank[n % 4][:], att_t[:, k, n * P:(n + 1) * P], w_sb[:, k, :],
                                            start=k == 0, stop=k == KT - 1)
                last.then_inc(made, 1)

        @block.vector
        def _(v):
            for n in range(NT):
                v.wait_ge(made, n + 1)
                nc.vector.tensor_tensor(x[:, n, :], bank[n % 4][:], x[:, n, :], ALU.add).then_inc(added, 1)


NE = 8
INTER = 512
IC = INTER // P
ROUTED_TILES = 2 * T // P + NE
TILES = NT + ROUTED_TILES
SLOTS = TILES * P


def at_least(eng, sem, value):
    if not isinstance(value, int) or value > 0:
        eng.wait_ge(sem, value)


def route(nc, tag, xt, gate_cols, consts, weight, slot, expert_of, h, rows):
    ne = NT * NE
    with ExitStack() as ctx:
        sc = Scope(nc, ctx, tag)
        gate = sc.sb("gate", [P, KT, NE])
        before, ones, back, tiles = sc.sb("before", [P, P]), sc.sb("ones", [P, P]), sc.sb("back", [P, 1, NE]), sc.sb("tiles", [P, TILES, 1])
        prob, left, hot, taken, pos = (sc.sb(n, [P, NT, NE]) for n in ("prob", "left", "hot", "taken", "pos"))
        hots = [sc.sb(f"hots{i}", [P, NT, NE]) for i in range(2)]
        sums, best, first, total = (sc.sb(n, [P, NT, 1]) for n in ("sums", "best", "first", "total"))
        tops = [sc.sb(f"tops{i}", [P, NT, 1]) for i in range(2)]
        run = sc.sb("run", [P, NE, NT])
        line = sc.sb("line", [P, NT])
        count, count_i, ends, base = sc.sb("count", [P, NE]), sc.sb("count_i", [P, NE], I32), sc.sb("ends", [P, NE]), sc.sb("base", [P, 1, NE])
        owner = sc.sb("owner", [P, TILES, NE])
        owned = sc.sb("owned", [P, TILES])
        at = sc.sb("at", [P, NT])
        blank = sc.sb("blank", [P, 8, D])
        logits, inside, whole = (sc.ps(n, [P, NT, NE]) for n in ("logits", "inside", "whole"))
        loaded, dve, logits_ready, centred, exp_done, counted, ranks_ready, routed, blank_set, blanked, copied = (
            sc.sem(n) for n in ("loaded", "dve", "logits_ready", "centred", "exp_done", "counted", "ranks_ready",
                                "routed", "blank_set", "blanked", "copied"))
        sent = sc.software_sem("sent")
        block = ctx.enter_context(nc.Block())

        @block.sync
        def _(sp):
            sp.dma_start(gate[:], gate_cols).then_inc(loaded, 16)
            for dst, source in zip((before, ones, back, tiles), consts):
                sp.dma_start(dst[:], source).then_inc(loaded, 16)
            sp.wait_ge(blank_set, 1)
            for n in range(NT, TILES, 8):
                sp.dma_start(rows[n * P:(n + 8) * P, :].rearrange("(i p) d -> p i d", p=P), blank[:]).then_inc(blanked, 16)
            sp.dma_start(rows[0:T, :].rearrange("(i p) d -> p i d", p=P), h[:]).then_inc(copied, 16)
            sp.wait_ge(copied, 16)

        @block.tensor
        def _(pe):
            pe.wait_ge(loaded, 16 * 5)
            for n in range(NT):
                for k in range(KT):
                    last = nc.tensor.matmul(logits[:, n, :], xt[:, k, n * P:(n + 1) * P], gate[:, k, :],
                                            start=k == 0, stop=k == KT - 1)
            last.then_inc(logits_ready, 1)
            pe.wait_ge(counted, 1)
            nc.tensor.matmul(inside[:], before[:], taken[:], start=True, stop=True)
            nc.tensor.matmul(whole[:], ones[:], taken[:], start=True, stop=True).then_inc(ranks_ready, 1)

        @block.scalar
        def _(act):
            act.wait_ge(centred, 1)
            nc.scalar.activation(prob[:], prob[:], ACT.Exp).then_inc(exp_done, 1)

        @block.vector
        def _(v):
            step = Chain(v, dve)
            tt, ts, stt, red = nc.vector.tensor_tensor, nc.vector.tensor_scalar, nc.vector.scalar_tensor_tensor, nc.vector.tensor_reduce

            def per_expert(x):
                return x.to_broadcast([P, NT, NE])

            nc.vector.memset(blank[:], 0.0).then_inc(blank_set, 1)
            v.wait_ge(loaded, 16 * 5)
            v.wait_ge(logits_ready, 1)
            step(red(best[:, :, 0], logits[:], AX.X, ALU.max))
            tt(prob[:], logits[:], per_expert(best[:]), ALU.subtract).then_inc(centred, 1)
            v.wait_ge(exp_done, 1)
            step(red(sums[:, :, 0], prob[:], AX.X, ALU.add))
            step(nc.vector.reciprocal(sums[:], sums[:]))
            step(tt(prob[:], prob[:], per_expert(sums[:]), ALU.mult))
            step(nc.vector.tensor_copy(left[:], prob[:]))
            for i in range(2):
                step(red(tops[i][:, :, 0], left[:], AX.X, ALU.max))
                step(tt(hot[:], left[:], per_expert(tops[i][:]), ALU.is_equal))
                step(tt(hot[:], hot[:], back[:].to_broadcast([P, NT, NE]), ALU.mult))
                step(red(first[:, :, 0], hot[:], AX.X, ALU.max))
                step(tt(hots[i][:], hot[:], per_expert(first[:]), ALU.is_equal))
                step(stt(left[:], hots[i][:], -2.0, left[:], ALU.mult, ALU.add))
            tt(taken[:], hots[0][:], hots[1][:], ALU.add).then_inc(counted, 1)
            step(tt(total[:], tops[0][:], tops[1][:], ALU.add))
            step(ts(total[:], total[:], 1e-5, None, ALU.add))
            step(nc.vector.reciprocal(total[:], total[:]))
            for i in range(2):
                step(tt(weight[:, i, :], tops[i][:, :, 0], total[:, :, 0], ALU.mult))
            v.wait_ge(ranks_ready, 1)
            step(nc.vector.tensor_copy(pos[:], whole[:]))
            step(nc.vector.memset(line[:], 1.0))
            for e in range(NE):
                last = nc.vector.tensor_tensor_scan(run[:, e, :], line[:], pos[:, :, e], 0.0, ALU.mult, ALU.add)
            step(last)
            step(nc.vector.tensor_copy(count[:], run[:, :, NT - 1]))
            step(tt(pos[:], run[:].rearrange("p e i -> p i e"), pos[:], ALU.subtract))
            step(tt(pos[:], pos[:], inside[:], ALU.add))
            step(ts(count[:], count[:], float(P - 1), None, ALU.add))
            step(nc.vector.tensor_copy(count_i[:], count[:]))
            step(ts(count_i[:], count_i[:], P.bit_length() - 1, None, ALU.logical_shift_right))
            step(nc.vector.tensor_copy(count[:], count_i[:]))
            step(nc.vector.tensor_tensor_scan(ends[:], line[:, 0:NE], count[:], float(NT), ALU.mult, ALU.add))
            step(tt(base[:, 0, :], ends[:], count[:], ALU.subtract))
            step(tt(owner[:], tiles[:].to_broadcast([P, TILES, NE]), base[:].to_broadcast([P, TILES, NE]), ALU.is_ge))
            step(red(owned[:], owner[:], AX.X, ALU.add))
            step(ts(owned[:], owned[:], -1.0, None, ALU.add))
            step(ts(owned[:, 0:NT], owned[:, 0:NT], 0.0, float(NE), ALU.mult, ALU.add))
            step(nc.vector.tensor_copy(expert_of[:], owned[:]))
            step(stt(pos[:], base[:].to_broadcast([P, NT, NE]), float(P), pos[:], ALU.mult, ALU.add))
            for i in range(2):
                step(tt(hot[:], hots[i][:], pos[:], ALU.mult))
                step(red(at[:], hot[:], AX.X, ALU.add))
                step(nc.vector.tensor_copy(slot[:, i, :], at[:]))
            nc.vector.tensor_copy(at[:], at[:]).then_inc(routed, 1)

        @block.gpsimd
        def _(pool):
            pool.wait_ge(routed, 1)
            pool.wait_ge(blanked, 16 * (ROUTED_TILES // 8))
            for n in range(NT):
                for i in range(2):
                    pool.indirect_dma_start(rows, bass.IndirectOffsetOnAxis(ap=slot[:, i, n:n + 1], axis=0),
                                            h[:, n, :], None).then_inc(sent, 16)
            pool.wait_ge(sent, 16 * 2 * NT)


def experts(nc, tag, rows, results, expert_of, w_gate, w_up, w_down, ident):
    with ExitStack() as ctx:
        sc = Scope(nc, ctx, tag)
        x_sb = [sc.sb(f"x{i}", [P, D]) for i in range(2)]
        xt_sb = [sc.sb(f"xt{i}", [P, KT, P]) for i in range(2)]
        silu = [sc.sb(f"silu{i}", [P, INTER]) for i in range(2)]
        hid = [sc.sb(f"hid{i}", [P, INTER]) for i in range(2)]
        ht_sb = [sc.sb(f"ht{i}", [P, IC, P]) for i in range(2)]
        y_sb = [sc.sb(f"y{i}", [P, D]) for i in range(2)]
        x_ps, h_ps, y_ps = sc.ps("x_ps", [P, KT, P]), sc.ps("h_ps", [P, IC, P]), sc.ps("y_ps", [P, D])
        g_ps = [sc.ps(f"g{i}", [P, INTER]) for i in range(2)]
        u_ps = [sc.ps(f"u{i}", [P, INTER]) for i in range(2)]
        loaded = [sc.sem(f"loaded{i}") for i in range(2)]
        stored = [sc.sem(f"stored{i}") for i in range(2)]
        x_turned, xt_copied, g_ready, u_ready, silu_done, hid_done, h_turned, ht_copied, y_ready, y_copied = (
            sc.sem(n) for n in ("x_turned", "xt_copied", "g_ready", "u_ready", "silu_done", "hid_done", "h_turned",
                                "ht_copied", "y_ready", "y_copied"))
        block = ctx.enter_context(nc.Block())

        def steps(eng, one):
            for t in range(3):
                one(t, t % 2, t // 2)
            with eng.Fori(1, TILES // 2 - 1) as pair:
                one(2 * pair + 1, 1, pair)
                one(2 * pair + 2, 0, pair + 1)
            one(TILES - 1, 1, TILES // 2 - 1)

        def some(t):
            return not isinstance(t, int)

        @block.sync
        def _(sp):
            def load(t, i):
                at_least(sp, x_turned, t - 1)
                sp.dma_start(x_sb[i][:], rows[bass.ds(t * P, P), :]).then_inc(loaded[i], 16)

            def store(t, i):
                sp.wait_ge(y_copied, t + 1)
                sp.dma_start(results[bass.ds(t * P, P), :], y_sb[i][:]).then_inc(stored[i], 16)

            load(0, 0)

            def one(t, i, n):
                if some(t) or t < TILES - 1:
                    load(t + 1, 1 - i)
                if some(t) or t > 0:
                    store(t - 1, 1 - i)

            steps(sp, one)
            store(TILES - 1, 1)
            for i in range(2):
                sp.wait_ge(stored[i], 16 * (TILES // 2))

        @block.tensor
        def _(pe):
            def turn_x(t, i, n):
                pe.wait_ge(loaded[i], 16 * (n + 1))
                at_least(pe, xt_copied, t)
                for k in range(KT):
                    last = nc.tensor.transpose(x_ps[:, k, :], x_sb[i][:, k * P:(k + 1) * P], ident[:])
                last.then_inc(x_turned, 1)

            def up(t, i):
                e = pe.value_load(expert_of[0:1, bass.ds(t, 1)], min_val=0, max_val=NE)
                pe.wait_ge(xt_copied, t + 1)
                at_least(pe, hid_done, t - 1)
                for bank, w, ready in ((g_ps[i], w_gate, g_ready), (u_ps[i], w_up, u_ready)):
                    for k in range(KT):
                        last = nc.tensor.matmul(bank[:], xt_sb[i][:, k, :],
                                                w[:, k, bass.ds(e, 1), :].rearrange("p e n -> p (e n)"),
                                                start=k == 0, stop=k == KT - 1)
                    last.then_inc(ready, 1)
                return e

            def turn_h(t, i):
                pe.wait_ge(hid_done, t + 1)
                at_least(pe, ht_copied, t)
                for k in range(IC):
                    last = nc.tensor.transpose(h_ps[:, k, :], hid[i][:, k * P:(k + 1) * P], ident[:])
                last.then_inc(h_turned, 1)

            def down(t, i):
                e = pe.value_load(expert_of[0:1, bass.ds(t, 1)], min_val=0, max_val=NE)
                pe.wait_ge(ht_copied, t + 1)
                at_least(pe, y_copied, t)
                for k in range(IC):
                    last = nc.tensor.matmul(y_ps[:], ht_sb[i][:, k, :],
                                            w_down[:, k, bass.ds(e, 1), :].rearrange("p e n -> p (e n)"),
                                            start=k == 0, stop=k == IC - 1)
                last.then_inc(y_ready, 1)

            turn_x(0, 0, 0)

            def one(t, i, n):
                if some(t) or t > 0:
                    turn_h(t - 1, 1 - i)
                up(t, i)
                if some(t) or t > 0:
                    down(t - 1, 1 - i)
                if some(t) or t < TILES - 1:
                    turn_x(t + 1, 1 - i, n + i)

            steps(pe, one)
            turn_h(TILES - 1, 1)
            down(TILES - 1, 1)

        @block.scalar
        def _(act):
            def copy_h(t, i):
                act.wait_ge(h_turned, t + 1)
                at_least(act, y_ready, t - 1)
                nc.scalar.activation(ht_sb[i][:], h_ps[:], ACT.Copy).then_inc(ht_copied, 1)

            def one(t, i, n):
                if some(t) or t > 0:
                    copy_h(t - 1, 1 - i)
                act.wait_ge(g_ready, t + 1)
                at_least(act, hid_done, t - 1)
                nc.scalar.activation(silu[i][:], g_ps[i][:], ACT.Silu).then_inc(silu_done, 1)

            steps(act, one)
            copy_h(TILES - 1, 1)

        @block.vector
        def _(v):
            def copy_x(t, i):
                v.wait_ge(x_turned, t + 1)
                at_least(v, u_ready, t - 1)
                nc.vector.tensor_copy(xt_sb[i][:], x_ps[:]).then_inc(xt_copied, 1)

            def copy_y(t, i, n):
                v.wait_ge(y_ready, t + 1)
                at_least(v, stored[i], 16 * n)
                nc.vector.tensor_copy(y_sb[i][:], y_ps[:]).then_inc(y_copied, 1)

            copy_x(0, 0)

            def one(t, i, n):
                v.wait_ge(u_ready, t + 1)
                v.wait_ge(silu_done, t + 1)
                at_least(v, h_turned, t - 1)
                nc.vector.tensor_tensor(hid[i][:], silu[i][:], u_ps[i][:], ALU.mult).then_inc(hid_done, 1)
                if some(t) or t > 0:
                    copy_y(t - 1, 1 - i, n - (1 - i))
                if some(t) or t < TILES - 1:
                    copy_x(t + 1, 1 - i)

            steps(v, one)
            copy_y(TILES - 1, 1, TILES // 2 - 1)


def combine(nc, tag, x, gate, results, weight, slot):
    bufs = 4
    with ExitStack() as ctx:
        sc = Scope(nc, ctx, tag)
        acc = [sc.sb(f"acc{i}", [P, D]) for i in range(bufs)]
        picked = [[sc.sb(f"picked{i}_{n}", [P, D]) for n in range(2)] for i in range(bufs)]
        loaded = [sc.sem(f"loaded{i}") for i in range(bufs)]
        fetched = [sc.software_sem(f"fetched{i}") for i in range(bufs)]
        summed, dve = sc.sem("summed"), sc.sem("dve")
        block = ctx.enter_context(nc.Block())

        @block.sync
        def _(sp):
            for n in range(NT):
                at_least(sp, summed, n - bufs + 1)
                sp.dma_start(acc[n % bufs][:], results[n * P:(n + 1) * P, :]).then_inc(loaded[n % bufs], 16)

        @block.gpsimd
        def _(pool):
            for n in range(NT):
                at_least(pool, summed, n - bufs + 1)
                for i in range(2):
                    pool.indirect_dma_start(picked[n % bufs][i][:], None, results,
                                            bass.IndirectOffsetOnAxis(ap=slot[:, i, n:n + 1], axis=0)
                                            ).then_inc(fetched[n % bufs], 16)

        @block.vector
        def _(v):
            step = Chain(v, dve)
            for n in range(NT):
                i, turn = n % bufs, n // bufs + 1
                v.wait_ge(loaded[i], 16 * turn)
                v.wait_ge(fetched[i], 32 * turn)
                for c in range(2):
                    step(nc.vector.scalar_tensor_tensor(acc[i][:], picked[i][c][:], weight[:, c, n:n + 1], acc[i][:],
                                                        ALU.mult, ALU.add))
                step(nc.vector.tensor_tensor(acc[i][:], acc[i][:], gate[:, n // TB, :], ALU.mult))
                nc.vector.tensor_tensor(x[:, n, :], x[:, n, :], acc[i][:], ALU.add).then_inc(summed, 1)


def recurrent_cell(nc, tag, xt, x, gate, w_dram, biases, c0_cols, ident, out):
    names = ("wf", "uf", "wi", "ui", "wc", "uc", "wo", "uo")
    with ExitStack() as ctx:
        sc = Scope(nc, ctx, tag)
        w = {n: sc.sb(n, [P, KT, D]) for n in names}
        bias = sc.sb("bias", [P, 4, KT])
        c0 = sc.sb("c0", [P, KT, 1])
        bias0 = sc.sb("bias0", [P, 3, KT])
        cell = [sc.sb(f"cell{i}", [P, KT, S]) for i in range(2)]
        gates = [[sc.sb(f"gate{i}_{n}", [P, CH]) for n in range(3)] for i in range(2)]
        prod = [sc.sb(f"prod{i}", [P, CH]) for i in range(2)]
        hidden = [sc.sb(f"hidden{i}", [P, KT, CH]) for i in range(2)]
        added = [sc.sb(f"added{i}", [P, 2, D]) for i in range(2)]
        bank = [[sc.ps(f"bank{i}_{n}", [P, CH]) for n in range(3)] for i in range(2)]
        back = [sc.ps(f"back{i}", [P, 2, D]) for i in range(2)]
        loaded = [sc.sem(f"loaded{i}") for i in range(len(names))]
        small, start_ready, dve, bias0_ready = sc.sem("small"), sc.sem("start_ready"), sc.sem("dve"), sc.sem("bias0_ready")
        made, gated, mixed, h_done, turned, scaled, summed, stored = (
            sc.sem(n) for n in ("made", "gated", "mixed", "h_done", "turned", "scaled", "summed", "stored"))
        block = ctx.enter_context(nc.Block())
        jobs = [(t, c, m) for t in range(B) for c in range(NC) for m in range(KT)]
        outs = [(t, c) for t in range(B) for c in range(NC)]
        kinds = (("wf", "uf"), ("wi", "ui"), ("wc", "uc"))

        def need(pe, *which):
            for n in which:
                pe.wait_ge(loaded[names.index(n)], 16)

        @block.sync
        def _(sp):
            for n, b in enumerate(biases):
                sp.dma_start(bias[:, n, :], b).then_inc(small, 16)
            sp.dma_start(c0[:, :, 0], c0_cols).then_inc(small, 16)
            for i, n in enumerate(names):
                sp.dma_start(w[n][:], w_dram[n].rearrange("(k p) n -> p k n", p=P)).then_inc(loaded[i], 16)
            view = out.rearrange("b (i p) d -> p (b i) d", p=P)
            for n in range(len(outs) * 2):
                sp.wait_ge(summed, n + 1)
                sp.dma_start(view[:, 2 * n:2 * n + 2, :], x[:, 2 * n:2 * n + 2, :]).then_inc(stored, 16)
            sp.wait_ge(stored, 16 * len(outs) * 2)

        @block.tensor
        def _(pe):
            pe.wait_ge(small, 16 * 5)
            need(pe, "uf", "ui", "uc")
            for n, (_, u) in enumerate(kinds):
                for m in range(KT):
                    for k in range(KT):
                        last = nc.tensor.matmul(back[0][:, 0, 2 * n + m:2 * n + m + 1], w[u][:, k, m * P:(m + 1) * P],
                                                c0[:, k, :], start=k == 0, stop=k == KT - 1)
            last.then_inc(start_ready, 1)
            need(pe, "wf", "wi", "wc")
            for n, (t, c, m) in enumerate(jobs):
                at_least(pe, gated, 3 * (n - 1))
                for g, (wn, un) in enumerate(kinds):
                    dst = bank[n % 2][g]
                    terms = [(w[wn][:, k, m * P:(m + 1) * P], xt[:, k, t * S + c * CH:t * S + (c + 1) * CH]) for k in range(KT)]
                    if t:
                        pe.wait_ge(mixed, KT * (c + 1))
                        terms += [(w[un][:, k, m * P:(m + 1) * P], cell[0][:, k, c * CH:(c + 1) * CH]) for k in range(KT)]
                    for k, (l, r) in enumerate(terms):
                        last = nc.tensor.matmul(dst[:], l, r, start=k == 0, stop=k == len(terms) - 1)
                    last.then_inc(made, 1)
            need(pe, "wo", "uo")

            def turn(n):
                pe.wait_ge(h_done, KT * (n + 1))
                for q in range(2):
                    at_least(pe, scaled, 2 * n + q - 1)
                    if n == 0:
                        pe.wait_ge(bias0_ready, 1)
                    for i in range(2):
                        for k in range(KT):
                            last = nc.tensor.transpose(back[q][:, i, k * P:(k + 1) * P],
                                                       hidden[n % 2][:, k, (2 * q + i) * P:(2 * q + i + 1) * P], ident[:])
                    last.then_inc(turned, 1)

            for n, (t, c) in enumerate(outs):
                for m in range(KT):
                    if n == 0:
                        pe.wait_ge(gated, 3 * len(jobs))
                    else:
                        at_least(pe, h_done, KT * (n - 2) + m + 1)
                    pe.wait_ge(mixed, KT * (NC + c + 1))
                    terms = [(w["wo"][:, k, m * P:(m + 1) * P], xt[:, k, t * S + c * CH:t * S + (c + 1) * CH]) for k in range(KT)]
                    terms += [(w["uo"][:, k, m * P:(m + 1) * P], cell[1][:, k, c * CH:(c + 1) * CH]) for k in range(KT)]
                    for k, (l, r) in enumerate(terms):
                        last = nc.tensor.matmul(bank[n % 2][m][:], l, r, start=k == 0, stop=k == len(terms) - 1)
                    last.then_inc(made, 1)
                if n:
                    turn(n - 1)
            turn(len(outs) - 1)

        @block.scalar
        def _(act):
            act.wait_ge(bias0_ready, 1)
            for n, (t, c, m) in enumerate(jobs):
                for g in range(3):
                    act.wait_ge(made, 3 * n + g + 1)
                    if g == 0:
                        at_least(act, mixed, n - 1)
                    b = bias0[:, g, m:m + 1] if t == 0 else bias[:, g, m:m + 1]
                    nc.scalar.activation(gates[n % 2][g][:], bank[n % 2][g][:], ACT.Tanh if g == 2 else ACT.Sigmoid,
                                         bias=b).then_inc(gated, 1)
            for n, (t, c) in enumerate(outs):
                for m in range(KT):
                    act.wait_ge(made, 3 * len(jobs) + KT * n + m + 1)
                    at_least(act, turned, 2 * (n - 1))
                    nc.scalar.activation(hidden[n % 2][:, m, :], bank[n % 2][m][:], ACT.Tanh,
                                         bias=bias[:, 3, m:m + 1]).then_inc(h_done, 1)

        @block.vector
        def _(v):
            step = Chain(v, dve)
            v.wait_ge(start_ready, 1)
            nc.vector.tensor_tensor(bias0[:].rearrange("p n m -> p (n m)"), back[0][:, 0, 0:6],
                                    bias[:, 0:3, :].rearrange("p n m -> p (n m)"), ALU.add).then_inc(bias0_ready, 1)
            for n, (t, c, m) in enumerate(jobs):
                f, i, g = gates[n % 2]
                cols = slice(c * CH, (c + 1) * CH)
                v.wait_ge(gated, 3 * (n + 1))
                at_least(v, mixed, n - 1)
                step(nc.vector.tensor_tensor(prod[n % 2][:], i[:], g[:], ALU.mult))
                if t == 0:
                    nc.vector.scalar_tensor_tensor(cell[0][:, m, cols], f[:], c0[:, m, :], prod[n % 2][:],
                                                   ALU.mult, ALU.add).then_inc(mixed, 1)
                else:
                    step(nc.vector.tensor_tensor(f[:], f[:], cell[0][:, m, cols], ALU.mult))
                    nc.vector.tensor_tensor(cell[1][:, m, cols], f[:], prod[n % 2][:], ALU.add).then_inc(mixed, 1)
            for n, (t, c) in enumerate(outs):
                for q in range(2):
                    k = 2 * n + q
                    v.wait_ge(turned, k + 1)
                    at_least(v, summed, k - 1)
                    nc.vector.tensor_tensor(added[q][:], back[q][:], gate[:, t:t + 1, :].to_broadcast([P, 2, D]),
                                            ALU.mult).then_inc(scaled, 1)
                    v.wait_ge(scaled, k + 1)
                    nc.vector.tensor_tensor(x[:, 2 * k:2 * k + 2, :], x[:, 2 * k:2 * k + 2, :], added[q][:],
                                            ALU.add).then_inc(summed, 1)


def rms_norm(nc, tag, src, dst, row_dram, eps):
    with ExitStack() as ctx:
        sc = Scope(nc, ctx, tag)
        work = norm_work(sc)
        row = sc.sb("row", [P, 1, D])
        row_loaded, asked, rooted, dve = (sc.sem(n) for n in ("row_loaded", "asked", "rooted", "dve"))
        block = ctx.enter_context(nc.Block())

        @block.sync
        def _(sp):
            sp.dma_start(row[:], row_dram.rearrange("(o n d) -> o n d", o=1, n=1).to_broadcast([P, 1, D])).then_inc(row_loaded, 16)

        @block.scalar
        def _(act):
            square_roots(nc, act, work[2], asked, rooted, 1)

        @block.vector
        def _(v):
            step = Chain(v, dve)
            v.wait_ge(row_loaded, 16)
            normalise(nc, v, step, (asked, rooted, 1), src, dst, eps, work, rms=True)
            by_row(nc, step, dst, dst, row[:], ALU.mult)


def modulated_norm(nc, tag, x, mod, first, second, h):
    with ExitStack() as ctx:
        sc = Scope(nc, ctx, tag)
        work = norm_work(sc)
        asked, rooted, dve = (sc.sem(n) for n in ("asked", "rooted", "dve"))
        block = ctx.enter_context(nc.Block())

        @block.scalar
        def _(act):
            square_roots(nc, act, work[2], asked, rooted, 1)

        @block.vector
        def _(v):
            step = Chain(v, dve)
            normalise(nc, v, step, (asked, rooted, 1), x, h, 1e-5, work)
            by_batch(nc, step, h, h, mod[:, :, second, :], ALU.mult)
            by_batch(nc, step, h, h, mod[:, :, first, :], ALU.add)


def load_constants(nc, i, ident, identb, masks):
    with ExitStack() as ctx:
        sc = Scope(nc, ctx, "constants")
        masks_sb = sc.sb("masks_sb", [P, 2, P + WIN])
        loaded, cast = sc.sem("loaded"), sc.sem("cast")
        block = ctx.enter_context(nc.Block())

        @block.sync
        def _(sp):
            sp.dma_start(ident[:], i["ident"]).then_inc(loaded, 16)
            sp.dma_start(masks_sb[:], i["masks"]).then_inc(loaded, 16)

        @block.vector
        def _(v):
            v.wait_ge(loaded, 32)
            nc.vector.tensor_copy(identb[:], ident[:]).then_inc(cast, 1)
            nc.vector.tensor_copy(masks[:], masks_sb[:]).then_inc(cast, 1)
            v.wait_ge(cast, 2)


def reset_semaphores(nc, name, numbers):
    with nc.Block(name) as block:
        @block.gpsimd
        def _(pool):
            pool.sem_clear(numbers)


def adaln_layers(nc, i, out):
    q_parts = nc.dram_tensor("q_parts", (3, B * D, S), BF16).ap()
    k_parts = nc.dram_tensor("k_parts", (3, B * D, S), BF16).ap()
    k1_parts = nc.dram_tensor("k1_parts", (3, B * KVH * HD, S), BF16).ap()
    o_rows = nc.dram_tensor("o_rows", (G, P, S), F32).ap()
    rows = nc.dram_tensor("expert_rows", (SLOTS, D), F32).ap()
    results = nc.dram_tensor("expert_results", (SLOTS, D), F32).ap()
    free = list(nc.free_semaphores)
    numbers = range(min(free), max(free) + 1)
    with ExitStack() as ctx:
        def keep(stack, name, shape, dt=F32):
            return stack.enter_context(nc.sbuf_tensor(name, shape, dt))

        x = keep(ctx, "x", [P, NT, D])
        mod = keep(ctx, "mod", [P, B, 6, D])
        ident = keep(ctx, "ident", [P, P])
        identb = keep(ctx, "identb", [P, P], BF16)
        masks = keep(ctx, "masks", [P, 2, P + WIN], BF16)
        load_constants(nc, i, ident, identb, masks)

        modulation(nc, "m0", i["L0_c"], i["L0_wmod"], mod)
        with ExitStack() as stage:
            values = keep(stage, "values0", [P, G, TB, GH * HD])
            with ExitStack() as inner:
                xt = keep(inner, "xt0", [P, KT, T])
                with ExitStack() as norms:
                    h, hn = keep(norms, "h0", [P, NT, D]), keep(norms, "hn0", [P, NT, D])
                    modulated_norms(nc, "n0", x, i["L0_attn_x"], mod, SA, CA, h, hn, 1e-6,
                                    (i["L0_attn_ln_scale"], i["L0_attn_ln_bias"]), add_gated=True)
                    transpose_tokens(nc, "t0", hn, xt, ident)
                w_qk = [keep(inner, f"w{n}", [P, KT, D]) for n in "qk"]
                w_v = keep(inner, "wv", [P, KT, D])

                def w_view(name):
                    return i[name].rearrange("(k p) n -> p k n", p=P)

                project_split(nc, "p0", xt, (q_parts, k_parts), w_qk,
                              [(w_qk[0][:], w_view("L0_attn_wq")), (w_qk[1][:], w_view("L0_attn_wk"))])
                token_projection(nc, "v0", lambda n, k: xt[:, k, n * P:(n + 1) * P], KT, lambda k: w_v[:, k, :], D,
                                 lambda n: [(values[:, (n // TB) * 4 + g, n % TB, :], slice(g * 64, (g + 1) * 64)) for g in range(4)],
                                 [(w_v[:], w_view("L0_attn_wv"))])
            full_attention(nc, q_parts, k_parts, values, o_rows, ident, float(D) ** -0.5)
        with ExitStack() as stage:
            att = keep(stage, "att0", [P, NT, D])
            gather_heads(nc, "g0", o_rows, att, ident)
            add_gated(nc, "r0", x, mod[:, :, GA, :], att)

        reset_semaphores(nc, "reset0", numbers)

        with ExitStack() as stage:
            weight = keep(stage, "weight", [P, 2, NT])
            slot = keep(stage, "slot", [P, 2, NT], I32)
            expert_of = keep(stage, "expert_of", [P, TILES], I32)
            with ExitStack() as inner:
                h = keep(inner, "h1", [P, NT, D])
                xt = keep(inner, "xt1", [P, KT, T])
                with ExitStack() as norms:
                    hn = keep(norms, "hn1", [P, NT, D])
                    modulated_norms(nc, "n1", x, None, mod, SB, CB, h, hn, 1e-5, (i["L0_ffn_ln_scale"], i["L0_ffn_ln_bias"]))
                    transpose_tokens(nc, "t1", hn, xt, ident)
                route(nc, "rt", xt, i["gate_cols"], (i["before"], i["ones"], i["back"], i["tiles"]), weight, slot,
                      expert_of, h, rows)
            with ExitStack() as inner:
                w_gate = keep(inner, "w_gate", [P, KT, NE + 1, INTER])
                w_up = keep(inner, "w_up", [P, KT, NE + 1, INTER])
                w_down = keep(inner, "w_down", [P, IC, NE + 1, D])
                load_weights(nc, i, w_gate, w_up, w_down)
                experts(nc, "ex", rows, results, expert_of, w_gate, w_up, w_down, ident)
            combine(nc, "cb", x, mod[:, :, GB, :], results, weight, slot)

        reset_semaphores(nc, "reset1", numbers)

        modulation(nc, "m1", i["L1_c"], i["L1_wmod"], mod)
        with ExitStack() as stage:
            hid = keep(stage, "hid", [P, NT, D])
            with ExitStack() as inner:
                hn = keep(inner, "hn2", [P, NT, D])
                modulated_norms(nc, "n2", x, None, mod, SA, CA, hid, hn, 1e-6, (i["L1_attn_norm1_w"],), rms=True)
                layer1_attention(nc, i, "g", hn, hid, ident, identb, masks[:, 0, :], q_parts, k1_parts, o_rows, causal_plan(), CH)
            reset_semaphores(nc, "reset2", numbers)
            with ExitStack() as inner:
                hn = keep(inner, "hn3", [P, NT, D])
                rms_norm(nc, "n3", hid, hn, i["L1_attn_norm2_w"], 1e-6)
                layer1_attention(nc, i, "l", hn, hid, ident, identb, masks[:, 1, :], q_parts, k1_parts, o_rows, window_plan(), P)
            add_gated(nc, "r1", x, mod[:, :, GA, :], hid)

        with ExitStack() as stage:
            xt = keep(stage, "xt4", [P, KT, T])
            with ExitStack() as inner:
                h = keep(inner, "h4", [P, NT, D])
                modulated_norm(nc, "n4", x, mod, SB, CB, h)
                transpose_tokens(nc, "t4", h, xt, ident)
            recurrent_cell(nc, "rc", xt, x, mod[:, :, GB, :], {n: i[f"cell_{n}"] for n in
                           ("wf", "uf", "wi", "ui", "wc", "uc", "wo", "uo")},
                           [i[f"cell_b{n}"] for n in "fico"], i["cell_c0"], ident, out)


def load_weights(nc, i, w_gate, w_up, w_down):
    with ExitStack() as ctx:
        loaded = ctx.enter_context(nc.semaphore("expert_weights_loaded"))
        block = ctx.enter_context(nc.Block())

        @block.sync
        def _(sp):
            for dst, routed, shared in ((w_gate, "Wg", "sWg"), (w_up, "Wu", "sWu"), (w_down, "Wd", "sWd")):
                for e in range(NE + 1):
                    source = i[f"L0_ffn_{routed}"][e] if e < NE else i[f"L0_ffn_{shared}"]
                    sp.dma_start(dst[:, :, e, :], source.rearrange("(k p) n -> p k n", p=P)).then_inc(loaded, 16)
            sp.wait_ge(loaded, 16 * 3 * (NE + 1))


def layer1_attention(nc, i, kind, hn, hid, ident, identb, mask, q_parts, k_parts, o_rows, plan, span):
    with ExitStack() as stage:
        def keep(stack, name, shape, dt=F32):
            return stack.enter_context(nc.sbuf_tensor(f"{kind}_{name}", shape, dt))

        values = keep(stage, "values", [P, G, TB, HD])
        with ExitStack() as heads:
            qkv = keep(heads, "qkv", [P, NT, QK])
            with ExitStack() as inner:
                xt = keep(inner, "xt", [P, KT, T])
                transpose_tokens(nc, f"{kind}t", hn, xt, ident)

                def w_view(name):
                    return i[f"L1_attn_{name}"].rearrange("(k p) n -> p k n", p=P)

                def v_out(first):
                    return lambda n: [(values[:, (n // TB) * KVH:(n // TB + 1) * KVH, n % TB, :], slice(first, first + KVH * HD))]

                width = KVH * HD
                if kind == "g":
                    latent = hn[0:width, 0:T // D, :].rearrange("p i d -> p (i d)")
                    w_q, w_down = keep(inner, "w_q", [P, KT, D]), keep(inner, "w_down", [P, KT, width])
                    w_up = keep(inner, "w_up", [width, 2 * width])
                    token_projection(nc, "gq", lambda n, k: xt[:, k, n * P:(n + 1) * P], KT, lambda k: w_q[:, k, :], D,
                                     lambda n: [(qkv[:, n, 0:D], slice(0, D))], [(w_q[:], w_view("g_wq"))])
                    latent_projection(nc, "gl", xt, w_down, latent,
                                      [(w_down[:], w_view("g_kv_down")), (w_up[:, 0:width], i["L1_attn_g_k_up"]),
                                       (w_up[:, width:2 * width], i["L1_attn_g_v_up"])])
                    token_projection(nc, "gkv", lambda n, k: latent[:, n * P:(n + 1) * P], 1, lambda k: w_up[:], 2 * width,
                                     lambda n: [(qkv[:, n, D:QK], slice(0, width))] + v_out(width)(n))
                else:
                    w_qkv = keep(inner, "w_qkv", [P, KT, QK + width])
                    token_projection(nc, "lq", lambda n, k: xt[:, k, n * P:(n + 1) * P], KT, lambda k: w_qkv[:, k, :], QK + width,
                                     lambda n: [(qkv[:, n, :], slice(0, QK))] + v_out(QK)(n),
                                     [(w_qkv[:, :, 0:D], w_view("l_wq")), (w_qkv[:, :, D:QK], w_view("l_wk")),
                                      (w_qkv[:, :, QK:QK + width], w_view("l_wv"))])
            rope_and_norm(nc, f"{kind}r", qkv, i["rope_g" if kind == "g" else "rope_l"])
            split_heads(nc, f"{kind}s", qkv, ident, q_parts, k_parts)
        masked_attention(nc, f"{kind}a", q_parts, k_parts, values, o_rows, mask, identb, plan, span, float(HD) ** -0.5)
    gather_heads(nc, f"{kind}g", o_rows, hn, ident)
    with ExitStack() as stage:
        att_t = stage.enter_context(nc.sbuf_tensor(f"{kind}_att_t", [P, KT, T], F32))
        w_o = stage.enter_context(nc.sbuf_tensor(f"{kind}_w_o", [P, KT, D], F32))
        transpose_tokens(nc, f"{kind}u", hn, att_t, ident)
        output_projection(nc, f"{kind}o", att_t, w_o, i[f"L1_attn_{kind}_wo"], hid)


def latent_projection(nc, tag, xt, w_sb, latent, loads):
    width = KVH * HD
    with ExitStack() as ctx:
        sc = Scope(nc, ctx, tag)
        bank = [sc.ps(f"bank{n}", [P, CH]) for n in range(4)]
        loaded, made, copied = (sc.sem(n) for n in ("loaded", "made", "copied"))
        block = ctx.enter_context(nc.Block())

        @block.sync
        def _(sp):
            for out, source in loads:
                sp.dma_start(out, source).then_inc(loaded, 16)

        @block.tensor
        def _(pe):
            pe.wait_ge(loaded, 16 * len(loads))
            for n in range(T // CH):
                at_least(pe, copied, n - 3)
                for k in range(KT):
                    last = nc.tensor.matmul(bank[n % 4][0:width, :], w_sb[:, k, :], xt[:, k, n * CH:(n + 1) * CH],
                                            start=k == 0, stop=k == KT - 1)
                last.then_inc(made, 1)

        @block.vector
        def _(v):
            for n in range(T // CH):
                v.wait_ge(made, n + 1)
                nc.vector.tensor_copy(latent[:, n * CH:(n + 1) * CH], bank[n % 4][0:width, :]).then_inc(copied, 1)


def columns(a):
    return np.ascontiguousarray(np.moveaxis(a.reshape(*a.shape[:-1], KT, P), (-1, -2), (0, 1)))


def rope_table(base):
    inv = (np.float32(1.0) / np.float32(base) ** (np.arange(0, HD, 2, dtype=np.float32) / np.float32(HD))).astype(np.float32)
    angle = np.arange(S, dtype=np.float32)[:, None] * inv[None, :]
    both = np.stack([np.cos(angle), np.sin(angle)]).astype(np.float32)
    return np.ascontiguousarray(both.reshape(2, TB, P, HD // 2).transpose(0, 2, 1, 3))


def constants():
    eye = np.eye(P, dtype=np.float32)
    key, query = np.mgrid[0:P, 0:P]
    ahead = np.concatenate([query - key, (query - key)[:, 0:WIN] + P], axis=1)
    allowed = np.stack([ahead >= 0, (ahead >= 0) & (ahead < WIN)], axis=1)
    return {
        "ident": eye,
        "masks": np.where(allowed, 0.0, -1e30).astype(np.float32),
        "before": (key < query).astype(np.float32),
        "ones": np.ones((P, P), np.float32),
        "back": np.tile(np.arange(NE, 0, -1, dtype=np.float32), (P, 1, 1)),
        "tiles": np.tile(np.arange(TILES, dtype=np.float32)[:, None], (P, 1, 1)),
        "rope_g": rope_table(1e6),
        "rope_l": rope_table(1e4),
    }


AS_THEY_ARE = ("L0_attn_x", "L0_attn_ln_scale", "L0_attn_ln_bias", "L0_attn_wq", "L0_attn_wk", "L0_attn_wv",
               "L0_ffn_ln_scale", "L0_ffn_ln_bias", "L0_ffn_Wg", "L0_ffn_Wu", "L0_ffn_Wd", "L0_ffn_sWg", "L0_ffn_sWu",
               "L0_ffn_sWd", "L0_wmod", "L1_attn_norm1_w", "L1_attn_norm2_w", "L1_attn_g_wq", "L1_attn_g_kv_down",
               "L1_attn_g_k_up", "L1_attn_g_v_up", "L1_attn_g_wo", "L1_attn_l_wq", "L1_attn_l_wk", "L1_attn_l_wv",
               "L1_attn_l_wo", "L1_wmod")


def laid_out(inputs):
    arrays = {name: np.ascontiguousarray(inputs[name]) for name in AS_THEY_ARE}
    for name in ("L0_c", "L1_c"):
        arrays[name] = columns(np.asarray(inputs[name]))
    arrays["gate_cols"] = columns(np.asarray(inputs["L0_ffn_gate_w"]))
    for name in ("wf", "uf", "wi", "ui", "wc", "uc", "wo", "uo"):
        arrays[f"cell_{name}"] = np.ascontiguousarray(np.asarray(inputs[f"L1_ffn_{name}"]).T)
    for name in "fico":
        arrays[f"cell_b{name}"] = columns(np.asarray(inputs[f"L1_ffn_b{name}"]))
    arrays["cell_c0"] = columns(np.asarray(inputs["L1_ffn_in_c"]))
    return arrays | constants()


def kernel(**inputs):
    import concourse.bacc as bacc
    from concourse.bass_utils import run_bass_kernel_spmd

    arrays = laid_out(inputs)
    nc = bacc.Bacc("TRN2", target_bir_lowering=False, num_devices=1)
    handles = {n: nc.dram_tensor(f"in_{n}", a.shape, mybir.dt.from_np(a.dtype), kind="ExternalInput").ap() for n, a in arrays.items()}
    out = nc.dram_tensor("out", (B, S, D), F32, kind="ExternalOutput").ap()
    adaln_layers(nc, handles, out)
    return run_bass_kernel_spmd(nc, [{f"in_{n}": a for n, a in arrays.items()}], core_ids=[0]).results[0]["out"]
```

```python
from contextlib import ExitStack

import numpy as np
import concourse.bass as bass
from concourse import mybir

F32 = mybir.dt.float32
BF16 = mybir.dt.bfloat16
I32 = mybir.dt.int32
ACT = mybir.ActivationFunctionType
ALU = mybir.AluOpType
AX = mybir.AxisListType

P = 128
B, S, D = 2, 2048, 256
T = B * S
NT = T // P
TB = S // P
KT = D // P
H, HD = 16, 16
KVH = 4
GH = 4
G = B * H // GH
CH = 512
NC = S // CH
WIN = 64
VW = 32
Q_PARTS = (0, 0, 1, 1, 0, 2)
K_PARTS = (0, 1, 0, 1, 2, 0)
NP_ = len(Q_PARTS)
ROWS = NP_ * HD
SHIFT = 3
SA, CA, GA, SB, CB, GB = range(6)


class Chain:

    def __init__(self, eng, sem):
        self.eng, self.sem, self.n = eng, sem, 0

    def __call__(self, instruction):
        self.n += 1
        instruction.then_inc(self.sem, 1)
        self.eng.wait_ge(self.sem, self.n)


class Scope:

    def __init__(self, nc, ctx, tag):
        self.nc, self.ctx, self.tag = nc, ctx, tag

    def sb(self, name, shape, dt=F32):
        return self.ctx.enter_context(self.nc.sbuf_tensor(f"{self.tag}_{name}", shape, dt))

    def ps(self, name, shape):
        used = int(np.prod(shape[1:]))
        banks = self.ctx.enter_context(self.nc.psum_tensor(f"{self.tag}_{name}", [P, -(-used // CH) * CH], F32))
        view = banks[:, 0:used]
        if len(shape) == 3:
            return view.rearrange("p (a b) -> p a b", b=shape[2])
        return view

    def sem(self, name):
        return self.ctx.enter_context(self.nc.semaphore(f"{self.tag}_{name}"))

    def software_sem(self, name):
        return self.nc.alloc_semaphore(f"{self.tag}_{name}")


def modulation(nc, tag, c_cols, w_mod, mod):
    with ExitStack() as ctx:
        sc = Scope(nc, ctx, tag)
        c_sb = sc.sb("c", [P, KT, B])
        sg = sc.sb("silu", [P, KT, B])
        ones = sc.sb("ones", [P, P])
        rep = sc.sb("rep", [P, KT, B, P])
        w_sb = sc.sb("w", [P, KT, 6 * D])
        sign = sc.sb("sign", [P, B, D])
        size = sc.sb("size", [P, B, D])
        bank = [sc.ps(f"bank{i}", [P, CH]) for i in range(6)]
        c_loaded, w_loaded = sc.sem("c_loaded"), sc.sem("w_loaded")
        silu_done, rep_done, rows_ready, dve = (sc.sem(n) for n in ("silu_done", "rep_done", "rows_ready", "dve"))
        block = ctx.enter_context(nc.Block())

        @block.sync
        def _(sp):
            sp.dma_start(c_sb[:], c_cols).then_inc(c_loaded, 16)
            sp.dma_start(w_sb[:], w_mod.rearrange("(k p) n -> p k n", p=P)).then_inc(w_loaded, 16)

        @block.scalar
        def _(act):
            act.wait_ge(c_loaded, 16)
            nc.scalar.activation(sg[:], c_sb[:], ACT.Silu).then_inc(silu_done, 1)

        @block.tensor
        def _(pe):
            pe.wait_ge(w_loaded, 16)
            pe.wait_ge(rep_done, 1)
            for b in range(B):
                for n in range(3):
                    for k in range(KT):
                        last = nc.tensor.matmul(bank[3 * b + n][:], rep[:, k, b, :], w_sb[:, k, n * CH:(n + 1) * CH],
                                                start=k == 0, stop=k == KT - 1)
                    last.then_inc(rows_ready, 1)

        @block.vector
        def _(v):
            step = Chain(v, dve)
            step(nc.vector.memset(ones[:], 1.0))
            v.wait_ge(silu_done, 1)
            for k in range(KT):
                for b in range(B):
                    last = nc.vector.tensor_scalar(rep[:, k, b, :], ones[:], sg[:, k, b:b + 1], None, ALU.mult)
            last.then_inc(rep_done, 1)
            for b in range(B):
                for n in range(3):
                    v.wait_ge(rows_ready, 3 * b + n + 1)
                    step(nc.vector.tensor_copy(mod[:, b, 2 * n:2 * n + 2, :].rearrange("p i d -> p (i d)"),
                                               bank[3 * b + n][:]))
            for i in (CA, CB):
                step(nc.vector.tensor_scalar(mod[:, :, i, :], mod[:, :, i, :], 1.0, None, ALU.add))
            for i in (GA, GB):
                gate = mod[:, :, i, :]
                step(nc.vector.tensor_scalar(sign[:], gate, 0.0, 2.0, ALU.is_ge, ALU.mult))
                step(nc.vector.scalar_tensor_tensor(size[:], gate, -1.0, gate, ALU.mult, ALU.max))
                step(nc.vector.tensor_scalar(size[:], size[:], 0.25, None, ALU.max))
                step(nc.vector.scalar_tensor_tensor(gate, sign[:], -1.0, size[:], ALU.add, ALU.mult))


SHARE = 10


def tiles_of(b, pool):
    return slice(b * TB + SHARE, (b + 1) * TB) if pool else slice(b * TB, b * TB + SHARE)


def on_rows(eng, step, b, pool, dst, src, row, op):
    tiles = tiles_of(b, pool)
    n = tiles.stop - tiles.start
    step(eng.tensor_tensor(dst[:, tiles, :], src[:, tiles, :], row(b).to_broadcast([P, n, D]), op))


def gated_sum(eng, step, b, pool, x, gate, add, scaled):
    tiles = tiles_of(b, pool)
    on_rows(eng, step, b, pool, scaled, add, gate, ALU.mult)
    step(eng.tensor_tensor(x[:, tiles, :], x[:, tiles, :], scaled[:, tiles, :], ALU.add))


def token_stats(nc, step, b, src, eps, rms, work, asked):
    tiles = slice(b * TB, (b + 1) * TB)
    stats, mean, rstd, tmp, _ = (w[:, tiles] for w in work)
    for i in range(TB):
        last = nc.vector.bn_stats(stats[:, i, :], src[:, b * TB + i, :])
    step(last)
    step(nc.vector.tensor_tensor(mean, stats[:, :, 1], stats[:, :, 4], ALU.add))
    step(nc.vector.tensor_scalar(mean, mean, 0.5, None, ALU.mult))
    step(nc.vector.tensor_tensor(tmp, stats[:, :, 1], stats[:, :, 4], ALU.subtract))
    step(nc.vector.scalar_tensor_tensor(tmp, tmp, 0.25, tmp, ALU.mult, ALU.mult))
    step(nc.vector.tensor_tensor(rstd, stats[:, :, 2], stats[:, :, 5], ALU.add))
    step(nc.vector.scalar_tensor_tensor(rstd, rstd, 1.0 / D, tmp, ALU.mult, ALU.add))
    if rms:
        step(nc.vector.tensor_tensor(tmp, mean, mean, ALU.mult))
        step(nc.vector.tensor_tensor(rstd, rstd, tmp, ALU.add))
    nc.vector.tensor_scalar(rstd, rstd, eps, None, ALU.add).then_inc(asked, 1)


def norms(nc, tag, passes, loads=(), x_sum=None, last_sum=None, turned=None):
    with ExitStack() as ctx:
        sc = Scope(nc, ctx, tag)
        works = [tuple(sc.sb(f"{name}{p}", [P, NT] + more) for name, more in
                       (("stats", [6]), ("mean", []), ("rstd", []), ("tmp", []), ("offset", []))) for p in range(len(passes))]
        loaded, asked, rooted, ready, applied, dve, pooled, pool_own = (
            sc.sem(n) for n in ("loaded", "asked", "rooted", "ready", "applied", "dve", "pooled", "pool_own"))
        scaled, bank_ready, bank_copied = sc.sem("scaled"), sc.sem("bank_ready"), sc.sem("bank_copied")
        bank = [sc.ps(f"bank{i}", [P, KT, 2 * P]) for i in range(4)] if turned else []
        block = ctx.enter_context(nc.Block())
        summed = B if x_sum else 0
        own = TB - SHARE

        @block.sync
        def _(sp):
            for dst, source in loads:
                sp.dma_start(dst, source).then_inc(loaded, 16)

        @block.tensor
        def _(pe):
            if not turned:
                return
            src, ident = passes[-1][1], turned[1]
            for n in range(NT // 2):
                b = 2 * n // TB
                if 2 * n % TB == 0:
                    pe.wait_ge(scaled, B * (len(passes) - 1) + b + 1)
                if (2 * n + 1) % TB == SHARE // 2 * 2 + 1:
                    pe.wait_ge(pooled, summed + B * (len(passes) - 1) + b + 1)
                if n >= 4:
                    pe.wait_ge(bank_copied, n - 3)
                for k in range(KT):
                    for t in range(2):
                        last = nc.tensor.transpose(bank[n % 4][:, k, t * P:(t + 1) * P],
                                                   src[:, 2 * n + t, k * P:(k + 1) * P], ident[:])
                last.then_inc(bank_ready, 1)

        @block.scalar
        def _(act):
            for p, (src, dst, *_r) in enumerate(passes):
                rstd, offset = works[p][2], works[p][4]
                for b in range(B):
                    act.wait_ge(asked, B * p + b + 1)
                    part = rstd[:, b * TB:(b + 1) * TB]
                    nc.scalar.activation(part, part, ACT.Sqrt).then_inc(rooted, 1)
                for b in range(B):
                    act.wait_ge(ready, B * p + b + 1)
                    tiles = tiles_of(b, True)
                    for n in range(tiles.start, tiles.stop):
                        nc.scalar.activation(dst[:, n, :], src[:, n, :], ACT.Identity, bias=offset[:, n:n + 1],
                                             scale=rstd[:, n:n + 1]).then_inc(applied, 1)
            if turned:
                for n in range(NT // 2):
                    act.wait_ge(bank_ready, n + 1)
                    nc.scalar.activation(turned[0][:, :, 2 * n * P:2 * (n + 1) * P], bank[n % 4][:],
                                         ACT.Copy).then_inc(bank_copied, 1)

        @block.gpsimd
        def _(pool):
            step = Chain(pool, pool_own)
            if loads:
                pool.wait_ge(loaded, 16 * len(loads))
            if x_sum:
                for b in range(B):
                    gated_sum(nc.gpsimd, step, b, True, *x_sum, x_sum[2])
                    pool.sem_inc(pooled, 1)
            for p, (_, dst, _, _, factor, addend) in enumerate(passes):
                for b in range(B):
                    pool.wait_ge(applied, own * (B * p + b + 1))
                    on_rows(nc.gpsimd, step, b, True, dst, dst, factor, ALU.mult)
                    if addend is not None:
                        on_rows(nc.gpsimd, step, b, True, dst, dst, addend, ALU.add)
                    pool.sem_inc(pooled, 1)
            if last_sum:
                for b in range(B):
                    gated_sum(nc.gpsimd, step, b, True, *last_sum)

        def scale_own(step, p, b):
            src, dst, _, rms, factor, addend = passes[p]
            _, mean, rstd, _, _ = works[p]
            tiles = tiles_of(b, False)
            if not rms:
                for n in range(tiles.start, tiles.stop):
                    last = nc.vector.scalar_tensor_tensor(dst[:, n, :], src[:, n, :], mean[:, n:n + 1], factor(b)[:, 0, :],
                                                          ALU.subtract, ALU.mult)
                step(last)
            for n in range(tiles.start, tiles.stop):
                last = nc.vector.scalar_tensor_tensor(dst[:, n, :], (src if rms else dst)[:, n, :], rstd[:, n:n + 1],
                                                      (factor if rms else addend)(b)[:, 0, :], ALU.mult,
                                                      ALU.mult if rms else ALU.add)
            last.then_inc(scaled, 1)

        @block.vector
        def _(v):
            step = Chain(v, dve)
            if loads:
                v.wait_ge(loaded, 16 * len(loads))
            for b in range(B):
                if x_sum:
                    gated_sum(nc.vector, step, b, False, *x_sum, x_sum[2])
                    v.wait_ge(pooled, b + 1)
                src, _, eps, rms, _, _ = passes[0]
                token_stats(nc, step, b, src, eps, rms, works[0], asked)
            for p, (_, _, _, rms, _, _) in enumerate(passes):
                for b in range(B):
                    _, mean, rstd, _, offset = (w[:, b * TB:(b + 1) * TB] for w in works[p])
                    v.wait_ge(rooted, B * p + b + 1)
                    if rms:
                        nc.vector.memset(offset, 0.0)
                        nc.vector.reciprocal(rstd, rstd).then_inc(ready, 1)
                    else:
                        step(nc.vector.reciprocal(rstd, rstd))
                        nc.vector.scalar_tensor_tensor(offset, mean, -1.0, rstd, ALU.mult, ALU.mult).then_inc(ready, 1)
                    v.wait_ge(ready, B * p + b + 1)
                for b in range(B):
                    scale_own(step, p, b)
                    v.wait_ge(scaled, B * p + b + 1)
                    if p + 1 < len(passes):
                        v.wait_ge(pooled, summed + B * p + b + 1)
                        src, _, eps, next_rms, _, _ = passes[p + 1]
                        token_stats(nc, step, b, src, eps, next_rms, works[p + 1], asked)
            if last_sum:
                for b in range(B):
                    gated_sum(nc.vector, step, b, False, *last_sum)
            v.wait_ge(pooled, summed + B * len(passes))


def row_load(row, source):
    return row[:], source.rearrange("(o n d) -> o n d", o=1, n=1).to_broadcast([P, 1, D])


def transpose_tokens(nc, tag, src, dst, ident):
    pairs = NT // 2
    with ExitStack() as ctx:
        sc = Scope(nc, ctx, tag)
        bank = [sc.ps(f"bank{i}", [P, KT, 2 * P]) for i in range(4)]
        turned, copied_act, copied_dve = (sc.sem(n) for n in ("turned", "copied_act", "copied_dve"))
        block = ctx.enter_context(nc.Block())

        @block.tensor
        def _(pe):
            for n in range(pairs):
                if n >= 4:
                    pe.wait_ge((copied_act, copied_dve)[n % 2], (n - 4) // 2 + 1)
                for k in range(KT):
                    for t in range(2):
                        last = nc.tensor.transpose(bank[n % 4][:, k, t * P:(t + 1) * P],
                                                   src[:, 2 * n + t, k * P:(k + 1) * P], ident[:])
                last.then_inc(turned, 1)

        def out(n):
            return dst[:, :, 2 * n * P:2 * (n + 1) * P]

        @block.scalar
        def _(act):
            for n in range(0, pairs, 2):
                act.wait_ge(turned, n + 1)
                nc.scalar.activation(out(n), bank[n % 4][:], ACT.Copy).then_inc(copied_act, 1)

        @block.vector
        def _(v):
            for n in range(1, pairs, 2):
                v.wait_ge(turned, n + 1)
                nc.vector.tensor_copy(out(n), bank[n % 4][:]).then_inc(copied_dve, 1)


def split_and_store(nc, tag, jobs, make_chunk, loads):
    with ExitStack() as ctx:
        sc = Scope(nc, ctx, tag)
        bank = [sc.ps(f"bank{i}", [P, CH]) for i in range(8)]
        part = [[sc.sb(f"part{i}_{n}", [P, S], BF16) for n in range(3)] for i in range(2)]
        rest = [sc.sb(f"rest{i}", [P, CH]) for i in range(2)]
        made, high, rest1, mid, low = (sc.sem(n) for n in ("made", "high", "rest1", "mid", "low"))
        loaded = sc.sem("loaded")
        stored = [sc.sem(f"stored{i}") for i in range(2)]
        block = ctx.enter_context(nc.Block())
        chunks = [(n, job, c) for n, job in enumerate(jobs) for c in range(NC)]
        stores_before = [0] * len(jobs)
        for n in range(2, len(jobs)):
            stores_before[n] = stores_before[n - 2] + len(jobs[n - 2][2])

        @block.sync
        def _(sp):
            for out, source in loads:
                sp.dma_start(out, source).then_inc(loaded, 16)
            for n, (_, rows, stores) in enumerate(jobs):
                sp.wait_ge(low, NC * (n + 1))
                sp.wait_ge(mid, NC * (n + 1))
                sp.wait_ge(high, NC * (n + 1))
                for view, which in stores:
                    sp.dma_start(view, part[n % 2][which][0:rows, :]).then_inc(stored[n % 2], 16)
            for i in range(2):
                total = sum(len(job[2]) for job in jobs[i::2])
                if total:
                    sp.wait_ge(stored[i], 16 * total)

        @block.tensor
        def _(pe):
            if loads:
                pe.wait_ge(loaded, 16 * len(loads))
            for m, (n, job, c) in enumerate(chunks):
                if m >= 8:
                    pe.wait_ge(rest1, m - 8 + 1)
                make_chunk(job, c, bank[m % 8]).then_inc(made, 1)

        def middle(act, m):
            n, (_, rows, _s), c = chunks[m]
            act.wait_ge(rest1, m + 1)
            nc.scalar.activation(part[n % 2][1][0:rows, c * CH:(c + 1) * CH], rest[m % 2][0:rows, :],
                                 ACT.Copy).then_inc(mid, 1)

        @block.scalar
        def _(act):
            for m, (n, (_, rows, _s), c) in enumerate(chunks):
                cols = slice(c * CH, (c + 1) * CH)
                act.wait_ge(made, m + 1)
                if n >= 2 and c == 0:
                    act.wait_ge(stored[n % 2], 16 * stores_before[n])
                nc.scalar.activation(part[n % 2][0][0:rows, cols], bank[m % 8][0:rows, :], ACT.Copy).then_inc(high, 1)
                if m >= 1:
                    middle(act, m - 1)
            middle(act, len(chunks) - 1)

        def lowest(v, m):
            n, (_, rows, _s), c = chunks[m]
            cols = slice(c * CH, (c + 1) * CH)
            v.wait_ge(mid, m + 1)
            nc.vector.tensor_tensor(part[n % 2][2][0:rows, cols], rest[m % 2][0:rows, :],
                                    part[n % 2][1][0:rows, cols], ALU.subtract).then_inc(low, 1)

        @block.vector
        def _(v):
            for m, (n, (_, rows, _s), c) in enumerate(chunks):
                v.wait_ge(high, m + 1)
                if m >= 2:
                    v.wait_ge(low, m - 1)
                nc.vector.tensor_tensor(rest[m % 2][0:rows, :], bank[m % 8][0:rows, :],
                                        part[n % 2][0][0:rows, c * CH:(c + 1) * CH], ALU.subtract).then_inc(rest1, 1)
                if m >= 1:
                    lowest(v, m - 1)
            lowest(v, len(chunks) - 1)


def part_rows(scratch, first, rows):
    return [(scratch[n, first:first + rows, :], n) for n in range(3)]


def load_split(eng, dst, scratch, first, j0, j1, blocks, loaded):
    for block, n in enumerate(blocks):
        rows = scratch[n, bass.ds(first + j0 * HD, (j1 - j0) * HD), :]
        eng.dma_start(dst[block * HD:(block + 1) * HD, j0:j1, :],
                      rows.rearrange("(j d) t -> d j t", d=HD)).then_inc(loaded, 16)


def full_attention(nc, q_parts, k_parts, values, o_rows, identf, scale):
    steps = NC * TB
    per = CH // P
    units = GH * per * NC
    turn_at = 4
    uses = units + 1
    ahead = 2
    with ExitStack() as ctx:
        sc = Scope(nc, ctx, "a0")
        q_st = [sc.sb(f"q{i}", [ROWS + SHIFT, NC, GH, CH], BF16) for i in range(2)]
        k_st = [sc.sb(f"k{i}", [ROWS + SHIFT, GH, S], BF16) for i in range(2)]
        v_st = [sc.sb(f"v{i}", [P, TB, GH, VW]) for i in range(2)]
        prob = [sc.sb(f"prob{i}", [P, 2, CH]) for i in range(4)]
        o_sb = [sc.sb(f"o{i}", [P, S]) for i in range(2)]
        peak = sc.sb("peak", [P, units])
        top = sc.sb("top", [P, P])
        shift = [sc.sb(f"shift{i}", [GH * per, P], BF16) for i in range(3)]
        left = [sc.sb(f"left{i}", [GH * per, P]) for i in range(2)]
        score = [sc.ps(f"score{i}", [P, 2, CH]) for i in range(2)]
        o_ps = sc.ps("o_ps", [P, CH])
        wide = [sc.ps(f"wide{i}", [P, CH]) for i in range(3)]
        first_loaded = [sc.sem(f"first_loaded{i}") for i in range(2)]
        rest_loaded = [sc.sem(f"rest_loaded{i}") for i in range(2)]
        o_stored = [sc.sem(f"o_stored{i}") for i in range(2)]
        v_ready, v_blank, ones_set = (sc.sem(n) for n in ("v_ready", "v_blank", "ones_set"))
        scores_ready, exp_done, pv_done, o_copied = (sc.sem(n) for n in ("scores_ready", "exp_done", "pv_done", "o_copied"))
        wide_ready, wide_used, top_ready, shift_ready, shift_loaded = (
            sc.sem(n) for n in ("wide_ready", "wide_used", "top_ready", "shift_ready", "shift_loaded"))
        dve = sc.sem("dve")
        block = ctx.enter_context(nc.Block())

        def groups(eng, one):
            with eng.Fori(0, G // 2 - 1) as pair:
                one(pair, 0, True)
                one(pair, 1, True)
            one(G // 2 - 1, 0, True)
            one(G // 2 - 1, 1, False)

        def load_part(sp, i, group, j0, j1, loaded):
            first = group * GH * HD + j0 * HD
            for block_, n in enumerate(Q_PARTS):
                for j in range(j0, j1):
                    sp.dma_start(q_st[i][block_ * HD:(block_ + 1) * HD, :, j, :],
                                 q_parts[n, bass.ds(first + (j - j0) * HD, HD), :].rearrange("d (c t) -> d c t", t=CH)
                                 ).then_inc(loaded[i], 16)
            for block_, n in enumerate(K_PARTS):
                sp.dma_start(k_st[i][block_ * HD:(block_ + 1) * HD, j0:j1, :],
                             k_parts[n, bass.ds(first, (j1 - j0) * HD), :].rearrange("(j d) t -> d j t", d=HD)
                             ).then_inc(loaded[i], 16)

        def loads(heads):
            return 16 * NP_ * (heads + 1)

        def load_group(sp, i, group):
            load_part(sp, i, group, 0, 1, first_loaded)
            load_part(sp, i, group, 1, GH, rest_loaded)

        def load_shift(sp, m, i, c):
            sp.wait_ge(shift_ready, m + 2)
            for n in range(SHIFT):
                sp.dma_start(q_st[i][ROWS + n:ROWS + n + 1, bass.ds(c, 1), :, :].rearrange("o c j t -> o (c j t)")
                             .rearrange("o (a b) -> o a b", b=P), shift[n][:]).then_inc(shift_loaded, 16)

        @block.sync
        def _(sp):
            load_group(sp, 0, 0)

            def store(i, g, c):
                sp.wait_ge(o_copied, NC * g + c + 2)
                sp.dma_start(o_rows[bass.ds(g, 1), :, bass.ds(c * CH, CH)]
                             .rearrange("g p n -> (g p) n"), o_sb[i][:, bass.ds(c * CH, CH)]).then_inc(o_stored[i], 16)

            def one(pair, i, more):
                g = 2 * pair + i
                m = NC * g
                if more:
                    sp.wait_ge(exp_done, 2 * steps * g + 2)
                    load_group(sp, 1 - i, g + 1)
                with sp.Fori(0, NC - 1) as c:
                    load_shift(sp, m + c + 1, i, c + 1)
                    store(i, g, c)
                if more:
                    load_shift(sp, m + NC, 1 - i, 0)
                store(i, g, NC - 1)

            load_shift(sp, 0, 0, 0)
            groups(sp, one)
            for i in range(2):
                sp.wait_ge(o_stored[i], 16 * NC * (G // 2 + 1))

        @block.gpsimd
        def _(pool):
            for i in range(2):
                nc.gpsimd.memset(k_st[i][ROWS:ROWS + SHIFT, :, :], 1.0).then_inc(ones_set, 1)
                pool.wait_ge(ones_set, i + 1)
                nc.gpsimd.memset(v_st[i][:], 0.0).then_inc(v_blank, 1)
                pool.wait_ge(v_blank, 2 * i + 1)
                nc.gpsimd.memset(v_st[i][:, :, :, HD:HD + 1], 1.0).then_inc(v_blank, 1)
                pool.wait_ge(v_blank, 2 * i + 2)

            def one(pair, i):
                g = 2 * pair + i
                if not isinstance(pair, int):
                    pool.wait_ge(pv_done, steps * (g - 1) + 2)
                nc.gpsimd.tensor_copy(v_st[i][:, :, :, 0:HD],
                                      values[:, bass.ds(g, 1), :, :].rearrange("p g i (j d) -> p (g i) j d", d=HD)).then_inc(v_ready, 1)

            one(0, 0)
            one(0, 1)
            with pool.Fori(1, G // 2) as pair:
                one(pair, 0)
                one(pair, 1)

        def scores(pe, i, c, kt, half):
            for j in range(2):
                head = 2 * half + j
                last = nc.tensor.matmul(score[half][:, j, :], k_st[i][:, head, kt * P:(kt + 1) * P],
                                        q_st[i][:, bass.ds(c, 1), head, :].rearrange("p c t -> p (c t)"), start=True, stop=True)
            last.then_inc(scores_ready, 1)

        def await_wide_bank(pe, r, x):
            pe.wait_ge(wide_used, uses * r + (x + 1 if x >= 3 else (2, 3, 1)[x]))

        def wide_use(pe, r, i, c, x):
            if x == turn_at:
                turn_top(pe, r, x)
                return
            u = x - (x > turn_at)
            head, qt, n = u // (per * NC), u // NC % per, u % NC
            await_wide_bank(pe, r, x)
            q_flat = q_st[i][0:ROWS, :, :, :].rearrange("p c j t -> p (c j t)")
            nc.tensor.matmul(wide[x % 3][:], q_flat[:, bass.ds(c * (GH * CH) + (head * CH + qt * P), P)],
                             k_st[i][0:ROWS, head, n * CH:(n + 1) * CH], start=True, stop=True).then_inc(wide_ready, 1)

        def turn_top(pe, r, x):
            pe.wait_ge(top_ready, r + 1)
            await_wide_bank(pe, r, x)
            nc.tensor.transpose(wide[x % 3][:, 0:P], top[:], identf[:]).then_inc(wide_ready, 1)

        @block.tensor
        def _(pe):
            nc.tensor.sem_inc(exp_done, 2)
            nc.tensor.sem_inc(pv_done, 2)
            nc.tensor.sem_inc(o_copied, 1)
            nc.tensor.sem_inc(wide_used, 3)
            pe.wait_ge(first_loaded[0], loads(1))
            with pe.Fori(0, ahead) as r:
                for x in range(uses):
                    if x == units // GH + 1:
                        pe.wait_ge(rest_loaded[0], loads(GH - 1))
                    wide_use(pe, r, 0, r, x)
            pe.wait_ge(ones_set, 2)
            pe.wait_ge(shift_loaded, 16 * SHIFT)
            for half in range(2):
                scores(pe, 0, 0, 0, half)

            def chunk(pair, i, c, source, following):
                g = 2 * pair + i
                m = NC * g + c
                x = 0
                for kt in range(TB):
                    s = steps * g + TB * c + kt
                    if kt + 1 == TB and following:
                        pe.wait_ge(shift_loaded, 16 * SHIFT * (m + 2))
                    for half, wide_units in enumerate((1, 1, 2)):
                        for _ in range(wide_units + (kt == 1 and half == 0) if source else 0):
                            wide_use(pe, m + ahead, source[0], source[1], x)
                            x += 1
                        if half < 2 and (kt + 1 < TB or following):
                            pe.wait_ge(exp_done, 2 * (s + 1) + half + 1)
                            if kt + 1 < TB:
                                scores(pe, i, c, kt + 1, half)
                            else:
                                scores(pe, following[0], following[1], 0, half)
                    if isinstance(m, int) and m + ahead == NC * G and kt == 0:
                        turn_top(pe, m + ahead, 0)
                    if kt == 0:
                        pe.wait_ge(v_ready, g + 1)
                        pe.wait_ge(o_copied, m + 1)
                    pe.wait_ge(exp_done, 2 * s + 4)
                    for head in range(GH):
                        last = nc.tensor.matmul(o_ps[head * VW:(head + 1) * VW, :], v_st[i][:, kt, head, :],
                                                prob[2 * (kt % 2) + head // 2][:, head % 2, :],
                                                start=kt == 0, stop=kt == TB - 1)
                    last.then_inc(pv_done, 1)

            def one(pair, i, more):
                with pe.Fori(0, NC - ahead) as c:
                    chunk(pair, i, c, (i, c + ahead), (i, c + 1))
                if more:
                    pe.wait_ge(first_loaded[1 - i], loads(1) * (pair + i + 1))
                    pe.wait_ge(rest_loaded[1 - i], loads(GH - 1) * (pair + i + 1))
                chunk(pair, i, NC - 2, (1 - i, 0) if more else None, (i, NC - 1))
                chunk(pair, i, NC - 1, (1 - i, 1) if more else None, (1 - i, 0) if more else None)

            groups(pe, one)

        @block.scalar
        def _(act):
            with act.Fori(0, G) as g:
                with act.Fori(0, NC) as c:
                    for kt in range(TB):
                        s = steps * g + TB * c + kt
                        act.wait_ge(pv_done, s + 1)
                        for half in range(2):
                            act.wait_ge(scores_ready, 2 * s + half + 1)
                            nc.scalar.activation(prob[2 * (kt % 2) + half][:], score[half][:], ACT.Exp,
                                                 scale=scale).then_inc(exp_done, 1)

        @block.vector
        def _(v):
            nc.vector.sem_inc(o_stored[0], 16 * NC)
            nc.vector.sem_inc(o_stored[1], 16 * NC)
            nc.vector.memset(top[:], 0.0).then_inc(top_ready, 1)

            def shifts(r, x):
                v.wait_ge(wide_ready, uses * r + x + 1)
                turned = wide[x % 3][0:GH * per, 0:P]
                nc.vector.tensor_copy(shift[0][:], turned).then_inc(dve, 1)
                v.wait_ge(dve, 3 * r + 1)
                nc.vector.tensor_tensor(left[0][:], turned, shift[0][:], ALU.subtract).then_inc(wide_used, 1)
                v.wait_ge(wide_used, uses * r + x + 4)
                nc.vector.tensor_copy(shift[1][:], left[0][:]).then_inc(dve, 1)
                v.wait_ge(dve, 3 * r + 2)
                nc.vector.tensor_tensor(left[1][:], left[0][:], shift[1][:], ALU.subtract).then_inc(dve, 1)
                v.wait_ge(dve, 3 * r + 3)
                nc.vector.tensor_copy(shift[2][:], left[1][:]).then_inc(shift_ready, 1)
                v.wait_ge(shift_ready, r + 1)

            def maxima(r, shift_read):
                for x in range(uses):
                    if x == turn_at:
                        if shift_read is not None:
                            v.wait_ge(shift_loaded, 16 * SHIFT * shift_read)
                        shifts(r, x)
                    else:
                        u = x - (x > turn_at)
                        v.wait_ge(wide_ready, uses * r + x + 1)
                        nc.vector.tensor_reduce(peak[:, u:u + 1], wide[x % 3][:], AX.X, ALU.max).then_inc(wide_used, 1)
                v.wait_ge(wide_used, uses * (r + 1) + 3)
                nc.vector.tensor_reduce(top[:, 0:GH * per], peak[:].rearrange("p (a n) -> p a n", n=NC), AX.X,
                                        ALU.max, negate=True).then_inc(top_ready, 1)
                v.wait_ge(top_ready, r + 2)

            def copy_out(pair, i, c):
                g = 2 * pair + i
                v.wait_ge(o_stored[i], 16 * NC * (pair + 1))
                v.wait_ge(pv_done, steps * g + TB * (c + 1) + 2)
                nc.vector.tensor_copy(o_sb[i][:, bass.ds(c * CH, CH)], o_ps[:]).then_inc(o_copied, 1)

            for r in range(ahead):
                maxima(r, None)

            def one(pair, i, more):
                m = NC * (2 * pair + i)
                with v.Fori(0, NC if more else NC - ahead) as c:
                    maxima(m + c + ahead, m + c + 1)
                    copy_out(pair, i, c)
                if not more:
                    v.wait_ge(shift_loaded, 16 * SHIFT * (NC * G - 1))
                    shifts(NC * G, 0)
                    copy_out(pair, i, NC - 2)
                    copy_out(pair, i, NC - 1)

            groups(v, one)


def causal_plan():
    plan = []
    for c in range(NC):
        per = CH // P
        for kt in range(per * (c + 1)):
            skip = max(0, kt - per * c) * P
            plan.append((c, c * CH + skip, CH - skip, kt, 0 if kt >= per * c else None))
    return plan


def window_plan():
    plan = []
    for qt in range(TB):
        plan.append((qt, qt * P, P, qt, 0))
        if qt:
            plan.append((qt, qt * P, WIN, qt - 1, P))
    return plan


def masked_attention(nc, tag, q_parts, k_parts, values, o_rows, mask, identb, plan, span, scale):
    steps = len(plan)
    spans = S // span
    with ExitStack() as ctx:
        sc = Scope(nc, ctx, tag)
        q_st = [sc.sb(f"q{i}", [ROWS, GH, S], BF16) for i in range(2)]
        k_st = [sc.sb(f"k{i}", [ROWS, S], BF16) for i in range(2)]
        v_st = [sc.sb(f"v{i}", [P, TB, VW]) for i in range(2)]
        prob = [sc.sb(f"prob{i}", [P, 2, CH]) for i in range(4)]
        o_sb = [sc.sb(f"o{i}", [P, S]) for i in range(2)]
        score = [sc.ps(f"score{i}", [P, 2, CH]) for i in range(3)]
        o_ps = [sc.ps(f"o_ps{i}", [P, CH]) for i in range(2)]
        loaded = [sc.sem(f"loaded{i}") for i in range(2)]
        o_stored = [sc.sem(f"o_stored{i}") for i in range(2)]
        v_ready, v_blank = sc.sem("v_ready"), sc.sem("v_blank")
        scores_ready, exp_done, pv_done, o_copied = (sc.sem(n) for n in ("scores_ready", "exp_done", "pv_done", "o_copied"))
        block = ctx.enter_context(nc.Block())
        first_of = {}
        last_of = {}
        for n, (c, *_r) in enumerate(plan):
            first_of.setdefault(c, n)
            last_of[c] = n
        jobs = 2 * steps

        def buffer_before(e):
            if e >= 3:
                return e - 3
            return max(x for x in range(jobs) if x % 3 == e) - jobs

        @block.sync
        def _(sp):
            def load_group(pair, i):
                g = 2 * pair + i
                for block_, n in enumerate(Q_PARTS):
                    sp.dma_start(q_st[i][block_ * HD:(block_ + 1) * HD, :, :],
                                 q_parts[n, bass.ds(g * GH * HD, GH * HD), :].rearrange("(j d) t -> d j t", d=HD)
                                 ).then_inc(loaded[i], 16)
                for block_, n in enumerate(K_PARTS):
                    sp.dma_start(k_st[i][block_ * HD:(block_ + 1) * HD, :],
                                 k_parts[n, bass.ds(g * HD, HD), :]).then_inc(loaded[i], 16)

            def store(pair, i):
                g = 2 * pair + i
                for c in range(spans):
                    sp.wait_ge(o_copied, spans * g + c + 3)
                    sp.dma_start(o_rows[bass.ds(g, 1), :, c * span:(c + 1) * span].rearrange("g p n -> (g p) n"),
                                 o_sb[i][:, c * span:(c + 1) * span]).then_inc(o_stored[i], 16)

            load_group(0, 0)
            load_group(0, 1)
            with sp.Fori(0, G // 2 - 1) as pair:
                for i in range(2):
                    store(pair, i)
                    load_group(pair + 1, i)
            for i in range(2):
                store(G // 2 - 1, i)
            for i in range(2):
                sp.wait_ge(o_stored[i], 16 * spans * (G // 2 + 1))

        @block.gpsimd
        def _(pool):
            for i in range(2):
                nc.gpsimd.memset(v_st[i][:], 0.0).then_inc(v_blank, 1)
                pool.wait_ge(v_blank, 2 * i + 1)
                nc.gpsimd.memset(v_st[i][:, :, HD:HD + 1], 1.0).then_inc(v_blank, 1)
            pool.wait_ge(v_blank, 4)

            def one(pair, i):
                g = 2 * pair + i
                if not isinstance(pair, int):
                    pool.wait_ge(pv_done, steps * (g - 1) + 2)
                nc.gpsimd.tensor_copy(v_st[i][:, :, 0:HD],
                                      values[:, bass.ds(g, 1), :, :].rearrange("p g i n -> p (g i) n")).then_inc(v_ready, 1)

            one(0, 0)
            one(0, 1)
            with pool.Fori(1, G // 2) as pair:
                one(pair, 0)
                one(pair, 1)

        @block.tensor
        def _(pe):
            nc.tensor.sem_inc(exp_done, jobs)
            nc.tensor.sem_inc(pv_done, 2)
            nc.tensor.sem_inc(o_copied, 2)

            def scores(i, g, n):
                _, q0, w, kt, masked = plan[n]
                for half in range(2):
                    e = 2 * n + half
                    pe.wait_ge(exp_done, jobs * (g + 1) + buffer_before(e) + 1)
                    out = score[e % 3]
                    for j in range(2):
                        last = nc.tensor.matmul(out[:, j, 0:w], k_st[i][:, kt * P:(kt + 1) * P],
                                                q_st[i][:, 2 * half + j, q0:q0 + w], start=True, stop=True)
                    if masked is not None:
                        for j in range(2):
                            m = min(w, P)
                            last = nc.tensor.matmul(out[:, j, 0:m], identb[:], mask[:, masked:masked + m],
                                                    start=False, stop=True, skip_group_check=True)
                    last.then_inc(scores_ready, 1)

            with pe.Fori(0, G // 2) as pair:
                for i in range(2):
                    g = 2 * pair + i
                    pe.wait_ge(loaded[i], 16 * 2 * NP_ * (pair + 1))
                    scores(i, g, 0)
                    pe.wait_ge(v_ready, g + 1)
                    for n, (c, q0, w, kt, masked) in enumerate(plan):
                        if n + 1 < steps:
                            scores(i, g, n + 1)
                        if n == first_of[c]:
                            pe.wait_ge(o_copied, spans * g + c + 1)
                        pe.wait_ge(exp_done, jobs * (g + 1) + 2 * n + 2)
                        at = q0 - c * span
                        for head in range(GH):
                            last = nc.tensor.matmul(o_ps[c % 2][head * VW:(head + 1) * VW, at:at + w], v_st[i][:, kt, :],
                                                    prob[2 * (n % 2) + head // 2][:, head % 2, 0:w],
                                                    start=n == first_of[c], stop=n == last_of[c], skip_group_check=True)
                        last.then_inc(pv_done, 1)

        @block.scalar
        def _(act):
            nc.scalar.sem_inc(o_stored[0], 16 * spans)
            nc.scalar.sem_inc(o_stored[1], 16 * spans)
            with act.Fori(0, G // 2) as pair:
                for i in range(2):
                    g = 2 * pair + i
                    for n, (c, q0, w, kt, masked) in enumerate(plan):
                        act.wait_ge(pv_done, steps * g + n + 1)
                        for half in range(2):
                            e = 2 * n + half
                            act.wait_ge(scores_ready, jobs * g + e + 1)
                            nc.scalar.activation(prob[2 * (n % 2) + half][:, :, 0:w], score[e % 3][:, :, 0:w], ACT.Exp,
                                                 scale=scale).then_inc(exp_done, 1)

        @block.vector
        def _(v):
            with v.Fori(0, G // 2) as pair:
                for i in range(2):
                    g = 2 * pair + i
                    v.wait_ge(o_stored[i], 16 * spans * (pair + 1))
                    for c in range(spans):
                        v.wait_ge(pv_done, steps * g + last_of[c] + 1 + 2)
                        nc.vector.tensor_copy(o_sb[i][:, c * span:(c + 1) * span], o_ps[c % 2][:, 0:span]).then_inc(o_copied, 1)


def gather_heads(nc, tag, o_rows, att, ident):
    hg = H // GH
    with ExitStack() as ctx:
        sc = Scope(nc, ctx, tag)
        rows = [sc.sb(f"rows{b}", [P, hg, S]) for b in range(B)]
        inverse = [sc.sb(f"inverse{i}", [P, H, 1]) for i in range(2)]
        bank = [sc.ps(f"bank{i}", [P, H, VW]) for i in range(4)]
        loaded = [sc.sem(f"loaded{b}") for b in range(B)]
        turned, inverted, scaled = (sc.sem(n) for n in ("turned", "inverted", "scaled"))
        block = ctx.enter_context(nc.Block())

        @block.sync
        def _(sp):
            for b in range(B):
                sp.dma_start(rows[b][:], o_rows[b * hg:(b + 1) * hg].rearrange("g p t -> p g t")).then_inc(loaded[b], 16)

        @block.tensor
        def _(pe):
            for n in range(NT):
                b, i = n // TB, n % TB
                if i == 0:
                    pe.wait_ge(loaded[b], 16)
                if n >= 4:
                    pe.wait_ge(scaled, n - 3)
                for g in range(hg):
                    last = nc.tensor.transpose(bank[n % 4][:, g * GH:(g + 1) * GH, :].rearrange("p h n -> p (h n)"),
                                               rows[b][:, g, i * P:(i + 1) * P], ident[:])
                last.then_inc(turned, 1)

        @block.vector
        def _(v):
            for n in range(NT + 1):
                if n < NT:
                    v.wait_ge(turned, n + 1)
                    if n >= 2:
                        v.wait_ge(scaled, n - 1)
                    nc.vector.reciprocal(inverse[n % 2][:], bank[n % 4][:, :, HD:HD + 1]).then_inc(inverted, 1)
                if n >= 1:
                    v.wait_ge(inverted, n)
                    nc.vector.tensor_tensor(att[:, n - 1, :].rearrange("p (h n) -> p h n", n=HD),
                                            bank[(n - 1) % 4][:, :, 0:HD],
                                            inverse[(n - 1) % 2][:].to_broadcast([P, H, HD]), ALU.mult).then_inc(scaled, 1)


def project_split(nc, tag, xt, scratches, w_sb, w_loads):
    jobs = []
    for which, scratch in enumerate(scratches):
        for b in range(B):
            for half in range(2):
                jobs.append(((which, b, half), P, part_rows(scratch, b * D + half * P, P)))

    def make_chunk(job, c, bank):
        (which, b, half), _, _ = job
        for k in range(KT):
            last = nc.tensor.matmul(bank[:], w_sb[which][:, k, half * P:(half + 1) * P],
                                    xt[:, k, b * S + c * CH:b * S + (c + 1) * CH], start=k == 0, stop=k == KT - 1)
        return last

    split_and_store(nc, tag, jobs, make_chunk, w_loads)


def token_projection(nc, tag, lhs, kparts, rhs, width, out_of, loads=()):
    with ExitStack() as ctx:
        sc = Scope(nc, ctx, tag)
        bank = [sc.ps(f"bank{i}", [P, CH]) for i in range(6)]
        loaded, made, copied_act, copied_dve = (sc.sem(n) for n in ("loaded", "made", "copied_act", "copied_dve"))
        block = ctx.enter_context(nc.Block())

        @block.sync
        def _(sp):
            for out, source in loads:
                sp.dma_start(out, source).then_inc(loaded, 16)

        @block.tensor
        def _(pe):
            if loads:
                pe.wait_ge(loaded, 16 * len(loads))
            for n in range(NT):
                if n >= 6:
                    pe.wait_ge((copied_act, copied_dve)[n % 2], (n - 6) // 2 + 1)
                for k in range(kparts):
                    last = nc.tensor.matmul(bank[n % 6][:, 0:width], lhs(n, k), rhs(k), start=k == 0, stop=k == kparts - 1)
                last.then_inc(made, 1)

        @block.scalar
        def _(act):
            for n in range(0, NT, 2):
                act.wait_ge(made, n + 1)
                for view, cols in out_of(n):
                    last = nc.scalar.activation(view, bank[n % 6][:, cols], ACT.Copy)
                last.then_inc(copied_act, 1)

        @block.vector
        def _(v):
            for n in range(1, NT, 2):
                v.wait_ge(made, n + 1)
                for view, cols in out_of(n):
                    last = nc.vector.tensor_copy(view, bank[n % 6][:, cols])
                last.then_inc(copied_dve, 1)


QK = (H + KVH) * HD


ROPE_HEADS = 14


def rope_and_norm(nc, tag, qkv, tables):
    nh = H + KVH
    with ExitStack() as ctx:
        sc = Scope(nc, ctx, tag)
        cos, sin = sc.sb("cos", [P, TB, HD // 2]), sc.sb("sin", [P, TB, HD // 2])
        halves = sc.sb("halves", [P, 4, TB, nh, HD // 2])
        square = [halves[:, 2 * b:2 * b + 2].rearrange("p a i h n -> p (a i h n)")
                  .rearrange("p (i h n) -> p i h n", h=nh, n=HD) for b in range(B)]
        total = [sc.sb(f"total{b}", [P, TB, nh]) for b in range(B)]
        loaded, dve, pool_own, rotated_dve, rotated_pool, squared, asked, rooted, inverted, pooled = (
            sc.sem(n) for n in ("loaded", "dve", "pool_own", "rotated_dve", "rotated_pool", "squared", "asked", "rooted",
                                "inverted", "pooled"))
        block = ctx.enter_context(nc.Block())

        def qk(b, heads):
            return qkv[:, b * TB:(b + 1) * TB, 0:QK].rearrange("p i (h n) -> p i h n", n=HD)[:, :, heads, :]

        def rotate(eng, step, b, heads, rotated):
            x = qk(b, heads)
            n = heads.stop - heads.start
            half = [halves[:, i, :, heads, :] for i in range(4)]
            even, odd = x[:, :, :, 0::2], x[:, :, :, 1::2]
            c, s = (t[:].rearrange("p i (h n) -> p i h n", h=1).to_broadcast([P, TB, n, HD // 2]) for t in (cos, sin))
            eng.tensor_tensor(half[0], even, c, ALU.mult)
            eng.tensor_tensor(half[1], odd, s, ALU.mult)
            eng.tensor_tensor(half[2], even, s, ALU.mult)
            step(eng.tensor_tensor(half[3], odd, c, ALU.mult))
            step(eng.tensor_tensor(even, half[0], half[1], ALU.subtract))
            eng.tensor_tensor(odd, half[2], half[3], ALU.add).then_inc(rotated, 1)

        def divide(eng, b, heads):
            x = qk(b, heads)
            n = heads.stop - heads.start
            inverse = total[b][:, :, heads].rearrange("p i (h n) -> p i h n", n=1)
            return eng.tensor_tensor(x, x, inverse.to_broadcast([P, TB, n, HD]), ALU.mult)

        first, others = slice(0, ROPE_HEADS), slice(ROPE_HEADS, nh)

        @block.sync
        def _(sp):
            for t, s in ((cos, 0), (sin, 1)):
                sp.dma_start(t[:], tables[s]).then_inc(loaded, 16)

        @block.scalar
        def _(act):
            act.wait_ge(rotated_dve, B)
            act.wait_ge(rotated_pool, B)
            for b in range(B):
                nc.scalar.activation(square[b].rearrange("p i h n -> p i (h n)"), qkv[:, b * TB:(b + 1) * TB, 0:QK],
                                     ACT.Square).then_inc(squared, 1)
            for b in range(B):
                act.wait_ge(asked, b + 1)
                nc.scalar.activation(total[b][:], total[b][:], ACT.Sqrt).then_inc(rooted, 1)

        @block.gpsimd
        def _(pool):
            step = Chain(pool, pool_own)
            pool.wait_ge(loaded, 32)
            for b in range(B):
                if b:
                    pool.wait_ge(rotated_pool, b)
                rotate(nc.gpsimd, step, b, others, rotated_pool)
            for b in range(B):
                pool.wait_ge(inverted, b + 1)
                divide(nc.gpsimd, b, others).then_inc(pooled, 1)
            pool.wait_ge(pooled, B)

        @block.vector
        def _(v):
            step = Chain(v, dve)
            v.wait_ge(loaded, 32)
            for b in range(B):
                if b:
                    v.wait_ge(rotated_dve, b)
                rotate(nc.vector, step, b, first, rotated_dve)
            for b in range(B):
                v.wait_ge(squared, b + 1)
                step(nc.vector.tensor_reduce(total[b][:], square[b], AX.X, ALU.add))
                nc.vector.tensor_scalar(total[b][:], total[b][:], 1.0 / HD, 1e-6, ALU.mult, ALU.add).then_inc(asked, 1)
                v.wait_ge(rooted, b + 1)
                nc.vector.reciprocal(total[b][:], total[b][:]).then_inc(inverted, 1)
                v.wait_ge(inverted, b + 1)
                step(divide(nc.vector, b, first))


def split_heads(nc, tag, qkv, ident, q_parts, k_parts):
    jobs = []
    for b in range(B):
        for half in range(2):
            jobs.append(((b, half * P, P), P, part_rows(q_parts, b * D + half * P, P)))
        jobs.append(((b, H * HD, KVH * HD), KVH * HD, part_rows(k_parts, b * KVH * HD, KVH * HD)))

    def make_chunk(job, c, bank):
        (b, col, rows), _, _ = job
        for t in range(CH // P):
            last = nc.tensor.transpose(bank[0:rows, t * P:(t + 1) * P],
                                       qkv[:, b * TB + c * (CH // P) + t, col:col + rows], ident[:])
        return last

    split_and_store(nc, tag, jobs, make_chunk, [])


def output_projection(nc, tag, att_t, w_sb, w_dram, x):
    with ExitStack() as ctx:
        sc = Scope(nc, ctx, tag)
        bank = [sc.ps(f"bank{i}", [P, D]) for i in range(4)]
        loaded, made, added = (sc.sem(n) for n in ("loaded", "made", "added"))
        block = ctx.enter_context(nc.Block())

        @block.sync
        def _(sp):
            sp.dma_start(w_sb[:], w_dram.rearrange("(k p) n -> p k n", p=P)).then_inc(loaded, 16)

        @block.tensor
        def _(pe):
            pe.wait_ge(loaded, 16)
            for n in range(NT):
                if n >= 4:
                    pe.wait_ge(added, n - 3)
                for k in range(KT):
                    last = nc.tensor.matmul(bank[n % 4][:], att_t[:, k, n * P:(n + 1) * P], w_sb[:, k, :],
                                            start=k == 0, stop=k == KT - 1)
                last.then_inc(made, 1)

        @block.vector
        def _(v):
            for n in range(NT):
                v.wait_ge(made, n + 1)
                nc.vector.tensor_tensor(x[:, n, :], bank[n % 4][:], x[:, n, :], ALU.add).then_inc(added, 1)


NE = 8
INTER = 512
IC = INTER // P
ROUTED_TILES = 2 * T // P + NE
TILES = NT + ROUTED_TILES
SLOTS = TILES * P


def at_least(eng, sem, value):
    if not isinstance(value, int) or value > 0:
        eng.wait_ge(sem, value)


def route(nc, tag, xt, gate_cols, consts, weight, slot, expert_of, h, rows):
    ne = NT * NE
    with ExitStack() as ctx:
        sc = Scope(nc, ctx, tag)
        gate = sc.sb("gate", [P, KT, NE])
        before, ones, back, tiles = sc.sb("before", [P, P]), sc.sb("ones", [P, P]), sc.sb("back", [P, 1, NE]), sc.sb("tiles", [P, TILES, 1])
        prob, left, hot, taken, pos = (sc.sb(n, [P, NT, NE]) for n in ("prob", "left", "hot", "taken", "pos"))
        hots = [sc.sb(f"hots{i}", [P, NT, NE]) for i in range(2)]
        sums, best, first, total = (sc.sb(n, [P, NT, 1]) for n in ("sums", "best", "first", "total"))
        tops = [sc.sb(f"tops{i}", [P, NT, 1]) for i in range(2)]
        run = sc.sb("run", [P, NE, NT])
        line = sc.sb("line", [P, NT])
        count, count_i, ends, base = sc.sb("count", [P, NE]), sc.sb("count_i", [P, NE], I32), sc.sb("ends", [P, NE]), sc.sb("base", [P, 1, NE])
        owner = sc.sb("owner", [P, TILES, NE])
        owned = sc.sb("owned", [P, TILES])
        at = sc.sb("at", [P, NT])
        blank = sc.sb("blank", [P, 8, D])
        logits, inside, whole = (sc.ps(n, [P, NT, NE]) for n in ("logits", "inside", "whole"))
        loaded, dve, logits_ready, centred, exp_done, counted, ranks_ready, routed, blank_set, blanked, copied = (
            sc.sem(n) for n in ("loaded", "dve", "logits_ready", "centred", "exp_done", "counted", "ranks_ready",
                                "routed", "blank_set", "blanked", "copied"))
        sent = sc.software_sem("sent")
        block = ctx.enter_context(nc.Block())

        @block.sync
        def _(sp):
            sp.dma_start(gate[:], gate_cols).then_inc(loaded, 16)
            for dst, source in zip((before, ones, back, tiles), consts):
                sp.dma_start(dst[:], source).then_inc(loaded, 16)
            sp.wait_ge(blank_set, 1)
            for n in range(NT, TILES, 8):
                sp.dma_start(rows[n * P:(n + 8) * P, :].rearrange("(i p) d -> p i d", p=P), blank[:]).then_inc(blanked, 16)
            sp.dma_start(rows[0:T, :].rearrange("(i p) d -> p i d", p=P), h[:]).then_inc(copied, 16)
            sp.wait_ge(copied, 16)

        @block.tensor
        def _(pe):
            pe.wait_ge(loaded, 16 * 5)
            for n in range(NT):
                for k in range(KT):
                    last = nc.tensor.matmul(logits[:, n, :], xt[:, k, n * P:(n + 1) * P], gate[:, k, :],
                                            start=k == 0, stop=k == KT - 1)
            last.then_inc(logits_ready, 1)
            pe.wait_ge(counted, 1)
            nc.tensor.matmul(inside[:], before[:], taken[:], start=True, stop=True)
            nc.tensor.matmul(whole[:], ones[:], taken[:], start=True, stop=True).then_inc(ranks_ready, 1)

        @block.scalar
        def _(act):
            act.wait_ge(centred, 1)
            nc.scalar.activation(prob[:], prob[:], ACT.Exp).then_inc(exp_done, 1)

        @block.vector
        def _(v):
            step = Chain(v, dve)
            tt, ts, stt, red = nc.vector.tensor_tensor, nc.vector.tensor_scalar, nc.vector.scalar_tensor_tensor, nc.vector.tensor_reduce

            def per_expert(x):
                return x.to_broadcast([P, NT, NE])

            nc.vector.memset(blank[:], 0.0).then_inc(blank_set, 1)
            v.wait_ge(loaded, 16 * 5)
            v.wait_ge(logits_ready, 1)
            step(red(best[:, :, 0], logits[:], AX.X, ALU.max))
            tt(prob[:], logits[:], per_expert(best[:]), ALU.subtract).then_inc(centred, 1)
            v.wait_ge(exp_done, 1)
            step(red(sums[:, :, 0], prob[:], AX.X, ALU.add))
            step(nc.vector.reciprocal(sums[:], sums[:]))
            step(tt(prob[:], prob[:], per_expert(sums[:]), ALU.mult))
            step(nc.vector.tensor_copy(left[:], prob[:]))
            for i in range(2):
                step(red(tops[i][:, :, 0], left[:], AX.X, ALU.max))
                step(tt(hot[:], left[:], per_expert(tops[i][:]), ALU.is_equal))
                step(tt(hot[:], hot[:], back[:].to_broadcast([P, NT, NE]), ALU.mult))
                step(red(first[:, :, 0], hot[:], AX.X, ALU.max))
                step(tt(hots[i][:], hot[:], per_expert(first[:]), ALU.is_equal))
                step(stt(left[:], hots[i][:], -2.0, left[:], ALU.mult, ALU.add))
            tt(taken[:], hots[0][:], hots[1][:], ALU.add).then_inc(counted, 1)
            step(tt(total[:], tops[0][:], tops[1][:], ALU.add))
            step(ts(total[:], total[:], 1e-5, None, ALU.add))
            step(nc.vector.reciprocal(total[:], total[:]))
            for i in range(2):
                step(tt(weight[:, i, :], tops[i][:, :, 0], total[:, :, 0], ALU.mult))
            v.wait_ge(ranks_ready, 1)
            step(nc.vector.tensor_copy(pos[:], whole[:]))
            step(nc.vector.memset(line[:], 1.0))
            for e in range(NE):
                last = nc.vector.tensor_tensor_scan(run[:, e, :], line[:], pos[:, :, e], 0.0, ALU.mult, ALU.add)
            step(last)
            step(nc.vector.tensor_copy(count[:], run[:, :, NT - 1]))
            step(tt(pos[:], run[:].rearrange("p e i -> p i e"), pos[:], ALU.subtract))
            step(tt(pos[:], pos[:], inside[:], ALU.add))
            step(ts(count[:], count[:], float(P - 1), None, ALU.add))
            step(nc.vector.tensor_copy(count_i[:], count[:]))
            step(ts(count_i[:], count_i[:], P.bit_length() - 1, None, ALU.logical_shift_right))
            step(nc.vector.tensor_copy(count[:], count_i[:]))
            step(nc.vector.tensor_tensor_scan(ends[:], line[:, 0:NE], count[:], float(NT), ALU.mult, ALU.add))
            step(tt(base[:, 0, :], ends[:], count[:], ALU.subtract))
            step(tt(owner[:], tiles[:].to_broadcast([P, TILES, NE]), base[:].to_broadcast([P, TILES, NE]), ALU.is_ge))
            step(red(owned[:], owner[:], AX.X, ALU.add))
            step(ts(owned[:], owned[:], -1.0, None, ALU.add))
            step(ts(owned[:, 0:NT], owned[:, 0:NT], 0.0, float(NE), ALU.mult, ALU.add))
            step(nc.vector.tensor_copy(expert_of[:], owned[:]))
            step(stt(pos[:], base[:].to_broadcast([P, NT, NE]), float(P), pos[:], ALU.mult, ALU.add))
            for i in range(2):
                step(tt(hot[:], hots[i][:], pos[:], ALU.mult))
                step(red(at[:], hot[:], AX.X, ALU.add))
                step(nc.vector.tensor_copy(slot[:, i, :], at[:]))
            nc.vector.tensor_copy(at[:], at[:]).then_inc(routed, 1)

        @block.gpsimd
        def _(pool):
            pool.wait_ge(routed, 1)
            pool.wait_ge(blanked, 16 * (ROUTED_TILES // 8))
            for n in range(NT):
                for i in range(2):
                    pool.indirect_dma_start(rows, bass.IndirectOffsetOnAxis(ap=slot[:, i, n:n + 1], axis=0),
                                            h[:, n, :], None).then_inc(sent, 16)
            pool.wait_ge(sent, 16 * 2 * NT)


def experts(nc, tag, rows, results, expert_of, w_gate, w_up, w_down, ident):
    with ExitStack() as ctx:
        sc = Scope(nc, ctx, tag)
        x_sb = [sc.sb(f"x{i}", [P, D]) for i in range(2)]
        xt_sb = [sc.sb(f"xt{i}", [P, KT, P]) for i in range(2)]
        silu = [sc.sb(f"silu{i}", [P, INTER]) for i in range(2)]
        hid = [sc.sb(f"hid{i}", [P, INTER]) for i in range(2)]
        ht_sb = [sc.sb(f"ht{i}", [P, IC, P]) for i in range(2)]
        y_sb = [sc.sb(f"y{i}", [P, D]) for i in range(2)]
        x_ps, h_ps, y_ps = sc.ps("x_ps", [P, KT, P]), sc.ps("h_ps", [P, IC, P]), sc.ps("y_ps", [P, D])
        g_ps = [sc.ps(f"g{i}", [P, INTER]) for i in range(2)]
        u_ps = [sc.ps(f"u{i}", [P, INTER]) for i in range(2)]
        loaded = [sc.sem(f"loaded{i}") for i in range(2)]
        stored = [sc.sem(f"stored{i}") for i in range(2)]
        x_turned, xt_copied, g_ready, u_ready, silu_done, hid_done, h_turned, ht_copied, y_ready, y_copied = (
            sc.sem(n) for n in ("x_turned", "xt_copied", "g_ready", "u_ready", "silu_done", "hid_done", "h_turned",
                                "ht_copied", "y_ready", "y_copied"))
        block = ctx.enter_context(nc.Block())

        def steps(eng, one):
            for t in range(3):
                one(t, t % 2, t // 2)
            with eng.Fori(1, TILES // 2 - 1) as pair:
                one(2 * pair + 1, 1, pair)
                one(2 * pair + 2, 0, pair + 1)
            one(TILES - 1, 1, TILES // 2 - 1)

        def some(t):
            return not isinstance(t, int)

        @block.sync
        def _(sp):
            def load(t, i):
                at_least(sp, x_turned, t - 1)
                sp.dma_start(x_sb[i][:], rows[bass.ds(t * P, P), :]).then_inc(loaded[i], 16)

            def store(t, i):
                sp.wait_ge(y_copied, t + 1)
                sp.dma_start(results[bass.ds(t * P, P), :], y_sb[i][:]).then_inc(stored[i], 16)

            load(0, 0)

            def one(t, i, n):
                if some(t) or t < TILES - 1:
                    load(t + 1, 1 - i)
                if some(t) or t > 0:
                    store(t - 1, 1 - i)

            steps(sp, one)
            store(TILES - 1, 1)
            for i in range(2):
                sp.wait_ge(stored[i], 16 * (TILES // 2))

        @block.tensor
        def _(pe):
            def turn_x(t, i, n):
                pe.wait_ge(loaded[i], 16 * (n + 1))
                at_least(pe, xt_copied, t)
                for k in range(KT):
                    last = nc.tensor.transpose(x_ps[:, k, :], x_sb[i][:, k * P:(k + 1) * P], ident[:])
                last.then_inc(x_turned, 1)

            def up(t, i):
                e = pe.value_load(expert_of[0:1, bass.ds(t, 1)], min_val=0, max_val=NE)
                pe.wait_ge(xt_copied, t + 1)
                at_least(pe, hid_done, t - 1)
                for bank, w, ready in ((g_ps[i], w_gate, g_ready), (u_ps[i], w_up, u_ready)):
                    for k in range(KT):
                        last = nc.tensor.matmul(bank[:], xt_sb[i][:, k, :],
                                                w[:, k, bass.ds(e, 1), :].rearrange("p e n -> p (e n)"),
                                                start=k == 0, stop=k == KT - 1)
                    last.then_inc(ready, 1)
                return e

            def turn_h(t, i):
                pe.wait_ge(hid_done, t + 1)
                at_least(pe, ht_copied, t)
                for k in range(IC):
                    last = nc.tensor.transpose(h_ps[:, k, :], hid[i][:, k * P:(k + 1) * P], ident[:])
                last.then_inc(h_turned, 1)

            def down(t, i):
                e = pe.value_load(expert_of[0:1, bass.ds(t, 1)], min_val=0, max_val=NE)
                pe.wait_ge(ht_copied, t + 1)
                at_least(pe, y_copied, t)
                for k in range(IC):
                    last = nc.tensor.matmul(y_ps[:], ht_sb[i][:, k, :],
                                            w_down[:, k, bass.ds(e, 1), :].rearrange("p e n -> p (e n)"),
                                            start=k == 0, stop=k == IC - 1)
                last.then_inc(y_ready, 1)

            turn_x(0, 0, 0)

            def one(t, i, n):
                if some(t) or t > 0:
                    turn_h(t - 1, 1 - i)
                up(t, i)
                if some(t) or t > 0:
                    down(t - 1, 1 - i)
                if some(t) or t < TILES - 1:
                    turn_x(t + 1, 1 - i, n + i)

            steps(pe, one)
            turn_h(TILES - 1, 1)
            down(TILES - 1, 1)

        @block.scalar
        def _(act):
            def copy_h(t, i):
                act.wait_ge(h_turned, t + 1)
                at_least(act, y_ready, t - 1)
                nc.scalar.activation(ht_sb[i][:], h_ps[:], ACT.Copy).then_inc(ht_copied, 1)

            def one(t, i, n):
                if some(t) or t > 0:
                    copy_h(t - 1, 1 - i)
                act.wait_ge(g_ready, t + 1)
                at_least(act, hid_done, t - 1)
                nc.scalar.activation(silu[i][:], g_ps[i][:], ACT.Silu).then_inc(silu_done, 1)

            steps(act, one)
            copy_h(TILES - 1, 1)

        @block.vector
        def _(v):
            def copy_x(t, i):
                v.wait_ge(x_turned, t + 1)
                at_least(v, u_ready, t - 1)
                nc.vector.tensor_copy(xt_sb[i][:], x_ps[:]).then_inc(xt_copied, 1)

            def copy_y(t, i, n):
                v.wait_ge(y_ready, t + 1)
                at_least(v, stored[i], 16 * n)
                nc.vector.tensor_copy(y_sb[i][:], y_ps[:]).then_inc(y_copied, 1)

            copy_x(0, 0)

            def one(t, i, n):
                v.wait_ge(u_ready, t + 1)
                v.wait_ge(silu_done, t + 1)
                at_least(v, h_turned, t - 1)
                nc.vector.tensor_tensor(hid[i][:], silu[i][:], u_ps[i][:], ALU.mult).then_inc(hid_done, 1)
                if some(t) or t > 0:
                    copy_y(t - 1, 1 - i, n - (1 - i))
                if some(t) or t < TILES - 1:
                    copy_x(t + 1, 1 - i)

            steps(v, one)
            copy_y(TILES - 1, 1, TILES // 2 - 1)


def combine(nc, tag, x, gate, results, weight, slot):
    bufs = 4
    with ExitStack() as ctx:
        sc = Scope(nc, ctx, tag)
        acc = [sc.sb(f"acc{i}", [P, D]) for i in range(bufs)]
        picked = [[sc.sb(f"picked{i}_{n}", [P, D]) for n in range(2)] for i in range(bufs)]
        loaded = [sc.sem(f"loaded{i}") for i in range(bufs)]
        fetched = [sc.software_sem(f"fetched{i}") for i in range(bufs)]
        summed, dve = sc.sem("summed"), sc.sem("dve")
        block = ctx.enter_context(nc.Block())

        @block.sync
        def _(sp):
            for n in range(NT):
                at_least(sp, summed, n - bufs + 1)
                sp.dma_start(acc[n % bufs][:], results[n * P:(n + 1) * P, :]).then_inc(loaded[n % bufs], 16)

        @block.gpsimd
        def _(pool):
            for n in range(NT):
                at_least(pool, summed, n - bufs + 1)
                for i in range(2):
                    pool.indirect_dma_start(picked[n % bufs][i][:], None, results,
                                            bass.IndirectOffsetOnAxis(ap=slot[:, i, n:n + 1], axis=0)
                                            ).then_inc(fetched[n % bufs], 16)

        @block.vector
        def _(v):
            step = Chain(v, dve)
            for n in range(NT):
                i, turn = n % bufs, n // bufs + 1
                v.wait_ge(loaded[i], 16 * turn)
                v.wait_ge(fetched[i], 32 * turn)
                for c in range(2):
                    step(nc.vector.scalar_tensor_tensor(acc[i][:], picked[i][c][:], weight[:, c, n:n + 1], acc[i][:],
                                                        ALU.mult, ALU.add))
                step(nc.vector.tensor_tensor(acc[i][:], acc[i][:], gate[:, n // TB, :], ALU.mult))
                nc.vector.tensor_tensor(x[:, n, :], x[:, n, :], acc[i][:], ALU.add).then_inc(summed, 1)


def recurrent_cell(nc, tag, xt, x, gate, w_dram, biases, c0_cols, ident, out):
    names = ("wf", "uf", "wi", "ui", "wc", "uc", "wo", "uo")
    with ExitStack() as ctx:
        sc = Scope(nc, ctx, tag)
        w = {n: sc.sb(n, [P, KT, D]) for n in names}
        bias = sc.sb("bias", [P, 4, KT])
        c0 = sc.sb("c0", [P, KT, 1])
        bias0 = sc.sb("bias0", [P, 3, KT])
        cell = [sc.sb(f"cell{i}", [P, KT, S]) for i in range(2)]
        gates = [[sc.sb(f"gate{i}_{n}", [P, CH]) for n in range(3)] for i in range(2)]
        prod = [sc.sb(f"prod{i}", [P, CH]) for i in range(2)]
        hidden = [sc.sb(f"hidden{i}", [P, KT, CH]) for i in range(2)]
        added = [sc.sb(f"added{i}", [P, 2, D]) for i in range(2)]
        bank = [[sc.ps(f"bank{i}_{n}", [P, CH]) for n in range(3)] for i in range(2)]
        back = [sc.ps(f"back{i}", [P, 2, D]) for i in range(2)]
        loaded = [sc.sem(f"loaded{i}") for i in range(len(names))]
        small, start_ready, dve, bias0_ready = sc.sem("small"), sc.sem("start_ready"), sc.sem("dve"), sc.sem("bias0_ready")
        made, gated, mixed, h_done, turned, scaled, summed, stored = (
            sc.sem(n) for n in ("made", "gated", "mixed", "h_done", "turned", "scaled", "summed", "stored"))
        block = ctx.enter_context(nc.Block())
        jobs = [(t, c, m) for t in range(B) for c in range(NC) for m in range(KT)]
        outs = [(t, c) for t in range(B) for c in range(NC)]
        kinds = (("wf", "uf"), ("wi", "ui"), ("wc", "uc"))

        def need(pe, *which):
            for n in which:
                pe.wait_ge(loaded[names.index(n)], 16)

        @block.sync
        def _(sp):
            for n, b in enumerate(biases):
                sp.dma_start(bias[:, n, :], b).then_inc(small, 16)
            sp.dma_start(c0[:, :, 0], c0_cols).then_inc(small, 16)
            for i, n in enumerate(names):
                sp.dma_start(w[n][:], w_dram[n].rearrange("(k p) n -> p k n", p=P)).then_inc(loaded[i], 16)
            view = out.rearrange("b (i p) d -> p (b i) d", p=P)
            for n in range(len(outs) * 2):
                sp.wait_ge(summed, n + 1)
                sp.dma_start(view[:, 2 * n:2 * n + 2, :], x[:, 2 * n:2 * n + 2, :]).then_inc(stored, 16)
            sp.wait_ge(stored, 16 * len(outs) * 2)

        @block.tensor
        def _(pe):
            pe.wait_ge(small, 16 * 5)
            need(pe, "uf", "ui", "uc")
            for n, (_, u) in enumerate(kinds):
                for m in range(KT):
                    for k in range(KT):
                        last = nc.tensor.matmul(back[0][:, 0, 2 * n + m:2 * n + m + 1], w[u][:, k, m * P:(m + 1) * P],
                                                c0[:, k, :], start=k == 0, stop=k == KT - 1)
            last.then_inc(start_ready, 1)
            need(pe, "wf", "wi", "wc")
            for n, (t, c, m) in enumerate(jobs):
                at_least(pe, gated, 3 * (n - 1))
                for g, (wn, un) in enumerate(kinds):
                    dst = bank[n % 2][g]
                    terms = [(w[wn][:, k, m * P:(m + 1) * P], xt[:, k, t * S + c * CH:t * S + (c + 1) * CH]) for k in range(KT)]
                    if t:
                        pe.wait_ge(mixed, KT * (c + 1))
                        terms += [(w[un][:, k, m * P:(m + 1) * P], cell[0][:, k, c * CH:(c + 1) * CH]) for k in range(KT)]
                    for k, (l, r) in enumerate(terms):
                        last = nc.tensor.matmul(dst[:], l, r, start=k == 0, stop=k == len(terms) - 1)
                    last.then_inc(made, 1)
            need(pe, "wo", "uo")

            def turn(n):
                pe.wait_ge(h_done, KT * (n + 1))
                for q in range(2):
                    at_least(pe, scaled, 2 * n + q - 1)
                    if n == 0:
                        pe.wait_ge(bias0_ready, 1)
                    for i in range(2):
                        for k in range(KT):
                            last = nc.tensor.transpose(back[q][:, i, k * P:(k + 1) * P],
                                                       hidden[n % 2][:, k, (2 * q + i) * P:(2 * q + i + 1) * P], ident[:])
                    last.then_inc(turned, 1)

            for n, (t, c) in enumerate(outs):
                for m in range(KT):
                    if n == 0:
                        pe.wait_ge(gated, 3 * len(jobs))
                    else:
                        at_least(pe, h_done, KT * (n - 2) + m + 1)
                    pe.wait_ge(mixed, KT * (NC + c + 1))
                    terms = [(w["wo"][:, k, m * P:(m + 1) * P], xt[:, k, t * S + c * CH:t * S + (c + 1) * CH]) for k in range(KT)]
                    terms += [(w["uo"][:, k, m * P:(m + 1) * P], cell[1][:, k, c * CH:(c + 1) * CH]) for k in range(KT)]
                    for k, (l, r) in enumerate(terms):
                        last = nc.tensor.matmul(bank[n % 2][m][:], l, r, start=k == 0, stop=k == len(terms) - 1)
                    last.then_inc(made, 1)
                if n:
                    turn(n - 1)
            turn(len(outs) - 1)

        @block.scalar
        def _(act):
            act.wait_ge(bias0_ready, 1)
            for n, (t, c, m) in enumerate(jobs):
                for g in range(3):
                    act.wait_ge(made, 3 * n + g + 1)
                    if g == 0:
                        at_least(act, mixed, n - 1)
                    b = bias0[:, g, m:m + 1] if t == 0 else bias[:, g, m:m + 1]
                    nc.scalar.activation(gates[n % 2][g][:], bank[n % 2][g][:], ACT.Tanh if g == 2 else ACT.Sigmoid,
                                         bias=b).then_inc(gated, 1)
            for n, (t, c) in enumerate(outs):
                for m in range(KT):
                    act.wait_ge(made, 3 * len(jobs) + KT * n + m + 1)
                    at_least(act, turned, 2 * (n - 1))
                    nc.scalar.activation(hidden[n % 2][:, m, :], bank[n % 2][m][:], ACT.Tanh,
                                         bias=bias[:, 3, m:m + 1]).then_inc(h_done, 1)

        @block.vector
        def _(v):
            step = Chain(v, dve)
            v.wait_ge(start_ready, 1)
            nc.vector.tensor_tensor(bias0[:].rearrange("p n m -> p (n m)"), back[0][:, 0, 0:6],
                                    bias[:, 0:3, :].rearrange("p n m -> p (n m)"), ALU.add).then_inc(bias0_ready, 1)
            for n, (t, c, m) in enumerate(jobs):
                f, i, g = gates[n % 2]
                cols = slice(c * CH, (c + 1) * CH)
                v.wait_ge(gated, 3 * (n + 1))
                at_least(v, mixed, n - 1)
                step(nc.vector.tensor_tensor(prod[n % 2][:], i[:], g[:], ALU.mult))
                if t == 0:
                    nc.vector.scalar_tensor_tensor(cell[0][:, m, cols], f[:], c0[:, m, :], prod[n % 2][:],
                                                   ALU.mult, ALU.add).then_inc(mixed, 1)
                else:
                    step(nc.vector.tensor_tensor(f[:], f[:], cell[0][:, m, cols], ALU.mult))
                    nc.vector.tensor_tensor(cell[1][:, m, cols], f[:], prod[n % 2][:], ALU.add).then_inc(mixed, 1)
            for n, (t, c) in enumerate(outs):
                for q in range(2):
                    k = 2 * n + q
                    v.wait_ge(turned, k + 1)
                    at_least(v, summed, k - 1)
                    nc.vector.tensor_tensor(added[q][:], back[q][:], gate[:, t:t + 1, :].to_broadcast([P, 2, D]),
                                            ALU.mult).then_inc(scaled, 1)
                    v.wait_ge(scaled, k + 1)
                    nc.vector.tensor_tensor(x[:, 2 * k:2 * k + 2, :], x[:, 2 * k:2 * k + 2, :], added[q][:],
                                            ALU.add).then_inc(summed, 1)


def load_constants(nc, i, ident, identb, masks):
    with ExitStack() as ctx:
        sc = Scope(nc, ctx, "constants")
        masks_sb = sc.sb("masks_sb", [P, 2, P + WIN])
        loaded, cast = sc.sem("loaded"), sc.sem("cast")
        block = ctx.enter_context(nc.Block())

        @block.sync
        def _(sp):
            sp.dma_start(ident[:], i["ident"]).then_inc(loaded, 16)
            sp.dma_start(masks_sb[:], i["masks"]).then_inc(loaded, 16)

        @block.vector
        def _(v):
            v.wait_ge(loaded, 32)
            nc.vector.tensor_copy(identb[:], ident[:]).then_inc(cast, 1)
            nc.vector.tensor_copy(masks[:], masks_sb[:]).then_inc(cast, 1)
            v.wait_ge(cast, 2)


def reset_semaphores(nc, name, numbers):
    with nc.Block(name) as block:
        @block.gpsimd
        def _(pool):
            pool.sem_clear(numbers)


def adaln_layers(nc, i, out):
    q_parts = nc.dram_tensor("q_parts", (3, B * D, S), BF16).ap()
    k_parts = nc.dram_tensor("k_parts", (3, B * D, S), BF16).ap()
    k1_parts = nc.dram_tensor("k1_parts", (3, B * KVH * HD, S), BF16).ap()
    o_rows = nc.dram_tensor("o_rows", (G, P, S), F32).ap()
    rows = nc.dram_tensor("expert_rows", (SLOTS, D), F32).ap()
    results = nc.dram_tensor("expert_results", (SLOTS, D), F32).ap()
    free = list(nc.free_semaphores)
    numbers = range(min(free), max(free) + 1)
    with ExitStack() as ctx:
        def keep(stack, name, shape, dt=F32):
            return stack.enter_context(nc.sbuf_tensor(name, shape, dt))

        x = keep(ctx, "x", [P, NT, D])
        mod = keep(ctx, "mod", [P, B, 6, D])
        ident = keep(ctx, "ident", [P, P])
        identb = keep(ctx, "identb", [P, P], BF16)
        masks = keep(ctx, "masks", [P, 2, P + WIN], BF16)
        load_constants(nc, i, ident, identb, masks)

        def mod_row(which):
            return lambda b: mod[:, b, which:which + 1, :]

        def weight_rows(row):
            return lambda b: row[0][:], (lambda b: row[1][:]) if len(row) > 1 else None

        modulation(nc, "m0", i["L0_c"], i["L0_wmod"], mod)
        with ExitStack() as stage:
            values = keep(stage, "values0", [P, G, TB, GH * HD])
            with ExitStack() as inner:
                xt = keep(inner, "xt0", [P, KT, T])
                with ExitStack() as normed:
                    h, hn = keep(normed, "h0", [P, NT, D]), keep(normed, "hn0", [P, NT, D])
                    row = [keep(normed, f"row0_{n}", [P, 1, D]) for n in range(2)]
                    norms(nc, "n0", [(x, h, 1e-5, False, mod_row(CA), mod_row(SA)), (h, hn, 1e-6, False, *weight_rows(row))],
                          loads=[(x[:], i["L0_attn_x"].rearrange("b (i p) d -> p (b i) d", p=P)),
                                 row_load(row[0], i["L0_attn_ln_scale"]), row_load(row[1], i["L0_attn_ln_bias"])],
                          last_sum=(x, mod_row(GA), hn, h), turned=(xt, ident))
                w_qk = [keep(inner, f"w{n}", [P, KT, D]) for n in "qk"]
                w_v = keep(inner, "wv", [P, KT, D])

                def w_view(name):
                    return i[name].rearrange("(k p) n -> p k n", p=P)

                project_split(nc, "p0", xt, (q_parts, k_parts), w_qk,
                              [(w_qk[0][:], w_view("L0_attn_wq")), (w_qk[1][:], w_view("L0_attn_wk"))])
                token_projection(nc, "v0", lambda n, k: xt[:, k, n * P:(n + 1) * P], KT, lambda k: w_v[:, k, :], D,
                                 lambda n: [(values[:, (n // TB) * 4 + g, n % TB, :], slice(g * 64, (g + 1) * 64)) for g in range(4)],
                                 [(w_v[:], w_view("L0_attn_wv"))])
            full_attention(nc, q_parts, k_parts, values, o_rows, ident, float(D) ** -0.5)
        with ExitStack() as stage:
            weight = keep(stage, "weight", [P, 2, NT])
            slot = keep(stage, "slot", [P, 2, NT], I32)
            expert_of = keep(stage, "expert_of", [P, TILES], I32)
            with ExitStack() as inner:
                h = keep(inner, "h1", [P, NT, D])
                xt = keep(inner, "xt1", [P, KT, T])
                with ExitStack() as normed:
                    att = keep(normed, "att0", [P, NT, D])
                    gather_heads(nc, "g0", o_rows, att, ident)
                    row = [keep(normed, f"row1_{n}", [P, 1, D]) for n in range(2)]
                    reset_semaphores(nc, "reset0", numbers)
                    norms(nc, "n1", [(x, h, 1e-5, False, mod_row(CB), mod_row(SB)), (h, att, 1e-5, False, *weight_rows(row))],
                          loads=[row_load(row[0], i["L0_ffn_ln_scale"]), row_load(row[1], i["L0_ffn_ln_bias"])],
                          x_sum=(x, mod_row(GA), att), turned=(xt, ident))
                route(nc, "rt", xt, i["gate_cols"], (i["before"], i["ones"], i["back"], i["tiles"]), weight, slot,
                      expert_of, h, rows)
            with ExitStack() as inner:
                w_gate = keep(inner, "w_gate", [P, KT, NE + 1, INTER])
                w_up = keep(inner, "w_up", [P, KT, NE + 1, INTER])
                w_down = keep(inner, "w_down", [P, IC, NE + 1, D])
                load_weights(nc, i, w_gate, w_up, w_down)
                experts(nc, "ex", rows, results, expert_of, w_gate, w_up, w_down, ident)
            combine(nc, "cb", x, mod[:, :, GB, :], results, weight, slot)

        reset_semaphores(nc, "reset1", numbers)

        modulation(nc, "m1", i["L1_c"], i["L1_wmod"], mod)
        with ExitStack() as stage:
            hid = keep(stage, "hid", [P, NT, D])
            with ExitStack() as inner:
                hn = keep(inner, "hn2", [P, NT, D])
                layer1_attention(nc, i, "g", [(x, hid, 1e-5, False, mod_row(CA), mod_row(SA))], hn, hid, ident, identb, masks[:, 0, :], q_parts, k1_parts, o_rows, causal_plan(), CH)
            reset_semaphores(nc, "reset2", numbers)
            with ExitStack() as inner:
                hn = keep(inner, "hn3", [P, NT, D])
                layer1_attention(nc, i, "l", [], hn, hid, ident, identb, masks[:, 1, :], q_parts, k1_parts, o_rows, window_plan(), P)
            xt = keep(stage, "xt4", [P, KT, T])
            norms(nc, "n4", [(x, hid, 1e-5, False, mod_row(CB), mod_row(SB))], x_sum=(x, mod_row(GA), hid),
                  turned=(xt, ident))
            recurrent_cell(nc, "rc", xt, x, mod[:, :, GB, :], {n: i[f"cell_{n}"] for n in
                           ("wf", "uf", "wi", "ui", "wc", "uc", "wo", "uo")},
                           [i[f"cell_b{n}"] for n in "fico"], i["cell_c0"], ident, out)


def load_weights(nc, i, w_gate, w_up, w_down):
    with ExitStack() as ctx:
        loaded = ctx.enter_context(nc.semaphore("expert_weights_loaded"))
        block = ctx.enter_context(nc.Block())

        @block.sync
        def _(sp):
            for dst, routed, shared in ((w_gate, "Wg", "sWg"), (w_up, "Wu", "sWu"), (w_down, "Wd", "sWd")):
                for e in range(NE + 1):
                    source = i[f"L0_ffn_{routed}"][e] if e < NE else i[f"L0_ffn_{shared}"]
                    sp.dma_start(dst[:, :, e, :], source.rearrange("(k p) n -> p k n", p=P)).then_inc(loaded, 16)
            sp.wait_ge(loaded, 16 * 3 * (NE + 1))


def layer1_attention(nc, i, kind, before, hn, hid, ident, identb, mask, q_parts, k_parts, o_rows, plan, span):
    with ExitStack() as stage:
        def keep(stack, name, shape, dt=F32):
            return stack.enter_context(nc.sbuf_tensor(f"{kind}_{name}", shape, dt))

        values = keep(stage, "values", [P, G, TB, HD])
        with ExitStack() as heads:
            qkv = keep(heads, "qkv", [P, NT, QK])
            with ExitStack() as inner:
                xt = keep(inner, "xt", [P, KT, T])
                row = keep(inner, "row", [P, 1, D])
                norms(nc, f"{kind}n", before + [(hid, hn, 1e-6, True, lambda b: row[:], None)],
                      loads=[row_load(row, i["L1_attn_norm1_w" if kind == "g" else "L1_attn_norm2_w"])], turned=(xt, ident))

                def w_view(name):
                    return i[f"L1_attn_{name}"].rearrange("(k p) n -> p k n", p=P)

                def v_out(first):
                    return lambda n: [(values[:, (n // TB) * KVH:(n // TB + 1) * KVH, n % TB, :], slice(first, first + KVH * HD))]

                width = KVH * HD
                if kind == "g":
                    latent = hn[0:width, 0:T // D, :].rearrange("p i d -> p (i d)")
                    w_q, w_down = keep(inner, "w_q", [P, KT, D]), keep(inner, "w_down", [P, KT, width])
                    w_up = keep(inner, "w_up", [width, 2 * width])
                    token_projection(nc, "gq", lambda n, k: xt[:, k, n * P:(n + 1) * P], KT, lambda k: w_q[:, k, :], D,
                                     lambda n: [(qkv[:, n, 0:D], slice(0, D))], [(w_q[:], w_view("g_wq"))])
                    latent_projection(nc, "gl", xt, w_down, latent,
                                      [(w_down[:], w_view("g_kv_down")), (w_up[:, 0:width], i["L1_attn_g_k_up"]),
                                       (w_up[:, width:2 * width], i["L1_attn_g_v_up"])])
                    token_projection(nc, "gkv", lambda n, k: latent[:, n * P:(n + 1) * P], 1, lambda k: w_up[:], 2 * width,
                                     lambda n: [(qkv[:, n, D:QK], slice(0, width))] + v_out(width)(n))
                else:
                    w_qkv = keep(inner, "w_qkv", [P, KT, QK + width])
                    token_projection(nc, "lq", lambda n, k: xt[:, k, n * P:(n + 1) * P], KT, lambda k: w_qkv[:, k, :], QK + width,
                                     lambda n: [(qkv[:, n, :], slice(0, QK))] + v_out(QK)(n),
                                     [(w_qkv[:, :, 0:D], w_view("l_wq")), (w_qkv[:, :, D:QK], w_view("l_wk")),
                                      (w_qkv[:, :, QK:QK + width], w_view("l_wv"))])
            rope_and_norm(nc, f"{kind}r", qkv, i["rope_g" if kind == "g" else "rope_l"])
            split_heads(nc, f"{kind}s", qkv, ident, q_parts, k_parts)
        masked_attention(nc, f"{kind}a", q_parts, k_parts, values, o_rows, mask, identb, plan, span, float(HD) ** -0.5)
    gather_heads(nc, f"{kind}g", o_rows, hn, ident)
    with ExitStack() as stage:
        att_t = stage.enter_context(nc.sbuf_tensor(f"{kind}_att_t", [P, KT, T], F32))
        w_o = stage.enter_context(nc.sbuf_tensor(f"{kind}_w_o", [P, KT, D], F32))
        transpose_tokens(nc, f"{kind}u", hn, att_t, ident)
        output_projection(nc, f"{kind}o", att_t, w_o, i[f"L1_attn_{kind}_wo"], hid)


def latent_projection(nc, tag, xt, w_sb, latent, loads):
    width = KVH * HD
    with ExitStack() as ctx:
        sc = Scope(nc, ctx, tag)
        bank = [sc.ps(f"bank{n}", [P, CH]) for n in range(4)]
        loaded, made, copied = (sc.sem(n) for n in ("loaded", "made", "copied"))
        block = ctx.enter_context(nc.Block())

        @block.sync
        def _(sp):
            for out, source in loads:
                sp.dma_start(out, source).then_inc(loaded, 16)

        @block.tensor
        def _(pe):
            pe.wait_ge(loaded, 16 * len(loads))
            for n in range(T // CH):
                at_least(pe, copied, n - 3)
                for k in range(KT):
                    last = nc.tensor.matmul(bank[n % 4][0:width, :], w_sb[:, k, :], xt[:, k, n * CH:(n + 1) * CH],
                                            start=k == 0, stop=k == KT - 1)
                last.then_inc(made, 1)

        @block.vector
        def _(v):
            for n in range(T // CH):
                v.wait_ge(made, n + 1)
                nc.vector.tensor_copy(latent[:, n * CH:(n + 1) * CH], bank[n % 4][0:width, :]).then_inc(copied, 1)


def columns(a):
    return np.ascontiguousarray(np.moveaxis(a.reshape(*a.shape[:-1], KT, P), (-1, -2), (0, 1)))


def rope_table(base):
    inv = (np.float32(1.0) / np.float32(base) ** (np.arange(0, HD, 2, dtype=np.float32) / np.float32(HD))).astype(np.float32)
    angle = np.arange(S, dtype=np.float32)[:, None] * inv[None, :]
    both = np.stack([np.cos(angle), np.sin(angle)]).astype(np.float32)
    return np.ascontiguousarray(both.reshape(2, TB, P, HD // 2).transpose(0, 2, 1, 3))


def constants():
    eye = np.eye(P, dtype=np.float32)
    key, query = np.mgrid[0:P, 0:P]
    ahead = np.concatenate([query - key, (query - key)[:, 0:WIN] + P], axis=1)
    allowed = np.stack([ahead >= 0, (ahead >= 0) & (ahead < WIN)], axis=1)
    return {
        "ident": eye,
        "masks": np.where(allowed, 0.0, -1e30).astype(np.float32),
        "before": (key < query).astype(np.float32),
        "ones": np.ones((P, P), np.float32),
        "back": np.tile(np.arange(NE, 0, -1, dtype=np.float32), (P, 1, 1)),
        "tiles": np.tile(np.arange(TILES, dtype=np.float32)[:, None], (P, 1, 1)),
        "rope_g": rope_table(1e6),
        "rope_l": rope_table(1e4),
    }


AS_THEY_ARE = ("L0_attn_x", "L0_attn_ln_scale", "L0_attn_ln_bias", "L0_attn_wq", "L0_attn_wk", "L0_attn_wv",
               "L0_ffn_ln_scale", "L0_ffn_ln_bias", "L0_ffn_Wg", "L0_ffn_Wu", "L0_ffn_Wd", "L0_ffn_sWg", "L0_ffn_sWu",
               "L0_ffn_sWd", "L0_wmod", "L1_attn_norm1_w", "L1_attn_norm2_w", "L1_attn_g_wq", "L1_attn_g_kv_down",
               "L1_attn_g_k_up", "L1_attn_g_v_up", "L1_attn_g_wo", "L1_attn_l_wq", "L1_attn_l_wk", "L1_attn_l_wv",
               "L1_attn_l_wo", "L1_wmod")


def laid_out(inputs):
    arrays = {name: np.ascontiguousarray(inputs[name]) for name in AS_THEY_ARE}
    for name in ("L0_c", "L1_c"):
        arrays[name] = columns(np.asarray(inputs[name]))
    arrays["gate_cols"] = columns(np.asarray(inputs["L0_ffn_gate_w"]))
    for name in ("wf", "uf", "wi", "ui", "wc", "uc", "wo", "uo"):
        arrays[f"cell_{name}"] = np.ascontiguousarray(np.asarray(inputs[f"L1_ffn_{name}"]).T)
    for name in "fico":
        arrays[f"cell_b{name}"] = columns(np.asarray(inputs[f"L1_ffn_b{name}"]))
    arrays["cell_c0"] = columns(np.asarray(inputs["L1_ffn_in_c"]))
    return arrays | constants()


def kernel(**inputs):
    import concourse.bacc as bacc
    from concourse.bass_utils import run_bass_kernel_spmd

    arrays = laid_out(inputs)
    nc = bacc.Bacc("TRN2", target_bir_lowering=False, num_devices=1)
    handles = {n: nc.dram_tensor(f"in_{n}", a.shape, mybir.dt.from_np(a.dtype), kind="ExternalInput").ap() for n, a in arrays.items()}
    out = nc.dram_tensor("out", (B, S, D), F32, kind="ExternalOutput").ap()
    adaln_layers(nc, handles, out)
    return run_bass_kernel_spmd(nc, [{f"in_{n}": a for n, a in arrays.items()}], core_ids=[0]).results[0]["out"]
```

```python
from contextlib import ExitStack

import numpy as np
import concourse.bass as bass
from concourse import mybir

F32 = mybir.dt.float32
BF16 = mybir.dt.bfloat16
I32 = mybir.dt.int32
ACT = mybir.ActivationFunctionType
ALU = mybir.AluOpType
AX = mybir.AxisListType

P = 128
B, S, D = 2, 2048, 256
T = B * S
NT = T // P
TB = S // P
KT = D // P
H, HD = 16, 16
KVH = 4
GH = 4
G = B * H // GH
CH = 512
NC = S // CH
WIN = 64
VW = 32
Q_PARTS = (0, 0, 1, 1, 0, 2)
K_PARTS = (0, 1, 0, 1, 2, 0)
NP_ = len(Q_PARTS)
ROWS = NP_ * HD
SHIFT = 3
SA, CA, GA, SB, CB, GB = range(6)


class Chain:

    def __init__(self, eng, sem):
        self.eng, self.sem, self.n = eng, sem, 0

    def __call__(self, instruction):
        self.n += 1
        instruction.then_inc(self.sem, 1)
        self.eng.wait_ge(self.sem, self.n)


def at_least(eng, sem, value):
    if not isinstance(value, int) or value > 0:
        eng.wait_ge(sem, value)


class Scope:

    def __init__(self, nc, ctx, tag):
        self.nc, self.ctx, self.tag = nc, ctx, tag

    def sb(self, name, shape, dt=F32):
        return self.ctx.enter_context(self.nc.sbuf_tensor(f"{self.tag}_{name}", shape, dt))

    def ps(self, name, shape):
        used = int(np.prod(shape[1:]))
        banks = self.ctx.enter_context(self.nc.psum_tensor(f"{self.tag}_{name}", [P, -(-used // CH) * CH], F32))
        view = banks[:, 0:used]
        if len(shape) == 3:
            return view.rearrange("p (a b) -> p a b", b=shape[2])
        return view

    def sem(self, name):
        return self.ctx.enter_context(self.nc.semaphore(f"{self.tag}_{name}"))

    def software_sem(self, name):
        return self.nc.alloc_semaphore(f"{self.tag}_{name}")


def modulation(nc, sc, c_cols, w_mod, mod):
    c_sb = sc.sb("mod_c", [P, KT, B])
    sg = sc.sb("mod_silu", [P, KT, B])
    ones = sc.sb("mod_ones", [P, P])
    rep = sc.sb("mod_rep", [P, KT, B, P])
    w_sb = sc.sb("mod_w", [P, KT, 6 * D])
    sign = sc.sb("mod_sign", [P, B, D])
    size = sc.sb("mod_size", [P, B, D])
    bank = [sc.ps(f"mod_bank{i}", [P, CH]) for i in range(3)]
    c_loaded, w_loaded, silu_done, rep_done, rows_ready, rows_copied = (
        sc.sem(f"mod_{n}") for n in ("c_loaded", "w_loaded", "silu_done", "rep_done", "rows_ready", "rows_copied"))

    def sync(sp):
        sp.dma_start(c_sb[:], c_cols).then_inc(c_loaded, 16)
        sp.dma_start(w_sb[:], w_mod.rearrange("(k p) n -> p k n", p=P)).then_inc(w_loaded, 16)

    def act_part(act):
        act.wait_ge(c_loaded, 16)
        nc.scalar.activation(sg[:], c_sb[:], ACT.Silu).then_inc(silu_done, 1)

    def pe_part(pe):
        pe.wait_ge(w_loaded, 16)
        pe.wait_ge(rep_done, 1)
        for b in range(B):
            for n in range(3):
                if b:
                    pe.wait_ge(rows_copied, n + 1)
                for k in range(KT):
                    last = nc.tensor.matmul(bank[n][:], rep[:, k, b, :], w_sb[:, k, n * CH:(n + 1) * CH],
                                            start=k == 0, stop=k == KT - 1)
                last.then_inc(rows_ready, 1)

    def spread(v, step):
        step(nc.vector.memset(ones[:], 1.0))
        v.wait_ge(silu_done, 1)
        for k in range(KT):
            for b in range(B):
                last = nc.vector.tensor_scalar(rep[:, k, b, :], ones[:], sg[:, k, b:b + 1], None, ALU.mult)
        last.then_inc(rep_done, 1)

    def finish(v, step):
        for b in range(B):
            for n in range(3):
                v.wait_ge(rows_ready, 3 * b + n + 1)
                nc.vector.tensor_copy(mod[:, b, 2 * n:2 * n + 2, :].rearrange("p i d -> p (i d)"),
                                      bank[n][:]).then_inc(rows_copied, 1)
        v.wait_ge(rows_copied, 6)
        for i in (CA, CB):
            step(nc.vector.tensor_scalar(mod[:, :, i, :], mod[:, :, i, :], 1.0, None, ALU.add))
        for i in (GA, GB):
            gate = mod[:, :, i, :]
            step(nc.vector.tensor_scalar(sign[:], gate, 0.0, 2.0, ALU.is_ge, ALU.mult))
            step(nc.vector.scalar_tensor_tensor(size[:], gate, -1.0, gate, ALU.mult, ALU.max))
            step(nc.vector.tensor_scalar(size[:], size[:], 0.25, None, ALU.max))
            step(nc.vector.scalar_tensor_tensor(gate, sign[:], -1.0, size[:], ALU.add, ALU.mult))

    return sync, act_part, pe_part, spread, finish


SHARE = 10


def tiles_of(b, pool):
    return slice(b * TB + SHARE, (b + 1) * TB) if pool else slice(b * TB, b * TB + SHARE)


def on_rows(eng, step, b, pool, dst, src, row, op):
    tiles = tiles_of(b, pool)
    n = tiles.stop - tiles.start
    step(eng.tensor_tensor(dst[:, tiles, :], src[:, tiles, :], row(b).to_broadcast([P, n, D]), op))


def gated_sum(eng, step, b, pool, x, gate, add, scaled):
    tiles = tiles_of(b, pool)
    on_rows(eng, step, b, pool, scaled, add, gate, ALU.mult)
    step(eng.tensor_tensor(x[:, tiles, :], x[:, tiles, :], scaled[:, tiles, :], ALU.add))


def token_stats(nc, step, b, src, eps, rms, work, asked):
    tiles = slice(b * TB, (b + 1) * TB)
    stats, mean, rstd, tmp, _ = (w[:, tiles] for w in work)
    for i in range(TB):
        last = nc.vector.bn_stats(stats[:, i, :], src[:, b * TB + i, :])
    step(last)
    step(nc.vector.tensor_tensor(mean, stats[:, :, 1], stats[:, :, 4], ALU.add))
    step(nc.vector.tensor_scalar(mean, mean, 0.5, None, ALU.mult))
    step(nc.vector.tensor_tensor(tmp, stats[:, :, 1], stats[:, :, 4], ALU.subtract))
    step(nc.vector.scalar_tensor_tensor(tmp, tmp, 0.25, tmp, ALU.mult, ALU.mult))
    step(nc.vector.tensor_tensor(rstd, stats[:, :, 2], stats[:, :, 5], ALU.add))
    step(nc.vector.scalar_tensor_tensor(rstd, rstd, 1.0 / D, tmp, ALU.mult, ALU.add))
    if rms:
        step(nc.vector.tensor_tensor(tmp, mean, mean, ALU.mult))
        step(nc.vector.tensor_tensor(rstd, rstd, tmp, ALU.add))
    nc.vector.tensor_scalar(rstd, rstd, eps, None, ALU.add).then_inc(asked, 1)


def norms(nc, tag, passes, loads=(), x_loads=(), stores=(), x_sum=None, last_sum=None, turned=None, product=None,
          modulate=None):
    with ExitStack() as ctx:
        sc = Scope(nc, ctx, tag)
        works = [tuple(sc.sb(f"{name}{p}", [P, NT] + more) for name, more in
                       (("stats", [6]), ("mean", []), ("rstd", []), ("tmp", []), ("offset", []))) for p in range(len(passes))]
        loaded, asked, rooted, ready, applied, dve, pooled, pool_own = (
            sc.sem(n) for n in ("loaded", "asked", "rooted", "ready", "applied", "dve", "pooled", "pool_own"))
        scaled, bank_ready, bank_copied, stored = (sc.sem(n) for n in ("scaled", "bank_ready", "bank_copied", "stored"))
        bank = [sc.ps(f"bank{i}", [P, KT, 2 * P]) for i in range(4)] if turned else []
        parts = modulation(nc, sc, *modulate) if modulate else None
        product_bank = sc.ps("product_bank", [P, NT, product[0].shape[2]]) if product else None
        product_made = sc.sem("product_made")
        x_loaded = [sc.sem(f"x_loaded{b}") for b in range(B)]
        block = ctx.enter_context(nc.Block())
        summed = B if x_sum else 0
        own = TB - SHARE

        @block.sync
        def _(sp):
            for b, (dst, source) in enumerate(x_loads):
                sp.dma_start(dst, source).then_inc(x_loaded[b], 16)
                if b == 0 and parts:
                    parts[0](sp)
            for dst, source in loads:
                sp.dma_start(dst, source).then_inc(loaded, 16)
            for dst, source in stores:
                sp.dma_start(dst, source).then_inc(stored, 16)
            if stores:
                sp.wait_ge(stored, 16 * len(stores))

        @block.tensor
        def _(pe):
            if parts:
                parts[2](pe)
            if not turned:
                return
            src, ident = passes[-1][1], turned[1]
            if product:
                pe.wait_ge(loaded, 16 * len(loads))

            def multiply(n):
                pe.wait_ge(bank_copied, n + 1)
                for t in range(2 * n, 2 * n + 2):
                    for k in range(KT):
                        last = nc.tensor.matmul(product_bank[:, t, :], turned[0][:, k, t * P:(t + 1) * P], product[0][:, k, :],
                                                start=k == 0, stop=k == KT - 1)
                last.then_inc(product_made, 1)

            for n in range(NT // 2):
                b = 2 * n // TB
                if 2 * n % TB == 0:
                    pe.wait_ge(scaled, B * (len(passes) - 1) + b + 1)
                if (2 * n + 1) % TB == SHARE // 2 * 2 + 1:
                    pe.wait_ge(pooled, summed + B * (len(passes) - 1) + b + 1)
                if n >= 4:
                    pe.wait_ge(bank_copied, n - 3)
                for k in range(KT):
                    for t in range(2):
                        last = nc.tensor.transpose(bank[n % 4][:, k, t * P:(t + 1) * P],
                                                   src[:, 2 * n + t, k * P:(k + 1) * P], ident[:])
                last.then_inc(bank_ready, 1)
                if product and n >= 2:
                    multiply(n - 2)
            if product:
                multiply(NT // 2 - 2)
                multiply(NT // 2 - 1)

        @block.scalar
        def _(act):
            if parts:
                parts[1](act)
            for p, (src, dst, *_r) in enumerate(passes):
                rstd, offset = works[p][2], works[p][4]
                for b in range(B):
                    act.wait_ge(asked, B * p + b + 1)
                    part = rstd[:, b * TB:(b + 1) * TB]
                    nc.scalar.activation(part, part, ACT.Sqrt).then_inc(rooted, 1)
                for b in range(B):
                    act.wait_ge(ready, B * p + b + 1)
                    tiles = tiles_of(b, True)
                    for n in range(tiles.start, tiles.stop):
                        nc.scalar.activation(dst[:, n, :], src[:, n, :], ACT.Identity, bias=offset[:, n:n + 1],
                                             scale=rstd[:, n:n + 1]).then_inc(applied, 1)
            if turned:
                for n in range(NT // 2):
                    act.wait_ge(bank_ready, n + 1)
                    nc.scalar.activation(turned[0][:, :, 2 * n * P:2 * (n + 1) * P], bank[n % 4][:],
                                         ACT.Copy).then_inc(bank_copied, 1)
            if product:
                act.wait_ge(product_made, NT // 2)
                nc.scalar.activation(product[1][:], product_bank[:], ACT.Copy)

        @block.gpsimd
        def _(pool):
            step = Chain(pool, pool_own)
            if loads:
                pool.wait_ge(loaded, 16 * len(loads))
            if x_sum:
                for b in range(B):
                    gated_sum(nc.gpsimd, step, b, True, *x_sum, x_sum[2])
                    pool.sem_inc(pooled, 1)
            for p, (_, dst, _, _, factor, addend) in enumerate(passes):
                for b in range(B):
                    pool.wait_ge(applied, own * (B * p + b + 1))
                    on_rows(nc.gpsimd, step, b, True, dst, dst, factor, ALU.mult)
                    if addend is not None:
                        on_rows(nc.gpsimd, step, b, True, dst, dst, addend, ALU.add)
                    pool.sem_inc(pooled, 1)
            if last_sum:
                for b in range(B):
                    gated_sum(nc.gpsimd, step, b, True, *last_sum)

        def scale_own(step, p, b):
            src, dst, _, rms, factor, addend = passes[p]
            _, mean, rstd, _, _ = works[p]
            tiles = tiles_of(b, False)
            if not rms:
                for n in range(tiles.start, tiles.stop):
                    last = nc.vector.scalar_tensor_tensor(dst[:, n, :], src[:, n, :], mean[:, n:n + 1], factor(b)[:, 0, :],
                                                          ALU.subtract, ALU.mult)
                step(last)
            for n in range(tiles.start, tiles.stop):
                last = nc.vector.scalar_tensor_tensor(dst[:, n, :], (src if rms else dst)[:, n, :], rstd[:, n:n + 1],
                                                      (factor if rms else addend)(b)[:, 0, :], ALU.mult,
                                                      ALU.mult if rms else ALU.add)
            last.then_inc(scaled, 1)

        @block.vector
        def _(v):
            step = Chain(v, dve)
            if parts:
                parts[3](v, step)
            for b in range(B):
                if x_sum:
                    gated_sum(nc.vector, step, b, False, *x_sum, x_sum[2])
                    v.wait_ge(pooled, b + 1)
                if x_loads:
                    v.wait_ge(x_loaded[b], 16)
                src, _, eps, rms, _, _ = passes[0]
                token_stats(nc, step, b, src, eps, rms, works[0], asked)
            if parts:
                parts[4](v, step)
            if loads:
                v.wait_ge(loaded, 16 * len(loads))
            for p, (_, _, _, rms, _, _) in enumerate(passes):
                for b in range(B):
                    _, mean, rstd, _, offset = (w[:, b * TB:(b + 1) * TB] for w in works[p])
                    v.wait_ge(rooted, B * p + b + 1)
                    if rms:
                        nc.vector.memset(offset, 0.0)
                        nc.vector.reciprocal(rstd, rstd).then_inc(ready, 1)
                    else:
                        step(nc.vector.reciprocal(rstd, rstd))
                        nc.vector.scalar_tensor_tensor(offset, mean, -1.0, rstd, ALU.mult, ALU.mult).then_inc(ready, 1)
                    v.wait_ge(ready, B * p + b + 1)
                for b in range(B):
                    scale_own(step, p, b)
                    v.wait_ge(scaled, B * p + b + 1)
                    if p + 1 < len(passes):
                        v.wait_ge(pooled, summed + B * p + b + 1)
                        src, _, eps, next_rms, _, _ = passes[p + 1]
                        token_stats(nc, step, b, src, eps, next_rms, works[p + 1], asked)
            if last_sum:
                for b in range(B):
                    gated_sum(nc.vector, step, b, False, *last_sum)
            v.wait_ge(pooled, summed + B * len(passes))


def row_load(row, source):
    return row[:], source.rearrange("(o n d) -> o n d", o=1, n=1).to_broadcast([P, 1, D])


def full_attention(nc, q_parts, k_parts, xt, w_v, w_v_dram, values, o_rows, identf, scale):
    steps = NC * TB
    per = CH // P
    units = GH * per * NC
    turn_at = 4
    uses = units + 1
    ahead = 2
    with ExitStack() as ctx:
        sc = Scope(nc, ctx, "a0")
        q_st = [sc.sb(f"q{i}", [ROWS + SHIFT, NC, GH, CH], BF16) for i in range(2)]
        k_st = [sc.sb(f"k{i}", [ROWS + SHIFT, GH, S], BF16) for i in range(2)]
        v_st = [sc.sb(f"v{i}", [P, TB, GH, VW]) for i in range(2)]
        room = xt[:].rearrange("p k t -> p (k t)")
        prob = [room[:, i * 2 * CH:(i + 1) * 2 * CH].rearrange("p (j t) -> p j t", t=CH) for i in range(4)]
        o_sb = [room[:, 8 * CH + i * S:8 * CH + (i + 1) * S] for i in range(2)]
        peak = sc.sb("peak", [P, units])
        top = sc.sb("top", [P, P])
        shift = [sc.sb(f"shift{i}", [GH * per, P], BF16) for i in range(3)]
        left = [sc.sb(f"left{i}", [GH * per, P]) for i in range(2)]
        score = [sc.ps(f"score{i}", [P, 2, CH]) for i in range(2)]
        o_ps = sc.ps("o_ps", [P, CH])
        wide = [sc.ps(f"wide{i}", [P, CH]) for i in range(3)]
        first_loaded = [sc.sem(f"first_loaded{i}") for i in range(2)]
        rest_loaded = [sc.sem(f"rest_loaded{i}") for i in range(2)]
        o_stored = [sc.sem(f"o_stored{i}") for i in range(2)]
        v_ready, v_blank, ones_set = (sc.sem(n) for n in ("v_ready", "v_blank", "ones_set"))
        scores_ready, exp_done, pv_done, o_copied = (sc.sem(n) for n in ("scores_ready", "exp_done", "pv_done", "o_copied"))
        wide_ready, wide_used, top_ready, shift_ready, shift_loaded = (
            sc.sem(n) for n in ("wide_ready", "wide_used", "top_ready", "shift_ready", "shift_loaded"))
        dve, w_v_loaded, v_made, v_copied = (sc.sem(n) for n in ("dve", "w_v_loaded", "v_made", "v_copied"))
        block = ctx.enter_context(nc.Block())

        def groups(eng, one):
            with eng.Fori(0, G // 2 - 1) as pair:
                one(pair, 0, True)
                one(pair, 1, True)
            one(G // 2 - 1, 0, True)
            one(G // 2 - 1, 1, False)

        def load_part(sp, i, group, j0, j1, loaded):
            first = group * GH * HD + j0 * HD
            for block_, n in enumerate(Q_PARTS):
                for j in range(j0, j1):
                    sp.dma_start(q_st[i][block_ * HD:(block_ + 1) * HD, :, j, :],
                                 q_parts[n, bass.ds(first + (j - j0) * HD, HD), :].rearrange("d (c t) -> d c t", t=CH)
                                 ).then_inc(loaded[i], 16)
            for block_, n in enumerate(K_PARTS):
                sp.dma_start(k_st[i][block_ * HD:(block_ + 1) * HD, j0:j1, :],
                             k_parts[n, bass.ds(first, (j1 - j0) * HD), :].rearrange("(j d) t -> d j t", d=HD)
                             ).then_inc(loaded[i], 16)

        def loads(heads):
            return 16 * NP_ * (heads + 1)

        def load_group(sp, i, group):
            load_part(sp, i, group, 0, 1, first_loaded)
            load_part(sp, i, group, 1, GH, rest_loaded)

        def load_shift(sp, m, i, c):
            sp.wait_ge(shift_ready, m + 2)
            for n in range(SHIFT):
                sp.dma_start(q_st[i][ROWS + n:ROWS + n + 1, bass.ds(c, 1), :, :].rearrange("o c j t -> o (c j t)")
                             .rearrange("o (a b) -> o a b", b=P), shift[n][:]).then_inc(shift_loaded, 16)

        @block.sync
        def _(sp):
            sp.dma_start(w_v[:], w_v_dram).then_inc(w_v_loaded, 16)
            load_group(sp, 0, 0)

            def store(i, g, c):
                sp.wait_ge(o_copied, NC * g + c + 2)
                sp.dma_start(o_rows[bass.ds(g, 1), :, bass.ds(c * CH, CH)]
                             .rearrange("g p n -> (g p) n"), o_sb[i][:, bass.ds(c * CH, CH)]).then_inc(o_stored[i], 16)

            def one(pair, i, more):
                g = 2 * pair + i
                m = NC * g
                if more:
                    sp.wait_ge(exp_done, 2 * steps * g + 2)
                    load_group(sp, 1 - i, g + 1)
                with sp.Fori(0, NC - 1) as c:
                    load_shift(sp, m + c + 1, i, c + 1)
                    store(i, g, c)
                if more:
                    load_shift(sp, m + NC, 1 - i, 0)
                store(i, g, NC - 1)

            load_shift(sp, 0, 0, 0)
            groups(sp, one)
            for i in range(2):
                sp.wait_ge(o_stored[i], 16 * NC * (G // 2 + 1))

        @block.gpsimd
        def _(pool):
            for i in range(2):
                nc.gpsimd.memset(k_st[i][ROWS:ROWS + SHIFT, :, :], 1.0).then_inc(ones_set, 1)
                pool.wait_ge(ones_set, i + 1)
                nc.gpsimd.memset(v_st[i][:], 0.0).then_inc(v_blank, 1)
                pool.wait_ge(v_blank, 2 * i + 1)
                nc.gpsimd.memset(v_st[i][:, :, :, HD:HD + 1], 1.0).then_inc(v_blank, 1)
                pool.wait_ge(v_blank, 2 * i + 2)

            def one(pair, i):
                g = 2 * pair + i
                if not isinstance(pair, int):
                    pool.wait_ge(pv_done, steps * (g - 1) + 2)
                nc.gpsimd.tensor_copy(v_st[i][:, :, :, 0:HD],
                                      values[:, bass.ds(g, 1), :, :].rearrange("p g i (j d) -> p (g i) j d", d=HD)).then_inc(v_ready, 1)

            pool.wait_ge(v_copied, TB)
            one(0, 0)
            one(0, 1)
            pool.wait_ge(v_copied, NT)
            with pool.Fori(1, G // 2) as pair:
                one(pair, 0)
                one(pair, 1)

        def scores(pe, i, c, kt, half):
            for j in range(2):
                head = 2 * half + j
                last = nc.tensor.matmul(score[half][:, j, :], k_st[i][:, head, kt * P:(kt + 1) * P],
                                        q_st[i][:, bass.ds(c, 1), head, :].rearrange("p c t -> p (c t)"), start=True, stop=True)
            last.then_inc(scores_ready, 1)

        def await_wide_bank(pe, r, x):
            pe.wait_ge(wide_used, uses * r + (x + 1 if x >= 3 else (2, 3, 1)[x]))

        def wide_use(pe, r, i, c, x):
            if x == turn_at:
                turn_top(pe, r, x)
                return
            u = x - (x > turn_at)
            head, qt, n = u // (per * NC), u // NC % per, u % NC
            await_wide_bank(pe, r, x)
            q_flat = q_st[i][0:ROWS, :, :, :].rearrange("p c j t -> p (c j t)")
            nc.tensor.matmul(wide[x % 3][:], q_flat[:, bass.ds(c * (GH * CH) + (head * CH + qt * P), P)],
                             k_st[i][0:ROWS, head, n * CH:(n + 1) * CH], start=True, stop=True).then_inc(wide_ready, 1)

        def value_bank(n):
            return score[n % 4 // 2][:, n % 2, 0:D]

        def turn_top(pe, r, x):
            pe.wait_ge(top_ready, r + 1)
            await_wide_bank(pe, r, x)
            nc.tensor.transpose(wide[x % 3][:, 0:P], top[:], identf[:]).then_inc(wide_ready, 1)

        @block.tensor
        def _(pe):
            nc.tensor.sem_inc(exp_done, 2)
            nc.tensor.sem_inc(pv_done, 2)
            nc.tensor.sem_inc(o_copied, 1)
            nc.tensor.sem_inc(wide_used, 3)
            def make_values(n):
                if n >= 4:
                    pe.wait_ge(v_copied, n - 3)
                for k in range(KT):
                    last = nc.tensor.matmul(value_bank(n), xt[:, k, n * P:(n + 1) * P], w_v[:, k, :],
                                            start=k == 0, stop=k == KT - 1)
                last.then_inc(v_made, 1)

            pe.wait_ge(w_v_loaded, 16)
            made = 2
            for n in range(made):
                make_values(n)
            pe.wait_ge(first_loaded[0], loads(1))
            for r in range(ahead):
                for x in range(uses):
                    if r == 0 and x == units // GH + 1:
                        pe.wait_ge(rest_loaded[0], loads(GH - 1))
                    wide_use(pe, r, 0, r, x)
                    if x % 4 == 3 and made < NT:
                        make_values(made)
                        made += 1
            pe.wait_ge(v_copied, NT)
            pe.wait_ge(ones_set, 2)
            pe.wait_ge(shift_loaded, 16 * SHIFT)
            for half in range(2):
                scores(pe, 0, 0, 0, half)

            def chunk(pair, i, c, source, following):
                g = 2 * pair + i
                m = NC * g + c
                x = 0
                for kt in range(TB):
                    s = steps * g + TB * c + kt
                    if kt + 1 == TB and following:
                        pe.wait_ge(shift_loaded, 16 * SHIFT * (m + 2))
                    for half, wide_units in enumerate((1, 1, 2)):
                        for _ in range(wide_units + (kt == 1 and half == 0) if source else 0):
                            wide_use(pe, m + ahead, source[0], source[1], x)
                            x += 1
                        if half < 2 and (kt + 1 < TB or following):
                            pe.wait_ge(exp_done, 2 * (s + 1) + half + 1)
                            if kt + 1 < TB:
                                scores(pe, i, c, kt + 1, half)
                            else:
                                scores(pe, following[0], following[1], 0, half)
                    if isinstance(m, int) and m + ahead == NC * G and kt == 0:
                        turn_top(pe, m + ahead, 0)
                    if kt == 0:
                        pe.wait_ge(v_ready, g + 1)
                        pe.wait_ge(o_copied, m + 1)
                    pe.wait_ge(exp_done, 2 * s + 4)
                    for head in range(GH):
                        last = nc.tensor.matmul(o_ps[head * VW:(head + 1) * VW, :], v_st[i][:, kt, head, :],
                                                prob[2 * (kt % 2) + head // 2][:, head % 2, :],
                                                start=kt == 0, stop=kt == TB - 1)
                    last.then_inc(pv_done, 1)

            def one(pair, i, more):
                with pe.Fori(0, NC - ahead) as c:
                    chunk(pair, i, c, (i, c + ahead), (i, c + 1))
                if more:
                    pe.wait_ge(first_loaded[1 - i], loads(1) * (pair + i + 1))
                    pe.wait_ge(rest_loaded[1 - i], loads(GH - 1) * (pair + i + 1))
                chunk(pair, i, NC - 2, (1 - i, 0) if more else None, (i, NC - 1))
                chunk(pair, i, NC - 1, (1 - i, 1) if more else None, (1 - i, 0) if more else None)

            groups(pe, one)

        @block.scalar
        def _(act):
            for n in range(NT):
                act.wait_ge(v_made, n + 1)
                first = n // TB * (G // B)
                nc.scalar.activation(values[:, first:first + G // B, n % TB, :],
                                     value_bank(n).rearrange("p (g v) -> p g v", v=GH * HD), ACT.Copy).then_inc(v_copied, 1)
            with act.Fori(0, G) as g:
                with act.Fori(0, NC) as c:
                    for kt in range(TB):
                        s = steps * g + TB * c + kt
                        act.wait_ge(pv_done, s + 1)
                        for half in range(2):
                            act.wait_ge(scores_ready, 2 * s + half + 1)
                            nc.scalar.activation(prob[2 * (kt % 2) + half][:], score[half][:], ACT.Exp,
                                                 scale=scale).then_inc(exp_done, 1)

        @block.vector
        def _(v):
            nc.vector.sem_inc(o_stored[0], 16 * NC)
            nc.vector.sem_inc(o_stored[1], 16 * NC)
            nc.vector.memset(top[:], 0.0).then_inc(top_ready, 1)

            def shifts(r, x):
                v.wait_ge(wide_ready, uses * r + x + 1)
                turned = wide[x % 3][0:GH * per, 0:P]
                nc.vector.tensor_copy(shift[0][:], turned).then_inc(dve, 1)
                v.wait_ge(dve, 3 * r + 1)
                nc.vector.tensor_tensor(left[0][:], turned, shift[0][:], ALU.subtract).then_inc(wide_used, 1)
                v.wait_ge(wide_used, uses * r + x + 4)
                nc.vector.tensor_copy(shift[1][:], left[0][:]).then_inc(dve, 1)
                v.wait_ge(dve, 3 * r + 2)
                nc.vector.tensor_tensor(left[1][:], left[0][:], shift[1][:], ALU.subtract).then_inc(dve, 1)
                v.wait_ge(dve, 3 * r + 3)
                nc.vector.tensor_copy(shift[2][:], left[1][:]).then_inc(shift_ready, 1)
                v.wait_ge(shift_ready, r + 1)

            def maxima(r, shift_read):
                for x in range(uses):
                    if x == turn_at:
                        if shift_read is not None:
                            v.wait_ge(shift_loaded, 16 * SHIFT * shift_read)
                        shifts(r, x)
                    else:
                        u = x - (x > turn_at)
                        v.wait_ge(wide_ready, uses * r + x + 1)
                        nc.vector.tensor_reduce(peak[:, u:u + 1], wide[x % 3][:], AX.X, ALU.max).then_inc(wide_used, 1)
                v.wait_ge(wide_used, uses * (r + 1) + 3)
                nc.vector.tensor_reduce(top[:, 0:GH * per], peak[:].rearrange("p (a n) -> p a n", n=NC), AX.X,
                                        ALU.max, negate=True).then_inc(top_ready, 1)
                v.wait_ge(top_ready, r + 2)

            def copy_out(pair, i, c):
                g = 2 * pair + i
                v.wait_ge(o_stored[i], 16 * NC * (pair + 1))
                v.wait_ge(pv_done, steps * g + TB * (c + 1) + 2)
                nc.vector.tensor_copy(o_sb[i][:, bass.ds(c * CH, CH)], o_ps[:]).then_inc(o_copied, 1)

            for r in range(ahead):
                maxima(r, None)

            def one(pair, i, more):
                m = NC * (2 * pair + i)
                with v.Fori(0, NC if more else NC - ahead) as c:
                    maxima(m + c + ahead, m + c + 1)
                    copy_out(pair, i, c)
                if not more:
                    v.wait_ge(shift_loaded, 16 * SHIFT * (NC * G - 1))
                    shifts(NC * G, 0)
                    copy_out(pair, i, NC - 2)
                    copy_out(pair, i, NC - 1)

            groups(v, one)


def causal_plan():
    plan = []
    for c in range(NC):
        per = CH // P
        for kt in range(per * (c + 1)):
            skip = max(0, kt - per * c) * P
            plan.append((c, c * CH + skip, CH - skip, kt, 0 if kt >= per * c else None))
    return plan


def window_plan():
    plan = []
    for qt in range(TB):
        plan.append((qt, qt * P, P, qt, 0))
        if qt:
            plan.append((qt, qt * P, WIN, qt - 1, P))
    return plan


def masked_attention(nc, tag, q_parts, k_parts, values, o_rows, mask, identb, plan, span, scale):
    steps = len(plan)
    spans = S // span
    width = min(span, CH)
    per_job = 4 if span == P else 2
    halves = GH // per_job
    bufs = 6 // (per_job * width // CH)
    slots = 4 // halves
    ahead = slots - 1
    with ExitStack() as ctx:
        sc = Scope(nc, ctx, tag)
        q_st = [sc.sb(f"q{i}", [ROWS, GH, S], BF16) for i in range(2)]
        k_st = [sc.sb(f"k{i}", [ROWS, S], BF16) for i in range(2)]
        v_st = [sc.sb(f"v{i}", [P, TB, VW]) for i in range(2)]
        prob = [sc.sb(f"prob{i}", [P, per_job, width]) for i in range(slots * halves)]
        o_sb = [sc.sb(f"o{i}", [P, S]) for i in range(2)]
        score = [sc.ps(f"score{i}", [P, per_job, width]) for i in range(bufs)]
        o_ps = [sc.ps(f"o_ps{i}", [P, CH]) for i in range(2)]
        loaded = [sc.sem(f"loaded{i}") for i in range(2)]
        o_stored = [sc.sem(f"o_stored{i}") for i in range(2)]
        v_ready, v_blank = sc.sem("v_ready"), sc.sem("v_blank")
        scores_ready, exp_done, pv_done, o_copied = (sc.sem(n) for n in ("scores_ready", "exp_done", "pv_done", "o_copied"))
        block = ctx.enter_context(nc.Block())
        first_of = {}
        last_of = {}
        for n, (c, *_r) in enumerate(plan):
            first_of.setdefault(c, n)
            last_of[c] = n
        jobs = halves * steps

        def buffer_before(e):
            if e >= bufs:
                return e - bufs
            return max(x for x in range(jobs) if x % bufs == e) - jobs

        @block.sync
        def _(sp):
            def load_group(pair, i):
                g = 2 * pair + i
                for block_, n in enumerate(Q_PARTS):
                    sp.dma_start(q_st[i][block_ * HD:(block_ + 1) * HD, :, :],
                                 q_parts[n, bass.ds(g * GH * HD, GH * HD), :].rearrange("(j d) t -> d j t", d=HD)
                                 ).then_inc(loaded[i], 16)
                for block_, n in enumerate(K_PARTS):
                    sp.dma_start(k_st[i][block_ * HD:(block_ + 1) * HD, :],
                                 k_parts[n, bass.ds(g * HD, HD), :]).then_inc(loaded[i], 16)

            def store(pair, i):
                g = 2 * pair + i
                for c in range(spans):
                    sp.wait_ge(o_copied, spans * g + c + 3)
                    sp.dma_start(o_rows[bass.ds(g, 1), :, c * span:(c + 1) * span].rearrange("g p n -> (g p) n"),
                                 o_sb[i][:, c * span:(c + 1) * span]).then_inc(o_stored[i], 16)

            load_group(0, 0)
            load_group(0, 1)
            with sp.Fori(0, G // 2 - 1) as pair:
                for i in range(2):
                    store(pair, i)
                    load_group(pair + 1, i)
            for i in range(2):
                store(G // 2 - 1, i)
            for i in range(2):
                sp.wait_ge(o_stored[i], 16 * spans * (G // 2 + 1))

        @block.gpsimd
        def _(pool):
            for i in range(2):
                nc.gpsimd.memset(v_st[i][:], 0.0).then_inc(v_blank, 1)
                pool.wait_ge(v_blank, 2 * i + 1)
                nc.gpsimd.memset(v_st[i][:, :, HD:HD + 1], 1.0).then_inc(v_blank, 1)
            pool.wait_ge(v_blank, 4)

            def one(pair, i):
                g = 2 * pair + i
                if not isinstance(pair, int):
                    pool.wait_ge(pv_done, steps * (g - 1) + slots)
                nc.gpsimd.tensor_copy(v_st[i][:, :, 0:HD],
                                      values[:, bass.ds(g, 1), :, :].rearrange("p g i n -> p (g i) n")).then_inc(v_ready, 1)

            one(0, 0)
            one(0, 1)
            with pool.Fori(1, G // 2) as pair:
                one(pair, 0)
                one(pair, 1)

        @block.tensor
        def _(pe):
            nc.tensor.sem_inc(exp_done, jobs)
            nc.tensor.sem_inc(pv_done, slots)
            nc.tensor.sem_inc(o_copied, 2)

            def scores(i, g, n):
                _, q0, w, kt, masked = plan[n]
                for half in range(halves):
                    e = halves * n + half
                    pe.wait_ge(exp_done, jobs * (g + 1) + buffer_before(e) + 1)
                    out = score[e % bufs]
                    for j in range(per_job):
                        last = nc.tensor.matmul(out[:, j, 0:w], k_st[i][:, kt * P:(kt + 1) * P],
                                                q_st[i][:, per_job * half + j, q0:q0 + w], start=True, stop=True)
                        if masked is not None:
                            m = min(w, P)
                            last = nc.tensor.matmul(out[:, j, 0:m], identb[:], mask[:, masked:masked + m],
                                                    start=False, stop=True, skip_group_check=True)
                    last.then_inc(scores_ready, 1)

            with pe.Fori(0, G // 2) as pair:
                for i in range(2):
                    g = 2 * pair + i
                    pe.wait_ge(loaded[i], 16 * 2 * NP_ * (pair + 1))
                    for n in range(ahead):
                        scores(i, g, n)
                    pe.wait_ge(v_ready, g + 1)
                    for n, (c, q0, w, kt, masked) in enumerate(plan):
                        if n + ahead < steps:
                            scores(i, g, n + ahead)
                        if n == first_of[c]:
                            pe.wait_ge(o_copied, spans * g + c + 1)
                        pe.wait_ge(exp_done, jobs * (g + 1) + halves * (n + 1))
                        at = q0 - c * span
                        for head in range(GH):
                            last = nc.tensor.matmul(o_ps[c % 2][head * VW:(head + 1) * VW, at:at + w], v_st[i][:, kt, :],
                                                    prob[halves * (n % slots) + head // per_job][:, head % per_job, 0:w],
                                                    start=n == first_of[c], stop=n == last_of[c], skip_group_check=True)
                        last.then_inc(pv_done, 1)

        @block.scalar
        def _(act):
            nc.scalar.sem_inc(o_stored[0], 16 * spans)
            nc.scalar.sem_inc(o_stored[1], 16 * spans)
            with act.Fori(0, G // 2) as pair:
                for i in range(2):
                    g = 2 * pair + i
                    for n, (c, q0, w, kt, masked) in enumerate(plan):
                        act.wait_ge(pv_done, steps * g + n + 1)
                        for half in range(halves):
                            e = halves * n + half
                            act.wait_ge(scores_ready, jobs * g + e + 1)
                            nc.scalar.activation(prob[halves * (n % slots) + half][:, :, 0:w], score[e % bufs][:, :, 0:w], ACT.Exp,
                                                 scale=scale).then_inc(exp_done, 1)

        @block.vector
        def _(v):
            with v.Fori(0, G // 2) as pair:
                for i in range(2):
                    g = 2 * pair + i
                    v.wait_ge(o_stored[i], 16 * spans * (pair + 1))
                    for c in range(spans):
                        v.wait_ge(pv_done, steps * g + last_of[c] + 1 + slots)
                        nc.vector.tensor_copy(o_sb[i][:, c * span:(c + 1) * span], o_ps[c % 2][:, 0:span]).then_inc(o_copied, 1)


def gather_heads(nc, tag, o_rows, att, ident):
    hg = H // GH
    with ExitStack() as ctx:
        sc = Scope(nc, ctx, tag)
        rows = [sc.sb(f"rows{b}", [P, hg, S]) for b in range(B)]
        inverse = [sc.sb(f"inverse{i}", [P, H, 1]) for i in range(2)]
        bank = [sc.ps(f"bank{i}", [P, H, VW]) for i in range(4)]
        loaded = [sc.sem(f"loaded{c}") for c in range(B * NC)]
        turned, inverted, scaled = (sc.sem(n) for n in ("turned", "inverted", "scaled"))
        block = ctx.enter_context(nc.Block())

        @block.sync
        def _(sp):
            for b in range(B):
                for c in range(NC):
                    sp.dma_start(rows[b][:, :, c * CH:(c + 1) * CH],
                                 o_rows[b * hg:(b + 1) * hg, :, c * CH:(c + 1) * CH].rearrange("g p t -> p g t")
                                 ).then_inc(loaded[b * NC + c], 16)

        @block.tensor
        def _(pe):
            for n in range(NT):
                b, i = n // TB, n % TB
                if n % (CH // P) == 0:
                    pe.wait_ge(loaded[n * P // CH], 16)
                if n >= 4:
                    pe.wait_ge(scaled, n - 3)
                for g in range(hg):
                    last = nc.tensor.transpose(bank[n % 4][:, g * GH:(g + 1) * GH, :].rearrange("p h n -> p (h n)"),
                                               rows[b][:, g, i * P:(i + 1) * P], ident[:])
                last.then_inc(turned, 1)

        @block.vector
        def _(v):
            for n in range(NT + 1):
                if n < NT:
                    v.wait_ge(turned, n + 1)
                    if n >= 2:
                        v.wait_ge(scaled, n - 1)
                    nc.vector.reciprocal(inverse[n % 2][:], bank[n % 4][:, :, HD:HD + 1]).then_inc(inverted, 1)
                if n >= 1:
                    v.wait_ge(inverted, n)
                    nc.vector.tensor_tensor(att[:, n - 1, :].rearrange("p (h n) -> p h n", n=HD),
                                            bank[(n - 1) % 4][:, :, 0:HD],
                                            inverse[(n - 1) % 2][:].to_broadcast([P, H, HD]), ALU.mult).then_inc(scaled, 1)


def project_heads(nc, tag, o_rows, w_dram, x, ident):
    hg = H // GH
    with ExitStack() as ctx:
        sc = Scope(nc, ctx, tag)
        rows = [sc.sb(f"rows{b}", [P, hg, S]) for b in range(B)]
        w_sb = sc.sb("w", [P, KT, D])
        inverse = [sc.sb(f"inverse{i}", [P, H, 1]) for i in range(2)]
        att = [sc.sb(f"att{i}", [P, D]) for i in range(2)]
        att_t = [sc.sb(f"att_t{i}", [P, KT, P]) for i in range(2)]
        bank = [sc.ps(f"bank{i}", [P, H, VW]) for i in range(3)]
        att_bank = [sc.ps(f"att_bank{i}", [P, KT, P]) for i in range(2)]
        out_bank = [sc.ps(f"out_bank{i}", [P, D]) for i in range(2)]
        loaded = [sc.sem(f"loaded{c}") for c in range(B * NC)]
        w_loaded, turned, inverted, scaled, att_turned, att_copied, made, added = (
            sc.sem(n) for n in ("w_loaded", "turned", "inverted", "scaled", "att_turned", "att_copied", "made", "added"))
        block = ctx.enter_context(nc.Block())

        @block.sync
        def _(sp):
            sp.dma_start(w_sb[:], w_dram.rearrange("(k p) n -> p k n", p=P)).then_inc(w_loaded, 16)
            for b in range(B):
                for c in range(NC):
                    sp.dma_start(rows[b][:, :, c * CH:(c + 1) * CH],
                                 o_rows[b * hg:(b + 1) * hg, :, c * CH:(c + 1) * CH].rearrange("g p t -> p g t")
                                 ).then_inc(loaded[b * NC + c], 16)

        @block.tensor
        def _(pe):
            def turn(n):
                if n % (CH // P) == 0:
                    pe.wait_ge(loaded[n * P // CH], 16)
                if n >= 3:
                    pe.wait_ge(scaled, n - 2)
                b, i = n // TB, n % TB
                for g in range(hg):
                    last = nc.tensor.transpose(bank[n % 3][:, g * GH:(g + 1) * GH, :].rearrange("p h n -> p (h n)"),
                                               rows[b][:, g, i * P:(i + 1) * P], ident[:])
                last.then_inc(turned, 1)

            def turn_att(n):
                pe.wait_ge(scaled, n + 1)
                if n >= 2:
                    pe.wait_ge(att_copied, n - 1)
                for k in range(KT):
                    last = nc.tensor.transpose(att_bank[n % 2][:, k, :], att[n % 2][:, k * P:(k + 1) * P], ident[:])
                last.then_inc(att_turned, 1)

            def product(n):
                pe.wait_ge(att_copied, n + 1)
                if n >= 2:
                    pe.wait_ge(added, n - 1)
                for k in range(KT):
                    last = nc.tensor.matmul(out_bank[n % 2][:], att_t[n % 2][:, k, :], w_sb[:, k, :],
                                            start=k == 0, stop=k == KT - 1)
                last.then_inc(made, 1)

            pe.wait_ge(w_loaded, 16)
            for n in range(NT + 2):
                if n < NT:
                    turn(n)
                if 1 <= n <= NT:
                    turn_att(n - 1)
                if n >= 2:
                    product(n - 2)

        @block.scalar
        def _(act):
            for n in range(NT):
                act.wait_ge(att_turned, n + 1)
                if n >= 2:
                    act.wait_ge(made, n - 1)
                nc.scalar.activation(att_t[n % 2][:], att_bank[n % 2][:], ACT.Copy).then_inc(att_copied, 1)

        @block.vector
        def _(v):
            def divide(n):
                v.wait_ge(turned, n + 1)
                nc.vector.reciprocal(inverse[n % 2][:], bank[n % 3][:, :, HD:HD + 1]).then_inc(inverted, 1)
                v.wait_ge(inverted, n + 1)
                if n >= 2:
                    v.wait_ge(att_turned, n - 1)
                nc.vector.tensor_tensor(att[n % 2][:].rearrange("p (h n) -> p h n", n=HD), bank[n % 3][:, :, 0:HD],
                                        inverse[n % 2][:].to_broadcast([P, H, HD]), ALU.mult).then_inc(scaled, 1)
                v.wait_ge(scaled, n + 1)

            for n in range(NT + 2):
                if n < NT:
                    divide(n)
                if n >= 2:
                    v.wait_ge(made, n - 1)
                    nc.vector.tensor_tensor(x[:, n - 2, :], out_bank[n % 2][:], x[:, n - 2, :], ALU.add).then_inc(added, 1)


def project_split(nc, tag, xt, scratches, w_dram):
    with ExitStack() as ctx:
        sc = Scope(nc, ctx, tag)
        w_sb = [sc.sb(f"w{n}", [P, KT, D]) for n in range(len(w_dram))]
        bank = [sc.ps(f"bank{i}", [P, CH]) for i in range(8)]
        part = [sc.sb(f"part{i}", [P, 3, S], BF16) for i in range(2)]
        rest = [sc.sb(f"rest{i}", [P, CH]) for i in range(2)]
        made, high, rest_ready, mid, low, loaded = (
            sc.sem(n) for n in ("made", "high", "rest_ready", "mid", "low", "loaded"))
        stored = [sc.sem(f"stored{i}") for i in range(2)]
        block = ctx.enter_context(nc.Block())
        jobs = [(which, b, half) for b in range(B) for half in range(D // P) for which in range(len(w_dram))]
        chunks = [(n, c) for n in range(len(jobs)) for c in range(NC)]

        @block.sync
        def _(sp):
            for w, source in zip(w_sb, w_dram):
                sp.dma_start(w[:], source.rearrange("(k p) n -> p k n", p=P)).then_inc(loaded, 16)
            for n, (which, b, half) in enumerate(jobs):
                first = b * D + half * P
                for c in range(1, NC, 2):
                    for sem in (high, mid, low):
                        sp.wait_ge(sem, NC * n + c + 1)
                    cols = slice((c - 1) * CH, (c + 1) * CH)
                    sp.dma_start(scratches[which][:, first:first + P, cols].rearrange("w r t -> r w t"),
                                 part[n % 2][:, :, cols]).then_inc(stored[n % 2], 16)
            for i in range(2):
                sp.wait_ge(stored[i], 16 * (NC // 2) * len(jobs) // 2)

        @block.tensor
        def _(pe):
            pe.wait_ge(loaded, 16 * len(w_dram))
            for m, (n, c) in enumerate(chunks):
                which, b, half = jobs[n]
                at_least(pe, rest_ready, m - 7)
                for k in range(KT):
                    last = nc.tensor.matmul(bank[m % 8][:], w_sb[which][:, k, half * P:(half + 1) * P],
                                            xt[:, k, b * S + c * CH:b * S + (c + 1) * CH], start=k == 0, stop=k == KT - 1)
                last.then_inc(made, 1)

        def of(m):
            n, c = chunks[m]
            return (bank[m % 8][:], *(part[n % 2][:, w, c * CH:(c + 1) * CH] for w in range(3)), rest[m % 2][:])

        @block.scalar
        def _(act):
            def middle(m):
                _, _, mid_part, _, remainder = of(m)
                act.wait_ge(rest_ready, m + 1)
                nc.scalar.activation(mid_part, remainder, ACT.Copy).then_inc(mid, 1)

            for m, (n, c) in enumerate(chunks):
                source, high_part, _, _, _ = of(m)
                act.wait_ge(made, m + 1)
                if n >= 2 and c == 0:
                    act.wait_ge(stored[n % 2], 16 * (NC // 2) * (n // 2))
                nc.scalar.activation(high_part, source, ACT.Copy).then_inc(high, 1)
                if m:
                    middle(m - 1)
            middle(len(chunks) - 1)

        @block.vector
        def _(v):
            def lowest(m):
                _, _, mid_part, low_part, remainder = of(m)
                v.wait_ge(mid, m + 1)
                nc.vector.tensor_tensor(low_part, remainder, mid_part, ALU.subtract).then_inc(low, 1)

            for m in range(len(chunks)):
                source, high_part, _, _, remainder = of(m)
                v.wait_ge(high, m + 1)
                at_least(v, low, m - 1)
                nc.vector.tensor_tensor(remainder, source, high_part, ALU.subtract).then_inc(rest_ready, 1)
                if m:
                    lowest(m - 1)
            lowest(len(chunks) - 1)


QK = (H + KVH) * HD


NQK = H + KVH
ROPE_HEADS = 14
KW = KVH * HD


def layer1_heads(nc, tag, xt, w_dram, latent_dram, scratch, qkv, values, tables, q_parts, k_parts, ident):
    quarter = NT // 4
    with ExitStack() as ctx:
        sc = Scope(nc, ctx, tag)
        w_x = sc.sb("w_x", [P, KT, sum(w.shape[1] for w in w_dram)])
        from_x = w_x.shape[2]
        w_down = sc.sb("w_down", [P, KT, KW]) if latent_dram else None
        w_up = sc.sb("w_up", [KW, 2 * KW]) if latent_dram else None
        latent = scratch[0:KW, 0:S // D, :].rearrange("p i d -> p (i d)")
        room = scratch[:].rearrange("p i d -> p (i d)")[:, S:S + 4 * quarter * NQK * HD // 2]
        halves = room.rearrange("p (a i h n) -> p a i h n", a=4, i=quarter, h=NQK)
        square = sc.sb("square", [P, quarter, NQK, HD])
        total = sc.sb("total", [P, NT, NQK])
        cos, sin = sc.sb("cos", [P, TB, HD // 2]), sc.sb("sin", [P, TB, HD // 2])
        parts_room = xt[:].rearrange("p k t -> p (k t)")
        part = [parts_room[:, 3 * i * S // 2:3 * (i + 1) * S // 2].bitcast(BF16).rearrange("p (w t) -> p w t", t=S)
                for i in range(2)]
        rest = [parts_room[:, 3 * S + i * CH:3 * S + (i + 1) * CH] for i in range(2)]
        bank = [sc.ps(f"bank{i}", [P, CH]) for i in range(4)]
        turned_bank = [sc.ps(f"turned_bank{i}", [P, CH]) for i in range(4)]
        w_loaded, tables_loaded, made, copied, squared, rooted, dve, pool_own = (
            sc.sem(n) for n in ("w_loaded", "tables_loaded", "made", "copied", "squared", "rooted", "dve", "pool_own"))
        rotated_dve, rotated_pool, asked, inverted, divided_dve, divided_pool = (
            sc.sem(n) for n in ("rotated_dve", "rotated_pool", "asked", "inverted", "divided_dve", "divided_pool"))
        turned, high, rest_ready, mid, low = (sc.sem(n) for n in ("turned", "high", "rest_ready", "mid", "low"))
        stored = [sc.sem(f"stored{i}") for i in range(2)]
        block = ctx.enter_context(nc.Block())

        fills = []
        for b in range(B):
            if latent_dram:
                fills += [("latent", b, c) for c in range(NC)]
            fills += [("tile", b, i) for i in range(TB)]

        def fills_to(kind, b, i):
            return fills.index((kind, b, i)) + 1

        jobs = []
        for b in range(B):
            for half in range(D // P):
                jobs.append((b, half * P, P, q_parts, b * D + half * P))
            jobs.append((b, D, KW, k_parts, b * KW))
        chunks = [(n, c) for n in range(len(jobs)) for c in range(NC)]

        @block.sync
        def _(sp):
            at = 0
            for w in w_dram:
                sp.dma_start(w_x[:, :, at:at + w.shape[1]], w.rearrange("(k p) n -> p k n", p=P)).then_inc(w_loaded, 16)
                at += w.shape[1]
            if latent_dram:
                sp.dma_start(w_down[:], latent_dram[0].rearrange("(k p) n -> p k n", p=P)).then_inc(w_loaded, 16)
                for n, w in enumerate(latent_dram[1]):
                    sp.dma_start(w_up[:, n * KW:(n + 1) * KW], w).then_inc(w_loaded, 16)
            for t, source in zip((cos, sin), (tables[0], tables[1])):
                sp.dma_start(t[:], source).then_inc(tables_loaded, 16)
            for n, (_, _, rows, dst, first) in enumerate(jobs):
                for c in range(1, NC, 2):
                    for sem in (high, mid, low):
                        sp.wait_ge(sem, NC * n + c + 1)
                    cols = slice((c - 1) * CH, (c + 1) * CH)
                    sp.dma_start(dst[:, first:first + rows, cols].rearrange("w r t -> r w t"),
                                 part[n % 2][0:rows, :, cols]).then_inc(stored[n % 2], 16)
            for i in range(2):
                sp.wait_ge(stored[i], 16 * (NC // 2) * len(jobs) // 2)

        @block.tensor
        def _(pe):
            pe.wait_ge(w_loaded, 16 * (len(w_dram) + (3 if latent_dram else 0)))
            for n, (kind, b, i) in enumerate(fills):
                at_least(pe, copied, n - 3)
                if kind == "latent":
                    for k in range(KT):
                        last = nc.tensor.matmul(bank[n % 4][0:KW, :], w_down[:, k, :],
                                                xt[:, k, b * S + i * CH:b * S + (i + 1) * CH], start=k == 0, stop=k == KT - 1)
                else:
                    t = b * TB + i
                    for k in range(KT):
                        last = nc.tensor.matmul(bank[n % 4][:, 0:from_x], xt[:, k, t * P:(t + 1) * P], w_x[:, k, :],
                                                start=k == 0, stop=k == KT - 1)
                    if latent_dram:
                        pe.wait_ge(copied, fills_to("latent", b, i * P // CH))
                        last = nc.tensor.matmul(bank[n % 4][:, from_x:from_x + 2 * KW], latent[:, i * P:(i + 1) * P],
                                                w_up[:], start=True, stop=True)
                last.then_inc(made, 1)
            for m, (n, c) in enumerate(chunks):
                b, col, rows, _, _ = jobs[n]
                if c == 0:
                    pe.wait_ge(divided_dve, 2 * (b + 1))
                    pe.wait_ge(divided_pool, 2 * (b + 1))
                at_least(pe, rest_ready, m - 3)
                for t in range(CH // P):
                    last = nc.tensor.transpose(turned_bank[m % 4][0:rows, t * P:(t + 1) * P],
                                               qkv[:, b * TB + c * (CH // P) + t, col:col + rows], ident[:])
                last.then_inc(turned, 1)

        def tiles(q):
            return slice(q * quarter, (q + 1) * quarter)

        def qk(q, heads):
            return qkv[:, tiles(q), 0:QK].rearrange("p i (h n) -> p i h n", n=HD)[:, :, heads, :]

        def rotate(eng, step, q, heads, rotated):
            x = qk(q, heads)
            n = heads.stop - heads.start
            half = [halves[:, i, :, heads, :] for i in range(4)]
            even, odd = x[:, :, :, 0::2], x[:, :, :, 1::2]
            first = q * quarter % TB
            c, s = (t[:, first:first + quarter, :].rearrange("p i (h n) -> p i h n", h=1).to_broadcast([P, quarter, n, HD // 2])
                    for t in (cos, sin))
            eng.tensor_tensor(half[0], even, c, ALU.mult)
            eng.tensor_tensor(half[1], odd, s, ALU.mult)
            eng.tensor_tensor(half[2], even, s, ALU.mult)
            step(eng.tensor_tensor(half[3], odd, c, ALU.mult))
            step(eng.tensor_tensor(even, half[0], half[1], ALU.subtract))
            eng.tensor_tensor(odd, half[2], half[3], ALU.add).then_inc(rotated, 1)

        def divide(eng, q, heads):
            x = qk(q, heads)
            inverse = total[:, tiles(q), heads].rearrange("p i (h n) -> p i h n", n=1)
            return eng.tensor_tensor(x, x, inverse.to_broadcast([P, quarter, heads.stop - heads.start, HD]), ALU.mult)

        first_heads, other_heads = slice(0, ROPE_HEADS), slice(ROPE_HEADS, NQK)

        def await_quarter(eng, q):
            t = (q + 1) * quarter - 1
            eng.wait_ge(copied, fills_to("tile", t // TB, t % TB))

        @block.gpsimd
        def _(pool):
            step = Chain(pool, pool_own)
            pool.wait_ge(tables_loaded, 32)
            for q in range(4):
                await_quarter(pool, q)
                at_least(pool, rotated_pool, q)
                rotate(nc.gpsimd, step, q, other_heads, rotated_pool)
                if q:
                    pool.wait_ge(inverted, q)
                    divide(nc.gpsimd, q - 1, other_heads).then_inc(divided_pool, 1)
            pool.wait_ge(inverted, 4)
            divide(nc.gpsimd, 3, other_heads).then_inc(divided_pool, 1)
            pool.wait_ge(divided_pool, 4)

        def split_high(m):
            n, c = chunks[m]
            rows = jobs[n][2]
            return (turned_bank[m % 4][0:rows, :], *(part[n % 2][0:rows, which, c * CH:(c + 1) * CH] for which in range(3)),
                    rest[m % 2][0:rows, :])

        @block.scalar
        def _(act):
            def copy_fill(n):
                kind, b, i = fills[n]
                act.wait_ge(made, n + 1)
                if kind == "latent":
                    nc.scalar.activation(latent[:, i * CH:(i + 1) * CH], bank[n % 4][0:KW, :], ACT.Copy).then_inc(copied, 1)
                    return
                nc.scalar.activation(qkv[:, b * TB + i, :], bank[n % 4][:, 0:QK], ACT.Copy)
                nc.scalar.activation(values[:, b * KVH:(b + 1) * KVH, i, :],
                                     bank[n % 4][:, QK:QK + KW].rearrange("p (g n) -> p g n", n=HD), ACT.Copy).then_inc(copied, 1)

            def square_quarter(q):
                act.wait_ge(rotated_dve, q + 1)
                act.wait_ge(rotated_pool, q + 1)
                at_least(act, asked, q)
                nc.scalar.activation(square[:].rearrange("p i h n -> p i (h n)"), qkv[:, tiles(q), 0:QK],
                                     ACT.Square).then_inc(squared, 1)

            def root(q):
                act.wait_ge(asked, q + 1)
                nc.scalar.activation(total[:, tiles(q), :], total[:, tiles(q), :], ACT.Sqrt).then_inc(rooted, 1)

            done = 0
            for q in range(4):
                t = (q + 1) * quarter - 1
                last = fills_to("tile", t // TB, t % TB)
                for lag, then in ((8, square_quarter), (12, root)):
                    for n in range(done, min(last + lag, len(fills))):
                        copy_fill(n)
                        done = n + 1
                    then(q)

            def middle(m):
                _, _, mid_part, _, remainder = split_high(m)
                act.wait_ge(rest_ready, m + 1)
                nc.scalar.activation(mid_part, remainder, ACT.Copy).then_inc(mid, 1)

            for m, (n, c) in enumerate(chunks):
                source, high_part, _, _, _ = split_high(m)
                act.wait_ge(turned, m + 1)
                if n >= 2 and c == 0:
                    act.wait_ge(stored[n % 2], 16 * (NC // 2) * (n // 2))
                nc.scalar.activation(high_part, source, ACT.Copy).then_inc(high, 1)
                if m:
                    middle(m - 1)
            middle(len(chunks) - 1)

        @block.vector
        def _(v):
            step = Chain(v, dve)
            v.wait_ge(tables_loaded, 32)

            def norm_quarter(q):
                v.wait_ge(squared, q + 1)
                step(nc.vector.tensor_reduce(total[:, tiles(q), :], square[:], AX.X, ALU.add))
                nc.vector.tensor_scalar(total[:, tiles(q), :], total[:, tiles(q), :], 1.0 / HD, 1e-6, ALU.mult,
                                        ALU.add).then_inc(asked, 1)
                v.wait_ge(rooted, q + 1)
                nc.vector.reciprocal(total[:, tiles(q), :], total[:, tiles(q), :]).then_inc(inverted, 1)
                v.wait_ge(inverted, q + 1)
                divide(nc.vector, q, first_heads).then_inc(divided_dve, 1)

            for q in range(4):
                await_quarter(v, q)
                at_least(v, rotated_dve, q)
                rotate(nc.vector, step, q, first_heads, rotated_dve)
                if q:
                    norm_quarter(q - 1)
            norm_quarter(3)

            def lowest(m):
                _, _, mid_part, low_part, remainder = split_high(m)
                v.wait_ge(mid, m + 1)
                nc.vector.tensor_tensor(low_part, remainder, mid_part, ALU.subtract).then_inc(low, 1)

            for m in range(len(chunks)):
                source, high_part, _, _, remainder = split_high(m)
                v.wait_ge(high, m + 1)
                at_least(v, low, m - 1)
                nc.vector.tensor_tensor(remainder, source, high_part, ALU.subtract).then_inc(rest_ready, 1)
                if m:
                    lowest(m - 1)
            lowest(len(chunks) - 1)


NE = 8
INTER = 512
IC = INTER // P
ROUTED_TILES = 2 * T // P + NE
TILES = NT + ROUTED_TILES
SLOTS = TILES * P


def route(nc, tag, logits, consts, weight, slot, expert_of):
    with ExitStack() as ctx:
        sc = Scope(nc, ctx, tag)
        before, ones = sc.sb("before", [P, P]), sc.sb("ones", [P, P])
        back, tiles = sc.sb("back", [P, 1, NE]), sc.sb("tiles", [P, TILES, 1])
        prob, left, hot, taken, pos = (sc.sb(n, [P, NT, NE]) for n in ("prob", "left", "hot", "taken", "pos"))
        hots = [sc.sb(f"hots{i}", [P, NT, NE]) for i in range(2)]
        sums, best, first, total = (sc.sb(n, [P, NT, 1]) for n in ("sums", "best", "first", "total"))
        tops = [sc.sb(f"tops{i}", [P, NT, 1]) for i in range(2)]
        run = sc.sb("run", [P, NE, NT])
        line = sc.sb("line", [P, NT])
        count, count_i = sc.sb("count", [P, NE]), sc.sb("count_i", [P, NE], I32)
        ends, base = sc.sb("ends", [P, NE]), sc.sb("base", [P, 1, NE])
        owner = sc.sb("owner", [P, TILES, NE])
        owned = sc.sb("owned", [P, TILES])
        at = sc.sb("at", [P, NT])
        inside, whole = (sc.ps(n, [P, NT, NE]) for n in ("inside", "whole"))
        loaded, dve, centred, exp_done, counted, ranks_ready = (
            sc.sem(n) for n in ("loaded", "dve", "centred", "exp_done", "counted", "ranks_ready"))
        block = ctx.enter_context(nc.Block())

        @block.sync
        def _(sp):
            for dst, source in zip((before, ones, back, tiles), consts):
                sp.dma_start(dst[:], source).then_inc(loaded, 16)

        @block.tensor
        def _(pe):
            pe.wait_ge(loaded, 16 * 4)
            pe.wait_ge(counted, 1)
            nc.tensor.matmul(inside[:], before[:], taken[:], start=True, stop=True)
            nc.tensor.matmul(whole[:], ones[:], taken[:], start=True, stop=True).then_inc(ranks_ready, 1)

        @block.scalar
        def _(act):
            act.wait_ge(centred, 1)
            nc.scalar.activation(prob[:], prob[:], ACT.Exp).then_inc(exp_done, 1)

        @block.vector
        def _(v):
            step = Chain(v, dve)
            tt, ts, stt, red = (nc.vector.tensor_tensor, nc.vector.tensor_scalar, nc.vector.scalar_tensor_tensor,
                                nc.vector.tensor_reduce)

            def per_expert(x):
                return x.to_broadcast([P, NT, NE])

            v.wait_ge(loaded, 16 * 4)
            step(red(best[:, :, 0], logits[:], AX.X, ALU.max))
            tt(prob[:], logits[:], per_expert(best[:]), ALU.subtract).then_inc(centred, 1)
            v.wait_ge(exp_done, 1)
            step(red(sums[:, :, 0], prob[:], AX.X, ALU.add))
            step(nc.vector.reciprocal(sums[:], sums[:]))
            step(tt(prob[:], prob[:], per_expert(sums[:]), ALU.mult))
            step(nc.vector.tensor_copy(left[:], prob[:]))
            for i in range(2):
                step(red(tops[i][:, :, 0], left[:], AX.X, ALU.max))
                step(tt(hot[:], left[:], per_expert(tops[i][:]), ALU.is_equal))
                step(tt(hot[:], hot[:], back[:].to_broadcast([P, NT, NE]), ALU.mult))
                step(red(first[:, :, 0], hot[:], AX.X, ALU.max))
                step(tt(hots[i][:], hot[:], per_expert(first[:]), ALU.is_equal))
                step(stt(left[:], hots[i][:], -2.0, left[:], ALU.mult, ALU.add))
            tt(taken[:], hots[0][:], hots[1][:], ALU.add).then_inc(counted, 1)
            step(tt(total[:], tops[0][:], tops[1][:], ALU.add))
            step(ts(total[:], total[:], 1e-5, None, ALU.add))
            step(nc.vector.reciprocal(total[:], total[:]))
            for i in range(2):
                step(tt(weight[:, i, :], tops[i][:, :, 0], total[:, :, 0], ALU.mult))
            v.wait_ge(ranks_ready, 1)
            step(nc.vector.tensor_copy(pos[:], whole[:]))
            step(nc.vector.memset(line[:], 1.0))
            for e in range(NE):
                last = nc.vector.tensor_tensor_scan(run[:, e, :], line[:], pos[:, :, e], 0.0, ALU.mult, ALU.add)
            step(last)
            step(nc.vector.tensor_copy(count[:], run[:, :, NT - 1]))
            step(tt(pos[:], run[:].rearrange("p e i -> p i e"), pos[:], ALU.subtract))
            step(tt(pos[:], pos[:], inside[:], ALU.add))
            step(ts(count[:], count[:], float(P - 1), None, ALU.add))
            step(nc.vector.tensor_copy(count_i[:], count[:]))
            step(ts(count_i[:], count_i[:], P.bit_length() - 1, None, ALU.logical_shift_right))
            step(nc.vector.tensor_copy(count[:], count_i[:]))
            step(nc.vector.tensor_tensor_scan(ends[:], line[:, 0:NE], count[:], float(NT), ALU.mult, ALU.add))
            step(tt(base[:, 0, :], ends[:], count[:], ALU.subtract))
            step(tt(owner[:], tiles[:].to_broadcast([P, TILES, NE]), base[:].to_broadcast([P, TILES, NE]), ALU.is_ge))
            step(red(owned[:], owner[:], AX.X, ALU.add))
            step(ts(owned[:], owned[:], -1.0, None, ALU.add))
            step(ts(owned[:, 0:NT], owned[:, 0:NT], 0.0, float(NE), ALU.mult, ALU.add))
            step(nc.vector.tensor_copy(expert_of[:], owned[:]))
            step(stt(pos[:], base[:].to_broadcast([P, NT, NE]), float(P), pos[:], ALU.mult, ALU.add))
            for i in range(2):
                step(tt(hot[:], hots[i][:], pos[:], ALU.mult))
                step(red(at[:], hot[:], AX.X, ALU.add))
                step(nc.vector.tensor_copy(slot[:, i, :], at[:]))


def experts(nc, tag, h, slot, rows, results, expert_of, w_dram, ident):
    with ExitStack() as ctx:
        sc = Scope(nc, ctx, tag)
        w_gate = sc.sb("w_gate", [P, KT, NE + 1, INTER])
        w_up = sc.sb("w_up", [P, KT, NE + 1, INTER])
        w_down = sc.sb("w_down", [P, IC, NE + 1, D])
        x_sb = [sc.sb(f"x{i}", [P, D]) for i in range(2)]
        xt_sb = [sc.sb(f"xt{i}", [P, KT, P]) for i in range(2)]
        silu = [sc.sb(f"silu{i}", [P, INTER]) for i in range(2)]
        hid = [sc.sb(f"hid{i}", [P, INTER]) for i in range(2)]
        ht_sb = [sc.sb(f"ht{i}", [P, IC, P]) for i in range(2)]
        y_sb = [sc.sb(f"y{i}", [P, D]) for i in range(2)]
        x_ps, h_ps, y_ps = sc.ps("x_ps", [P, KT, P]), sc.ps("h_ps", [P, IC, P]), sc.ps("y_ps", [P, D])
        g_ps = [sc.ps(f"g{i}", [P, INTER]) for i in range(2)]
        u_ps = [sc.ps(f"u{i}", [P, INTER]) for i in range(2)]
        loaded = [sc.sem(f"loaded{i}") for i in range(2)]
        stored = [sc.sem(f"stored{i}") for i in range(2)]
        shared_loaded, routed_loaded = sc.sem("shared_loaded"), sc.sem("routed_loaded")
        sent = sc.software_sem("sent")
        x_turned, xt_copied, g_ready, u_ready, silu_done, hid_done, h_turned, ht_copied, y_ready, y_copied = (
            sc.sem(n) for n in ("x_turned", "xt_copied", "g_ready", "u_ready", "silu_done", "hid_done", "h_turned",
                                "ht_copied", "y_ready", "y_copied"))
        block = ctx.enter_context(nc.Block())

        def pairs(eng, one, first, end):
            with eng.Fori(first, end) as pair:
                one(2 * pair + 1, 1, pair)
                one(2 * pair + 2, 0, pair + 1)

        def steps(eng, one, before_routed=None):
            for t in range(3):
                one(t, t % 2, t // 2)
            pairs(eng, one, 1, NT // 2 - 1)
            if before_routed:
                eng.wait_ge(*before_routed)
            pairs(eng, one, NT // 2 - 1, TILES // 2 - 1)
            one(TILES - 1, 1, TILES // 2 - 1)

        def some(t):
            return not isinstance(t, int)

        @block.sync
        def _(sp):
            def load_weights(e, loaded_by):
                for dst, (routed, shared) in zip((w_gate, w_up, w_down), w_dram):
                    source = shared.rearrange("(k p) n -> p k n", p=P) if isinstance(e, int) else \
                        routed[bass.ds(e, 1)].rearrange("e (k p) n -> p k (e n)", p=P)
                    sp.dma_start(dst[:, :, bass.ds(e, 1), :].rearrange("p k e n -> p k (e n)"),
                                 source).then_inc(loaded_by, 16)

            def load(t, i, routed):
                at_least(sp, x_turned, t - 1)
                sp.dma_start(x_sb[i][:], rows[bass.ds(t * P, P), :] if routed else
                             h[:, bass.ds(t, 1), :].rearrange("p o d -> p (o d)")).then_inc(loaded[i], 16)

            load(0, 0, False)
            load_weights(NE, shared_loaded)

            def one(t, i, routed):
                if some(t) or t < TILES - 1:
                    load(t + 1, 1 - i, routed)

            for t in range(3):
                one(t, t % 2, False)
            with sp.Fori(1, 1 + NE) as pair:
                one(2 * pair + 1, 1, False)
                one(2 * pair + 2, 0, False)
                load_weights(pair - 1, routed_loaded)
            with sp.Fori(1 + NE, NT // 2 - 1) as pair:
                one(2 * pair + 1, 1, False)
                one(2 * pair + 2, 0, False)
            sp.wait_ge(sent, 16 * 2 * NT)
            with sp.Fori(NT // 2 - 1, TILES // 2 - 1) as pair:
                one(2 * pair + 1, 1, True)
                one(2 * pair + 2, 0, True)
            for i in range(2):
                sp.wait_ge(stored[i], 16 * (TILES // 2))

        @block.gpsimd
        def _(pool):
            for n in range(NT):
                for i in range(2):
                    pool.indirect_dma_start(rows, bass.IndirectOffsetOnAxis(ap=slot[:, i, n:n + 1], axis=0),
                                            h[:, n, :], None).then_inc(sent, 16)

        @block.tensor
        def _(pe):
            def turn_x(t, i, n):
                pe.wait_ge(loaded[i], 16 * (n + 1))
                at_least(pe, xt_copied, t)
                for k in range(KT):
                    last = nc.tensor.transpose(x_ps[:, k, :], x_sb[i][:, k * P:(k + 1) * P], ident[:])
                last.then_inc(x_turned, 1)

            def up(t, i):
                e = pe.value_load(expert_of[0:1, bass.ds(t, 1)], min_val=0, max_val=NE)
                pe.wait_ge(xt_copied, t + 1)
                at_least(pe, hid_done, t - 1)
                for bank, w, ready in ((g_ps[i], w_gate, g_ready), (u_ps[i], w_up, u_ready)):
                    for k in range(KT):
                        last = nc.tensor.matmul(bank[:], xt_sb[i][:, k, :],
                                                w[:, k, bass.ds(e, 1), :].rearrange("p e n -> p (e n)"),
                                                start=k == 0, stop=k == KT - 1)
                    last.then_inc(ready, 1)
                return e

            def turn_h(t, i):
                pe.wait_ge(hid_done, t + 1)
                at_least(pe, ht_copied, t)
                for k in range(IC):
                    last = nc.tensor.transpose(h_ps[:, k, :], hid[i][:, k * P:(k + 1) * P], ident[:])
                last.then_inc(h_turned, 1)

            def down(t, i):
                e = pe.value_load(expert_of[0:1, bass.ds(t, 1)], min_val=0, max_val=NE)
                pe.wait_ge(ht_copied, t + 1)
                at_least(pe, y_copied, t)
                for k in range(IC):
                    last = nc.tensor.matmul(y_ps[:], ht_sb[i][:, k, :],
                                            w_down[:, k, bass.ds(e, 1), :].rearrange("p e n -> p (e n)"),
                                            start=k == 0, stop=k == IC - 1)
                last.then_inc(y_ready, 1)

            turn_x(0, 0, 0)
            pe.wait_ge(shared_loaded, 16 * len(w_dram))

            def one(t, i, n):
                if some(t) or t > 0:
                    turn_h(t - 1, 1 - i)
                up(t, i)
                if some(t) or t < TILES - 1:
                    turn_x(t + 1, 1 - i, n + i)
                if some(t) or t > 0:
                    down(t - 1, 1 - i)

            steps(pe, one, (routed_loaded, 16 * len(w_dram) * NE))
            turn_h(TILES - 1, 1)
            down(TILES - 1, 1)

        @block.scalar
        def _(act):
            def copy_h(t, i):
                act.wait_ge(h_turned, t + 1)
                at_least(act, y_ready, t - 1)
                nc.scalar.activation(ht_sb[i][:], h_ps[:], ACT.Copy).then_inc(ht_copied, 1)

            def store(t, i):
                act.wait_ge(y_copied, t + 1)
                act.dma_start(results[bass.ds(t * P, P), :], y_sb[i][:]).then_inc(stored[i], 16)

            def one(t, i, n):
                if some(t) or t > 0:
                    copy_h(t - 1, 1 - i)
                act.wait_ge(g_ready, t + 1)
                at_least(act, hid_done, t - 1)
                nc.scalar.activation(silu[i][:], g_ps[i][:], ACT.Silu).then_inc(silu_done, 1)
                if some(t) or t > 1:
                    store(t - 2, i)

            steps(act, one)
            copy_h(TILES - 1, 1)
            store(TILES - 2, 0)
            store(TILES - 1, 1)

        @block.vector
        def _(v):
            def copy_x(t, i):
                v.wait_ge(x_turned, t + 1)
                at_least(v, u_ready, t - 1)
                nc.vector.tensor_copy(xt_sb[i][:], x_ps[:]).then_inc(xt_copied, 1)

            def copy_y(t, i, n):
                v.wait_ge(y_ready, t + 1)
                at_least(v, stored[i], 16 * n)
                nc.vector.tensor_copy(y_sb[i][:], y_ps[:]).then_inc(y_copied, 1)

            copy_x(0, 0)

            def one(t, i, n):
                v.wait_ge(u_ready, t + 1)
                v.wait_ge(silu_done, t + 1)
                at_least(v, h_turned, t - 1)
                nc.vector.tensor_tensor(hid[i][:], silu[i][:], u_ps[i][:], ALU.mult).then_inc(hid_done, 1)
                if some(t) or t < TILES - 1:
                    copy_x(t + 1, 1 - i)
                if some(t) or t > 0:
                    copy_y(t - 1, 1 - i, n - (1 - i))

            steps(v, one)
            copy_y(TILES - 1, 1, TILES // 2 - 1)


def combine(nc, tag, x, gate_rows, results, weight, slot, next_modulation):
    bufs = 8
    with ExitStack() as ctx:
        sc = Scope(nc, ctx, tag)
        acc = [sc.sb(f"acc{i}", [P, D]) for i in range(bufs)]
        picked = [[sc.sb(f"picked{i}_{n}", [P, D]) for n in range(2)] for i in range(bufs)]
        loaded = [sc.sem(f"loaded{i}") for i in range(bufs)]
        fetched = [sc.software_sem(f"fetched{i}") for i in range(bufs)]
        summed, dve = sc.sem("summed"), sc.sem("dve")
        gate = sc.sb("gate", [P, B, D])
        mod_sync, mod_act, mod_pe, mod_spread, mod_finish = modulation(nc, sc, *next_modulation)
        block = ctx.enter_context(nc.Block())

        @block.sync
        def _(sp):
            mod_sync(sp)
            for n in range(NT):
                at_least(sp, summed, n - bufs + 1)
                sp.dma_start(acc[n % bufs][:], results[n * P:(n + 1) * P, :]).then_inc(loaded[n % bufs], 16)

        @block.gpsimd
        def _(pool):
            for n in range(NT):
                at_least(pool, summed, n - bufs + 1)
                for i in range(2):
                    pool.indirect_dma_start(picked[n % bufs][i][:], None, results,
                                            bass.IndirectOffsetOnAxis(ap=slot[:, i, n:n + 1], axis=0)
                                            ).then_inc(fetched[n % bufs], 16)

        @block.scalar
        def _(act):
            mod_act(act)

        @block.tensor
        def _(pe):
            mod_pe(pe)

        @block.vector
        def _(v):
            step = Chain(v, dve)
            step(nc.vector.tensor_copy(gate[:], gate_rows))
            mod_spread(v, step)
            for n in range(NT):
                if n == NT // 2:
                    mod_finish(v, step)
                i, turn = n % bufs, n // bufs + 1
                v.wait_ge(loaded[i], 16 * turn)
                v.wait_ge(fetched[i], 32 * turn)
                for c in range(2):
                    step(nc.vector.scalar_tensor_tensor(acc[i][:], picked[i][c][:], weight[:, c, n:n + 1], acc[i][:],
                                                        ALU.mult, ALU.add))
                step(nc.vector.tensor_tensor(acc[i][:], acc[i][:], gate[:, n // TB, :], ALU.mult))
                nc.vector.tensor_tensor(x[:, n, :], x[:, n, :], acc[i][:], ALU.add).then_inc(summed, 1)


def recurrent_cell(nc, tag, xt, x, gate, w_dram, biases, c0_cols, ident, out):
    names = ("wf", "uf", "wi", "ui", "wc", "uc", "wo", "uo")
    with ExitStack() as ctx:
        sc = Scope(nc, ctx, tag)
        w = {n: sc.sb(n, [P, KT, D]) for n in names}
        bias = sc.sb("bias", [P, 4, KT])
        c0 = sc.sb("c0", [P, KT, 1])
        bias0 = sc.sb("bias0", [P, 3, KT])
        cell = [sc.sb(f"cell{i}", [P, KT, S]) for i in range(2)]
        gates = [[sc.sb(f"gate{i}_{n}", [P, CH]) for n in range(3)] for i in range(2)]
        prod = [sc.sb(f"prod{i}", [P, CH]) for i in range(2)]
        hidden = [sc.sb(f"hidden{i}", [P, KT, CH]) for i in range(2)]
        state_term = [sc.sb(f"state_term{i}", [P, KT, CH]) for i in range(2)]
        added = [sc.sb(f"added{i}", [P, 2, D]) for i in range(2)]
        bank = [[sc.ps(f"bank{i}_{n}", [P, CH]) for n in range(3)] for i in range(2)]
        back = [sc.ps(f"back{i}", [P, 2, D]) for i in range(2)]
        loaded = [sc.sem(f"loaded{i}") for i in range(len(names))]
        small, start_ready, dve, bias0_ready = sc.sem("small"), sc.sem("start_ready"), sc.sem("dve"), sc.sem("bias0_ready")
        term_made, term_copied, out_made, joined = (sc.sem(n) for n in ("term_made", "term_copied", "out_made", "joined"))
        made, gated, mixed, h_done, turned, scaled, summed, stored = (
            sc.sem(n) for n in ("made", "gated", "mixed", "h_done", "turned", "scaled", "summed", "stored"))
        block = ctx.enter_context(nc.Block())
        jobs = [(t, c, m) for t in range(B) for c in range(NC) for m in range(KT)]
        outs = [(t, c) for c in range(NC) for t in range(B)]
        kinds = (("wf", "uf"), ("wi", "ui"), ("wc", "uc"))

        def tiles_at(t, c, q):
            first = t * TB + c * (CH // P) + 2 * q
            return slice(first, first + 2)

        def need(pe, *which):
            for n in which:
                pe.wait_ge(loaded[names.index(n)], 16)

        @block.sync
        def _(sp):
            for n, b in enumerate(biases):
                sp.dma_start(bias[:, n, :], b).then_inc(small, 16)
            sp.dma_start(c0[:, :, 0], c0_cols).then_inc(small, 16)
            for i, n in enumerate(names):
                sp.dma_start(w[n][:], w_dram[n].rearrange("(k p) n -> p k n", p=P)).then_inc(loaded[i], 16)
            view = out.rearrange("b (i p) d -> p (b i) d", p=P)
            for n, (t, c) in enumerate(outs):
                for q in range(2):
                    sp.wait_ge(summed, 2 * n + q + 1)
                    sp.dma_start(view[:, tiles_at(t, c, q), :], x[:, tiles_at(t, c, q), :]).then_inc(stored, 16)
            sp.wait_ge(stored, 16 * len(outs) * 2)

        @block.tensor
        def _(pe):
            pe.wait_ge(small, 16 * 5)
            need(pe, "uf", "ui", "uc")
            for n, (_, u) in enumerate(kinds):
                for m in range(KT):
                    for k in range(KT):
                        last = nc.tensor.matmul(back[0][:, 0, 2 * n + m:2 * n + m + 1], w[u][:, k, m * P:(m + 1) * P],
                                                c0[:, k, :], start=k == 0, stop=k == KT - 1)
            last.then_inc(start_ready, 1)
            need(pe, "wf", "wi", "wc")
            for n, (t, c, m) in enumerate(jobs):
                at_least(pe, gated, 3 * (n - 1))
                for g, (wn, un) in enumerate(kinds):
                    dst = bank[n % 2][g]
                    terms = [(w[wn][:, k, m * P:(m + 1) * P], xt[:, k, t * S + c * CH:t * S + (c + 1) * CH]) for k in range(KT)]
                    if t:
                        pe.wait_ge(mixed, KT * (c + 1))
                        terms += [(w[un][:, k, m * P:(m + 1) * P], cell[0][:, k, c * CH:(c + 1) * CH]) for k in range(KT)]
                    for k, (l, r) in enumerate(terms):
                        last = nc.tensor.matmul(dst[:], l, r, start=k == 0, stop=k == len(terms) - 1)
                    last.then_inc(made, 1)
            need(pe, "wo", "uo")

            def turn(n):
                pe.wait_ge(h_done, KT * (n + 1))
                for q in range(2):
                    at_least(pe, scaled, 2 * n + q - 1)
                    if n == 0:
                        pe.wait_ge(bias0_ready, 1)
                    for i in range(2):
                        for k in range(KT):
                            last = nc.tensor.transpose(back[q][:, i, k * P:(k + 1) * P],
                                                       hidden[n % 2][:, k, (2 * q + i) * P:(2 * q + i + 1) * P], ident[:])
                    last.then_inc(turned, 1)

            def product(dst, weights, source):
                for k in range(KT):
                    last = nc.tensor.matmul(dst[:], weights[k], source[k], start=k == 0, stop=k == KT - 1)
                return last

            for n, (t, c) in enumerate(outs):
                for m in range(KT):
                    cols = slice(m * P, (m + 1) * P)
                    if n == 0:
                        pe.wait_ge(gated, 3 * len(jobs))
                    if t == 0:
                        pe.wait_ge(mixed, KT * (NC + c + 1))
                        at_least(pe, term_copied, KT * (c - 1) + m + 1)
                        product(bank[m][2], [w["uo"][:, k, cols] for k in range(KT)],
                                [cell[1][:, k, c * CH:(c + 1) * CH] for k in range(KT)]).then_inc(term_made, 1)
                    at_least(pe, joined, KT * (n - 2) + m + 1)
                    product(bank[n % 2][m], [w["wo"][:, k, cols] for k in range(KT)],
                            [xt[:, k, t * S + c * CH:t * S + (c + 1) * CH] for k in range(KT)]).then_inc(out_made, 1)
                if n:
                    turn(n - 1)
            turn(len(outs) - 1)

        @block.scalar
        def _(act):
            act.wait_ge(bias0_ready, 1)
            for n, (t, c, m) in enumerate(jobs):
                for g in range(3):
                    act.wait_ge(made, 3 * n + g + 1)
                    if g == 0:
                        at_least(act, mixed, n - 1)
                    b = bias0[:, g, m:m + 1] if t == 0 else bias[:, g, m:m + 1]
                    nc.scalar.activation(gates[n % 2][g][:], bank[n % 2][g][:], ACT.Tanh if g == 2 else ACT.Sigmoid,
                                         bias=b).then_inc(gated, 1)
            for n, (t, c) in enumerate(outs):
                for m in range(KT):
                    if t == 0:
                        act.wait_ge(term_made, KT * c + m + 1)
                        at_least(act, joined, KT * B * (c - 1))
                        nc.scalar.activation(state_term[c % 2][:, m, :], bank[m][2][:], ACT.Copy).then_inc(term_copied, 1)
                for m in range(KT):
                    act.wait_ge(joined, KT * n + m + 1)
                    nc.scalar.activation(hidden[n % 2][:, m, :], hidden[n % 2][:, m, :], ACT.Tanh,
                                         bias=bias[:, 3, m:m + 1]).then_inc(h_done, 1)

        @block.vector
        def _(v):
            step = Chain(v, dve)
            v.wait_ge(start_ready, 1)
            nc.vector.tensor_tensor(bias0[:].rearrange("p n m -> p (n m)"), back[0][:, 0, 0:6],
                                    bias[:, 0:3, :].rearrange("p n m -> p (n m)"), ALU.add).then_inc(bias0_ready, 1)
            for n, (t, c, m) in enumerate(jobs):
                f, i, g = gates[n % 2]
                cols = slice(c * CH, (c + 1) * CH)
                v.wait_ge(gated, 3 * (n + 1))
                at_least(v, mixed, n - 1)
                step(nc.vector.tensor_tensor(prod[n % 2][:], i[:], g[:], ALU.mult))
                if t == 0:
                    nc.vector.scalar_tensor_tensor(cell[0][:, m, cols], f[:], c0[:, m, :], prod[n % 2][:],
                                                   ALU.mult, ALU.add).then_inc(mixed, 1)
                else:
                    step(nc.vector.tensor_tensor(f[:], f[:], cell[0][:, m, cols], ALU.mult))
                    nc.vector.tensor_tensor(cell[1][:, m, cols], f[:], prod[n % 2][:], ALU.add).then_inc(mixed, 1)
            def join(n):
                t, c = outs[n]
                for m in range(KT):
                    v.wait_ge(term_copied, KT * c + m + 1)
                    v.wait_ge(out_made, KT * n + m + 1)
                    at_least(v, turned, 2 * (n - 1))
                    nc.vector.tensor_tensor(hidden[n % 2][:, m, :], bank[n % 2][m][:], state_term[c % 2][:, m, :],
                                            ALU.add).then_inc(joined, 1)

            def add(n):
                t, c = outs[n]
                for q in range(2):
                    k = 2 * n + q
                    v.wait_ge(turned, k + 1)
                    at_least(v, summed, k - 1)
                    nc.vector.tensor_tensor(added[q][:], back[q][:], gate[:, t:t + 1, :].to_broadcast([P, 2, D]),
                                            ALU.mult).then_inc(scaled, 1)
                    v.wait_ge(scaled, k + 1)
                    tiles = tiles_at(t, c, q)
                    nc.vector.tensor_tensor(x[:, tiles, :], x[:, tiles, :], added[q][:], ALU.add).then_inc(summed, 1)

            for n in range(len(outs)):
                join(n)
                if n:
                    add(n - 1)
            add(len(outs) - 1)


def load_constants(nc, i, ident, identb, masks):
    with ExitStack() as ctx:
        sc = Scope(nc, ctx, "constants")
        masks_sb = sc.sb("masks_sb", [P, 2, P + WIN])
        loaded, cast = sc.sem("loaded"), sc.sem("cast")
        block = ctx.enter_context(nc.Block())

        @block.sync
        def _(sp):
            sp.dma_start(ident[:], i["ident"]).then_inc(loaded, 16)
            sp.dma_start(masks_sb[:], i["masks"]).then_inc(loaded, 16)

        @block.vector
        def _(v):
            v.wait_ge(loaded, 32)
            nc.vector.tensor_copy(identb[:], ident[:]).then_inc(cast, 1)
            nc.vector.tensor_copy(masks[:], masks_sb[:]).then_inc(cast, 1)
            v.wait_ge(cast, 2)


def reset_semaphores(nc, name, numbers):
    with nc.Block(name) as block:
        @block.gpsimd
        def _(pool):
            pool.sem_clear(numbers)


def adaln_layers(nc, i, out):
    q_parts = nc.dram_tensor("q_parts", (3, B * D, S), BF16).ap()
    k_parts = nc.dram_tensor("k_parts", (3, B * D, S), BF16).ap()
    k1_parts = nc.dram_tensor("k1_parts", (3, B * KVH * HD, S), BF16).ap()
    o_rows = nc.dram_tensor("o_rows", (G, P, S), F32).ap()
    rows = nc.dram_tensor("expert_rows", (SLOTS, D), F32).ap()
    results = nc.dram_tensor("expert_results", (SLOTS, D), F32).ap()
    free = list(nc.free_semaphores)
    numbers = range(min(free), max(free) + 1)
    with ExitStack() as ctx:
        def keep(stack, name, shape, dt=F32):
            return stack.enter_context(nc.sbuf_tensor(name, shape, dt))

        x = keep(ctx, "x", [P, NT, D])
        mod = keep(ctx, "mod", [P, B, 6, D])
        ident = keep(ctx, "ident", [P, P])
        identb = keep(ctx, "identb", [P, P], BF16)
        masks = keep(ctx, "masks", [P, 2, P + WIN], BF16)
        load_constants(nc, i, ident, identb, masks)

        def mod_row(which):
            return lambda b: mod[:, b, which:which + 1, :]

        def weight_rows(row):
            return lambda b: row[0][:], (lambda b: row[1][:]) if len(row) > 1 else None

        with ExitStack() as stage:
            values = keep(stage, "values0", [P, G, TB, GH * HD])
            xt = keep(stage, "xt0", [P, KT, T])
            with ExitStack() as normed:
                h, hn = keep(normed, "h0", [P, NT, D]), keep(normed, "hn0", [P, NT, D])
                row = [keep(normed, f"row0_{n}", [P, 1, D]) for n in range(2)]
                norms(nc, "n0", [(x, h, 1e-5, False, mod_row(CA), mod_row(SA)), (h, hn, 1e-6, False, *weight_rows(row))],
                      loads=[row_load(row[0], i["L0_attn_ln_scale"]), row_load(row[1], i["L0_attn_ln_bias"])],
                      x_loads=[(x[:, b * TB:(b + 1) * TB, :], i["L0_attn_x"][b].rearrange("(i p) d -> p i d", p=P))
                               for b in range(B)],
                      last_sum=(x, mod_row(GA), hn, h), turned=(xt, ident), modulate=(i["L0_c"], i["L0_wmod"], mod))
            project_split(nc, "p0", xt, (q_parts, k_parts), [i["L0_attn_wq"], i["L0_attn_wk"]])
            w_v = keep(stage, "wv", [P, KT, D])
            full_attention(nc, q_parts, k_parts, xt, w_v, i["L0_attn_wv"].rearrange("(k p) n -> p k n", p=P), values,
                           o_rows, ident, float(D) ** -0.5)

        with ExitStack() as stage:
            weight = keep(stage, "weight", [P, 2, NT])
            slot = keep(stage, "slot", [P, 2, NT], I32)
            expert_of = keep(stage, "expert_of", [P, TILES], I32)
            h = keep(stage, "h1", [P, NT, D])
            logits = keep(stage, "logits", [P, NT, NE])
            gate = keep(stage, "gate", [P, KT, NE])
            with ExitStack() as inner:
                xt = keep(inner, "xt1", [P, KT, T])
                with ExitStack() as normed:
                    att = keep(normed, "att0", [P, NT, D])
                    gather_heads(nc, "g0", o_rows, att, ident)
                    row = [keep(normed, f"row1_{n}", [P, 1, D]) for n in range(2)]
                    reset_semaphores(nc, "reset0", numbers)
                    norms(nc, "n1",
                          [(x, h, 1e-5, False, mod_row(CB), mod_row(SB)), (h, att, 1e-5, False, *weight_rows(row))],
                          loads=[row_load(row[0], i["L0_ffn_ln_scale"]), row_load(row[1], i["L0_ffn_ln_bias"]),
                                 (gate[:], i["gate_cols"])],
                          x_sum=(x, mod_row(GA), att), turned=(xt, ident), product=(gate, logits),
                          stores=[(rows[n * P:(n + NE) * P, :], i["zeros"]) for n in range(NT, TILES, NE)])
                route(nc, "rt", logits, (i["before"], i["ones"], i["back"], i["tiles"]), weight, slot, expert_of)
            experts(nc, "ex", h, slot, rows, results, expert_of,
                    [(i[f"L0_ffn_{n}"], i[f"L0_ffn_s{n}"]) for n in ("Wg", "Wu", "Wd")], ident)
            combine(nc, "cb", x, mod[:, :, GB, :], results, weight, slot, (i["L1_c"], i["L1_wmod"], mod))

        reset_semaphores(nc, "reset1", numbers)

        with ExitStack() as stage:
            hid = keep(stage, "hid", [P, NT, D])
            with ExitStack() as inner:
                hn = keep(inner, "hn2", [P, NT, D])
                layer1_attention(nc, i, "g", [(x, hid, 1e-5, False, mod_row(CA), mod_row(SA))], hn, hid, ident, identb,
                                 masks[:, 0, :], q_parts, k1_parts, o_rows, causal_plan(), CH)
            reset_semaphores(nc, "reset2", numbers)
            with ExitStack() as inner:
                hn = keep(inner, "hn3", [P, NT, D])
                layer1_attention(nc, i, "l", [], hn, hid, ident, identb, masks[:, 1, :], q_parts, k1_parts, o_rows,
                                 window_plan(), P)
            xt = keep(stage, "xt4", [P, KT, T])
            norms(nc, "n4", [(x, hid, 1e-5, False, mod_row(CB), mod_row(SB))], x_sum=(x, mod_row(GA), hid),
                  turned=(xt, ident))
            recurrent_cell(nc, "rc", xt, x, mod[:, :, GB, :], {n: i[f"cell_{n}"] for n in
                           ("wf", "uf", "wi", "ui", "wc", "uc", "wo", "uo")},
                           [i[f"cell_b{n}"] for n in "fico"], i["cell_c0"], ident, out)


def layer1_attention(nc, i, kind, before, hn, hid, ident, identb, mask, q_parts, k_parts, o_rows, plan, span):
    with ExitStack() as stage:
        def keep(stack, name, shape, dt=F32):
            return stack.enter_context(nc.sbuf_tensor(f"{kind}_{name}", shape, dt))

        values = keep(stage, "values", [P, G, TB, HD])
        with ExitStack() as heads:
            qkv = keep(heads, "qkv", [P, NT, QK])
            with ExitStack() as inner:
                xt = keep(inner, "xt", [P, KT, T])
                row = keep(inner, "row", [P, 1, D])
                norms(nc, f"{kind}n", before + [(hid, hn, 1e-6, True, lambda b: row[:], None)],
                      loads=[row_load(row, i["L1_attn_norm1_w" if kind == "g" else "L1_attn_norm2_w"])], turned=(xt, ident))

                def weights(*names):
                    return [i[f"L1_attn_{name}"] for name in names]

                layer1_heads(nc, f"{kind}h", xt, weights("g_wq") if kind == "g" else weights("l_wq", "l_wk", "l_wv"),
                             (i["L1_attn_g_kv_down"], weights("g_k_up", "g_v_up")) if kind == "g" else None,
                             hn, qkv, values, i["rope_g" if kind == "g" else "rope_l"], q_parts, k_parts, ident)
        masked_attention(nc, f"{kind}a", q_parts, k_parts, values, o_rows, mask, identb, plan, span, float(HD) ** -0.5)
    project_heads(nc, f"{kind}o", o_rows, i[f"L1_attn_{kind}_wo"], hid, ident)


def columns(a):
    return np.ascontiguousarray(np.moveaxis(a.reshape(*a.shape[:-1], KT, P), (-1, -2), (0, 1)))


def rope_table(base):
    inv = (np.float32(1.0) / np.float32(base) ** (np.arange(0, HD, 2, dtype=np.float32) / np.float32(HD))).astype(np.float32)
    angle = np.arange(S, dtype=np.float32)[:, None] * inv[None, :]
    both = np.stack([np.cos(angle), np.sin(angle)]).astype(np.float32)
    return np.ascontiguousarray(both.reshape(2, TB, P, HD // 2).transpose(0, 2, 1, 3))


def constants():
    eye = np.eye(P, dtype=np.float32)
    key, query = np.mgrid[0:P, 0:P]
    ahead = np.concatenate([query - key, (query - key)[:, 0:WIN] + P], axis=1)
    allowed = np.stack([ahead >= 0, (ahead >= 0) & (ahead < WIN)], axis=1)
    return {
        "ident": eye,
        "masks": np.where(allowed, 0.0, -1e30).astype(np.float32),
        "before": (key < query).astype(np.float32),
        "ones": np.ones((P, P), np.float32),
        "zeros": np.zeros((NE * P, D), np.float32),
        "back": np.tile(np.arange(NE, 0, -1, dtype=np.float32), (P, 1, 1)),
        "tiles": np.tile(np.arange(TILES, dtype=np.float32)[:, None], (P, 1, 1)),
        "rope_g": rope_table(1e6),
        "rope_l": rope_table(1e4),
    }


AS_THEY_ARE = ("L0_attn_x", "L0_attn_ln_scale", "L0_attn_ln_bias", "L0_attn_wq", "L0_attn_wk", "L0_attn_wv",
               "L0_ffn_ln_scale", "L0_ffn_ln_bias", "L0_ffn_Wg", "L0_ffn_Wu", "L0_ffn_Wd", "L0_ffn_sWg", "L0_ffn_sWu",
               "L0_ffn_sWd", "L0_wmod", "L1_attn_norm1_w", "L1_attn_norm2_w", "L1_attn_g_wq", "L1_attn_g_kv_down",
               "L1_attn_g_k_up", "L1_attn_g_v_up", "L1_attn_g_wo", "L1_attn_l_wq", "L1_attn_l_wk", "L1_attn_l_wv",
               "L1_attn_l_wo", "L1_wmod")


def laid_out(inputs):
    arrays = {name: np.ascontiguousarray(inputs[name]) for name in AS_THEY_ARE}
    for name in ("L0_c", "L1_c"):
        arrays[name] = columns(np.asarray(inputs[name]))
    arrays["gate_cols"] = columns(np.asarray(inputs["L0_ffn_gate_w"]))
    for name in ("wf", "uf", "wi", "ui", "wc", "uc", "wo", "uo"):
        arrays[f"cell_{name}"] = np.ascontiguousarray(np.asarray(inputs[f"L1_ffn_{name}"]).T)
    for name in "fico":
        arrays[f"cell_b{name}"] = columns(np.asarray(inputs[f"L1_ffn_b{name}"]))
    arrays["cell_c0"] = columns(np.asarray(inputs["L1_ffn_in_c"]))
    return arrays | constants()


def kernel(**inputs):
    import concourse.bacc as bacc
    from concourse.bass_utils import run_bass_kernel_spmd

    arrays = laid_out(inputs)
    nc = bacc.Bacc("TRN2", target_bir_lowering=False, num_devices=1)
    handles = {n: nc.dram_tensor(f"in_{n}", a.shape, mybir.dt.from_np(a.dtype), kind="ExternalInput").ap()
               for n, a in arrays.items()}
    out = nc.dram_tensor("out", (B, S, D), F32, kind="ExternalOutput").ap()
    adaln_layers(nc, handles, out)
    return run_bass_kernel_spmd(nc, [{f"in_{n}": a for n, a in arrays.items()}], core_ids=[0]).results[0]["out"]
```
